# Optimizing a Trainium2 kernel written in Bass

```python
import numpy as np
import jax
import jax.numpy as jnp

def _softmax(x, axis=-1):
    return jax.nn.softmax(x, axis=axis)

def _gelu(x):
    return jax.nn.gelu(x, approximate=True)

def _silu(x):
    return jax.nn.silu(x)

def _sigmoid(x):
    return jax.nn.sigmoid(x)

def _layernorm(x, axis=-1, eps=1e-05):
    m = jnp.mean(x, axis=axis, keepdims=True)
    v = jnp.var(x, axis=axis, keepdims=True)
    return (x - m) / jnp.sqrt(v + eps)

def _scatter_add(tgt, idx, src, axis=0):
    return tgt.at[idx].add(src)

def _segment_sum(src, seg, n):
    return jax.ops.segment_sum(src, seg, n)
kernel_name = 'mk_gnn_preln_d4_gnn_r32_b72212'

def setup_inputs(seed: int=0):
    np.random.seed(seed)
    _w = jnp.asarray

    def _rec_inputs():
        import jax
        import jax.numpy as jnp
        _gk = jax.random.key(seed)
        x = -0.0007083 + 1.001 * jax.random.normal(jax.random.fold_in(_gk, 1), (50000, 48), jnp.float32)
        src = jax.random.randint(jax.random.fold_in(_gk, 2), (50000,), 0, 50000, jnp.int32)
        dst = jax.random.randint(jax.random.fold_in(_gk, 3), (50000,), 0, 50000, jnp.int32)
        _o = jnp.argsort(dst, stable=True)
        src = src[_o]
        dst = dst[_o]
        edge_attr_40 = jax.random.uniform(jax.random.fold_in(_gk, 12), (50000, 40), jnp.float32, 0.0, 1)
        edge_weight = jax.random.uniform(jax.random.fold_in(_gk, 14), (50000,), jnp.float32, 0.0, 6.99999)
        node_type_119 = jax.random.randint(jax.random.fold_in(_gk, 15), (50000,), 0, 119, jnp.int32)
        node_vec = jax.random.uniform(jax.random.fold_in(_gk, 16), (50000,), jnp.float32, 0.0, 1.49999)
        return (x, src, dst, edge_attr_40, edge_weight, node_type_119, node_vec)
    x, src, dst, edge_attr_40, edge_weight, node_type_119, node_vec = _rec_inputs()

    def _L0_gnn_setup():
        import jax, jax.numpy as jnp
        import numpy as np
        N_NODES = 50000
        N_EDGES = 50000
        D_IN = 48
        D_OUT = 48
        K = 4
        key = jax.random.key(seed)
        k1, k2, k3, k4, k5 = jax.random.split(key, 5)
        x = jax.random.normal(k1, (N_NODES, D_IN), dtype=jnp.float32)
        edge_index = jax.random.randint(k2, (2, N_EDGES), 0, N_NODES, dtype=jnp.int64)
        weight = jax.random.normal(k3, (K, D_IN, D_OUT), dtype=jnp.float32) * (1.0 / np.sqrt(D_IN))
        bias = jax.random.normal(k4, (D_OUT,), dtype=jnp.float32) * 0.01
        return {'x': x, 'edge_index': edge_index, 'weight': weight, 'bias': bias}
    _L0_gnn_all = _L0_gnn_setup()
    _L0_gnn_in = {k: v for k, v in _L0_gnn_all.items() if k in ('weight', 'bias')}
    del _L0_gnn_all

    def _L1_gnn_setup():
        import jax, jax.numpy as jnp
        import numpy as np
        import math
        K = 10
        A = 1.0
        B = 1.0
        ALPHA = 1.0

        def _An(n, a, b):
            nab = 2 * n + a + b
            return nab * (nab - 1) * (nab - 2) / (2 * n * (nab - n) * (nab - 2))

        def _Bn(n, a, b):
            nab = 2 * n + a + b
            return (nab - 1) * (a * a - b * b) / (2 * n * (nab - n) * (nab - 2))

        def _Cn(n, a, b):
            nab = 2 * n + a + b
            return -(2 * (n + a - 1) * (n + b - 1) * nab) / (2 * n * (nab - n) * (nab - 2))

        def _norm_weights(a, b):
            ws = []
            for i in range(K + 1):
                t1 = math.pow(2.0, a + b + 1) / (2 * i + a + b + 1)
                t2 = math.exp(math.lgamma(i + a + 1) - math.lgamma(i + a + b + 1))
                t3 = math.exp(math.lgamma(i + b + 1) - math.lgamma(i + 1))
                ws.append(math.sqrt(t1 * t2 * t3))
            return ws
        key = jax.random.key(seed)
        k1, k2 = jax.random.split(key)
        N, E, D = (3125, 50000, 48)
        x = jax.random.normal(k1, (N, D), dtype=jnp.float32)
        edge_index = jax.random.randint(k2, (2, E), 0, N, dtype=jnp.int64)
        lap_coefs = jnp.ones((K + 1,), dtype=jnp.float32)
        mf_weights = jnp.ones((1, K + 1, 1), dtype=jnp.float32)
        return {'x': x, 'edge_index': edge_index, 'lap_coefs': lap_coefs, 'mf_weights': mf_weights}
    _L1_gnn_all = _L1_gnn_setup()
    _L1_gnn_in = {k: v for k, v in _L1_gnn_all.items() if k in ('lap_coefs', 'mf_weights')}
    del _L1_gnn_all

    def _L2_gnn_setup():
        import jax, jax.numpy as jnp
        import numpy as np
        CUTOFF = 6.0
        LN_EPS = 1e-05
        key = jax.random.key(seed)
        ks = jax.random.split(key, 16)
        N, E, H, R, NEL, G = (50000, 25000, 48, 40, 119, 32)
        inp = {'h': jax.random.normal(ks[0], (N, H), jnp.float32), 'edge_index': jax.random.randint(ks[1], (2, E), 0, N, jnp.int64), 'edge_attr': jax.random.uniform(ks[2], (E, R), jnp.float32), 'distances': jax.random.uniform(ks[3], (E,), jnp.float32) * 7.0, 'atom_z': jax.random.randint(ks[4], (N,), 0, NEL, jnp.int64), 'node_mult': jax.random.uniform(ks[5], (N,), jnp.float32) + 0.5, 'batch': jnp.zeros((N,), jnp.int64), 'W1': jax.random.normal(ks[6], (H, R), jnp.float32) / np.sqrt(R), 'b1': jax.random.normal(ks[7], (H,), jnp.float32) * 0.01, 'W2': jax.random.normal(ks[8], (H, H), jnp.float32) / np.sqrt(H), 'b2': jax.random.normal(ks[9], (H,), jnp.float32) * 0.01, 'emb': jax.random.normal(ks[10], (NEL, G), jnp.float32) * 0.01, 'adaptW': jax.random.normal(ks[11], (G, G), jnp.float32) * 0.01, 'gamma': jnp.ones((H,), jnp.float32), 'beta': jnp.zeros((H,), jnp.float32)}
        return inp
    _L2_gnn_all = _L2_gnn_setup()
    _L2_gnn_in = {k: v for k, v in _L2_gnn_all.items() if k in ('W1', 'b1', 'W2', 'b2', 'emb', 'adaptW', 'gamma', 'beta')}
    del _L2_gnn_all

    def _L3_gnn_setup():
        import jax, jax.numpy as jnp
        import numpy as np
        N_NODES = 3125
        N_EDGES = 50000
        D_IN = 48
        D_H = 48
        D_OUT = 48

        def _graph_conv(x, src, dst, w_rel, w_root, b, num_nodes):
            agg = jax.ops.segment_sum(x[src], dst, num_segments=num_nodes)
            return agg @ w_rel + x @ w_root + b
        key = jax.random.key(seed)
        ks = jax.random.split(key, 8)
        s = 0.05
        x = jax.random.normal(ks[0], (N_NODES, D_IN), dtype=jnp.float32)
        edge_index = jax.random.randint(ks[1], (2, N_EDGES), 0, N_NODES, dtype=jnp.int64)
        w_rel1 = jax.random.normal(ks[2], (D_IN, D_H), dtype=jnp.float32) * s
        w_root1 = jax.random.normal(ks[3], (D_IN, D_H), dtype=jnp.float32) * s
        b1 = jax.random.normal(ks[4], (D_H,), dtype=jnp.float32) * s
        w_rel2 = jax.random.normal(ks[5], (D_H, D_OUT), dtype=jnp.float32) * s
        w_root2 = jax.random.normal(ks[6], (D_H, D_OUT), dtype=jnp.float32) * s
        b2 = jax.random.normal(ks[7], (D_OUT,), dtype=jnp.float32) * s
        return {'x': x, 'edge_index': edge_index, 'w_rel1': w_rel1, 'w_root1': w_root1, 'b1': b1, 'w_rel2': w_rel2, 'w_root2': w_root2, 'b2': b2}
    _L3_gnn_all = _L3_gnn_setup()
    _L3_gnn_in = {k: v for k, v in _L3_gnn_all.items() if k in ('w_rel1', 'w_root1', 'b1', 'w_rel2', 'w_root2', 'b2')}
    del _L3_gnn_all
    return {'x': x, 'src': src, 'dst': dst, 'edge_attr_40': edge_attr_40, 'edge_weight': edge_weight, 'node_type_119': node_type_119, 'node_vec': node_vec, 'L0_gnn_weight': _L0_gnn_in['weight'], 'L0_gnn_bias': _L0_gnn_in['bias'], 'L1_gnn_lap_coefs': _L1_gnn_in['lap_coefs'], 'L1_gnn_mf_weights': _L1_gnn_in['mf_weights'], 'L2_gnn_W1': _L2_gnn_in['W1'], 'L2_gnn_b1': _L2_gnn_in['b1'], 'L2_gnn_W2': _L2_gnn_in['W2'], 'L2_gnn_b2': _L2_gnn_in['b2'], 'L2_gnn_emb': _L2_gnn_in['emb'], 'L2_gnn_adaptW': _L2_gnn_in['adaptW'], 'L2_gnn_gamma': _L2_gnn_in['gamma'], 'L2_gnn_beta': _L2_gnn_in['beta'], 'L3_gnn_w_rel1': _L3_gnn_in['w_rel1'], 'L3_gnn_w_root1': _L3_gnn_in['w_root1'], 'L3_gnn_b1': _L3_gnn_in['b1'], 'L3_gnn_w_rel2': _L3_gnn_in['w_rel2'], 'L3_gnn_w_root2': _L3_gnn_in['w_root2'], 'L3_gnn_b2': _L3_gnn_in['b2']}

def reference(x, src, dst, edge_attr_40, edge_weight, node_type_119, node_vec, L0_gnn_weight, L0_gnn_bias, L1_gnn_lap_coefs, L1_gnn_mf_weights, L2_gnn_W1, L2_gnn_b1, L2_gnn_W2, L2_gnn_b2, L2_gnn_emb, L2_gnn_adaptW, L2_gnn_gamma, L2_gnn_beta, L3_gnn_w_rel1, L3_gnn_w_root1, L3_gnn_b1, L3_gnn_w_rel2, L3_gnn_w_root2, L3_gnn_b2):
    import jax
    import jax.numpy as jnp

    def _L0_gnn_ref(x, edge_index, weight, bias):
        import jax, jax.numpy as jnp
        import numpy as np
        N_NODES = 50000
        N_EDGES = 50000
        D_IN = 48
        D_OUT = 48
        K = 4
        'PyG ChebConv forward with sym normalization, lambda_max=2.0.\n\n            L_hat = 2L/lambda_max - I. With lambda_max=2 and sym Laplacian, the\n            diagonal becomes 0 and off-diagonal weights are -d_i^{-1/2} d_j^{-1/2}.\n            T0 = x, T1 = L_hat x, Tk = 2 L_hat T_{k-1} - T_{k-2};  out = sum_k Tk W_k + b.\n            '
        n = x.shape[0]
        row, col = (edge_index[0], edge_index[1])
        ew = (row != col).astype(x.dtype)
        deg = jax.ops.segment_sum(ew, row, num_segments=n)
        dis = jnp.where(deg > 0, jax.lax.rsqrt(deg), 0.0)
        w = -dis[row] * ew * dis[col]

        def prop(h):
            return jax.ops.segment_sum(w[:, None] * h[row], col, num_segments=n)
        tx0 = x
        out = tx0 @ weight[0]
        tx1 = prop(x)
        out = out + tx1 @ weight[1]
        for k in range(2, weight.shape[0]):
            tx2 = 2.0 * prop(tx1) - tx0
            out = out + tx2 @ weight[k]
            tx0, tx1 = (tx1, tx2)
        return out + bias

    def _L1_gnn_ref(x, edge_index, lap_coefs, mf_weights):
        import jax, jax.numpy as jnp
        import numpy as np
        import math
        K = 10
        A = 1.0
        B = 1.0
        ALPHA = 1.0

        def _An(n, a, b):
            nab = 2 * n + a + b
            return nab * (nab - 1) * (nab - 2) / (2 * n * (nab - n) * (nab - 2))

        def _Bn(n, a, b):
            nab = 2 * n + a + b
            return (nab - 1) * (a * a - b * b) / (2 * n * (nab - n) * (nab - 2))

        def _Cn(n, a, b):
            nab = 2 * n + a + b
            return -(2 * (n + a - 1) * (n + b - 1) * nab) / (2 * n * (nab - n) * (nab - 2))

        def _norm_weights(a, b):
            ws = []
            for i in range(K + 1):
                t1 = math.pow(2.0, a + b + 1) / (2 * i + a + b + 1)
                t2 = math.exp(math.lgamma(i + a + 1) - math.lgamma(i + a + b + 1))
                t3 = math.exp(math.lgamma(i + b + 1) - math.lgamma(i + 1))
                ws.append(math.sqrt(t1 * t2 * t3))
            return ws
        N = x.shape[0]
        src = edge_index[0]
        dst = edge_index[1]
        deg = jax.ops.segment_sum(jnp.ones(src.shape, dtype=x.dtype), dst, num_segments=N)
        dinv = jnp.where(deg > 0, jax.lax.rsqrt(jnp.where(deg > 0, deg, 1.0)), 0.0)
        enorm = dinv[src] * dinv[dst]

        def prop(h):
            return jax.ops.segment_sum(enorm[:, None] * h[src], dst, num_segments=N)
        nw = _norm_weights(A, B)
        c0 = (A - B) / 2.0
        c1 = (A + B + 2.0) / 2.0
        P0 = x
        P1 = c0 * x + c1 * prop(x)
        outs = [P0, P1]
        for n in range(2, K + 1):
            an, bn, cn = (_An(n, A, B), _Bn(n, A, B), _Cn(n, A, B))
            outs.append(bn * outs[-1] + cn * outs[-2] + an * prop(outs[-1]))
        lap = jnp.cumprod(ALPHA * jnp.tanh(lap_coefs))
        coef_outs = [outs[0] / nw[0]]
        for i in range(1, K + 1):
            coef_outs.append(lap[i - 1] / nw[i] * outs[i])
        stacked = jnp.stack(coef_outs, axis=1)
        return jnp.sum(stacked * mf_weights, axis=1)

    def _L2_gnn_ref(h, edge_index, edge_attr, distances, atom_z, node_mult, batch, W1, b1, W2, b2, emb, adaptW, gamma, beta):
        import jax, jax.numpy as jnp
        import numpy as np
        CUTOFF = 6.0
        LN_EPS = 1e-05
        src, dst = (edge_index[0], edge_index[1])
        N = h.shape[0]
        gate = jax.nn.silu(edge_attr @ W1.T + b1) @ W2.T + b2
        ei = emb[atom_z[src]]
        ej = emb[atom_z[dst]]
        adapt_logit = jnp.sum(ei * (ej @ adaptW.T), axis=-1, keepdims=True)
        gate = gate + adapt_logit
        cw = jnp.where(distances < CUTOFF, 0.5 * (jnp.cos(jnp.pi * distances / CUTOFF) + 1.0), 0.0)
        mj = node_mult[dst]
        msg = gate * h[dst] * (cw * mj)[:, None]
        agg = jax.ops.segment_sum(msg, src, num_segments=N)
        tot = jax.ops.segment_sum(mj, src, num_segments=N)
        agg = agg / jnp.clip(tot, 1e-08, None)[:, None]
        x = h + agg
        mu = jnp.mean(x, axis=-1, keepdims=True)
        var = jnp.mean(jnp.square(x - mu), axis=-1, keepdims=True)
        return (x - mu) / jnp.sqrt(var + LN_EPS) * gamma + beta

    def _L3_gnn_ref(x, edge_index, w_rel1, w_root1, b1, w_rel2, w_root2, b2):
        import jax, jax.numpy as jnp
        import numpy as np
        N_NODES = 3125
        N_EDGES = 50000
        D_IN = 48
        D_H = 48
        D_OUT = 48

        def _graph_conv(x, src, dst, w_rel, w_root, b, num_nodes):
            agg = jax.ops.segment_sum(x[src], dst, num_segments=num_nodes)
            return agg @ w_rel + x @ w_root + b
        src, dst = (edge_index[0], edge_index[1])
        n = x.shape[0]
        h = jax.nn.relu(_graph_conv(x, src, dst, w_rel1, w_root1, b1, n))
        out = _graph_conv(h, src, dst, w_rel2, w_root2, b2, n)
        return out
    edge_index = jnp.stack([src, dst])
    batch0 = jnp.zeros((50000,), jnp.int32)
    h = jnp.maximum(_layernorm(x, axis=-1), 0.0)
    x = x + _L0_gnn_ref(h, edge_index, L0_gnn_weight, L0_gnn_bias)
    h = jnp.maximum(_layernorm(x, axis=-1), 0.0)
    x = x + _L1_gnn_ref(h, edge_index, L1_gnn_lap_coefs, L1_gnn_mf_weights)
    h = jnp.maximum(_layernorm(x, axis=-1), 0.0)
    x = x + _L2_gnn_ref(h, edge_index, edge_attr_40, edge_weight, node_type_119, node_vec, batch0, L2_gnn_W1, L2_gnn_b1, L2_gnn_W2, L2_gnn_b2, L2_gnn_emb, L2_gnn_adaptW, L2_gnn_gamma, L2_gnn_beta)
    h = jnp.maximum(_layernorm(x, axis=-1), 0.0)
    x = x + _L3_gnn_ref(h, edge_index, L3_gnn_w_rel1, L3_gnn_w_root1, L3_gnn_b1, L3_gnn_w_rel2, L3_gnn_w_root2, L3_gnn_b2)
    return x

_drawn_inputs = setup_inputs


def setup_inputs(seed=0):
    import zlib

    import numpy as np

    out = dict(_drawn_inputs(seed))
    spreads = {'L1_gnn_lap_coefs': (1.0, 0.2),
     'L1_gnn_mf_weights': (1.0, 0.2),
     'L2_gnn_gamma': (1.0, 0.6),
     'L2_gnn_beta': (0.0, 0.8)}
    factors = {'edge_attr_40': 8.0,
     'edge_weight': 6.397,
     'node_vec': 88.983,
     'L0_gnn_bias': 8.0,
     'L2_gnn_W1': 5.064,
     'L2_gnn_b1': 200.0,
     'L2_gnn_W2': 4.29,
     'L2_gnn_b2': 200.0,
     'L2_gnn_emb': 200.0,
     'L2_gnn_adaptW': 200.0,
     'L3_gnn_w_rel1': 7.472,
     'L3_gnn_w_root1': 8.0,
     'L3_gnn_b1': 8.0,
     'L3_gnn_w_rel2': 6.158,
     'L3_gnn_w_root2': 7.137,
     'L3_gnn_b2': 8.0}
    for name, (base, spread) in spreads.items():
        noise = np.random.default_rng([zlib.crc32(name.encode()), seed]).standard_normal(out[name].shape)
        drawn = base * np.exp(spread * noise) if base else spread * noise
        out[name] = jnp.asarray(drawn.astype(out[name].dtype))
    for name, factor in factors.items():
        out[name] = (out[name] * factor).astype(out[name].dtype)
    return out
```

```python
from contextlib import ExitStack
import math

import concourse.bass as bass
from concourse import mybir

ALU = mybir.AluOpType
ACT = mybir.ActivationFunctionType
AX = mybir.AxisListType.X
F32 = mybir.dt.float32
F16 = mybir.dt.float16
I32 = mybir.dt.int32

P = 128
N = 50000
D = 48
R = 40
NZ = 119
EMB = 32
BS = 14
COLS = 2 * BS * -(-N // (P * 2 * BS))
NB = COLS // BS
IT = NB // 2
NPAD = P * COLS
ZROW = NPAD + P
ROWS = NPAD + P + 1
NPAIR = BS // 2
D2 = 2 * D
W1ROW = 104
EX = 2 * D
H2ROW = 52
NAGG = 4
K1 = 10
CUTOFF = 6.0
EPS = 1e-5
ROUND = 12582912.0

SAME, FIRST, D0, D1, NDIS, DINV, ZSRC = range(7)
EW = D0
NSC = 7


def jacobi(n):
    if n == 1:
        return 2.0, 0.0
    m = 2 * n + 2
    return (m * (m - 1) * (m - 2) / (2 * n * (m - n) * (m - 2)),
            -2.0 * n * n * m / (2 * n * (m - n) * (m - 2)))


def jacobi_norms():
    out = []
    for i in range(K1 + 1):
        t1 = math.pow(2.0, 3.0) / (2 * i + 3.0)
        t2 = math.exp(math.lgamma(i + 2.0) - math.lgamma(i + 3.0))
        t3 = math.exp(math.lgamma(i + 2.0) - math.lgamma(i + 1.0))
        out.append(math.sqrt(t1 * t2 * t3))
    return out


SCALE = [1.0]
for _k in range(1, K1 + 1):
    SCALE.append(SCALE[-1] * jacobi(_k)[0])
BETA = [0.0, 0.0] + [jacobi(k)[1] * SCALE[k - 2] / SCALE[k] for k in range(2, K1 + 1)]


def over_features(scalars, w=D):
    return scalars.unsqueeze(2).broadcast_to([P, BS, w])


def over_columns(row, n=BS):
    return row.unsqueeze(1).broadcast_to([P, n, D])


def block_of(table, i, h, w):
    return table[0:NPAD, :].rearrange("(p c) w -> p c w", p=P)[:, bass.ds((2 * i + h) * BS, BS), 0:w]


def turned(tp, c):
    return tp[:, c // 4, (c % 4) * P:(c % 4 + 1) * P]


def product(mm, c):
    return mm[:, c // 5, (c % 5) * D2:(c % 5 + 1) * D2]


def products(mm):
    n = min(5, NPAIR)
    out = [(slice(0, 2 * n), mm[:, 0, 0:n * D2].rearrange("p (c f) -> p c f", f=D))]
    if NPAIR > n:
        out.append((slice(2 * n, BS), mm[:, 1, 0:(NPAIR - n) * D2].rearrange("p (c f) -> p c f", f=D)))
    return out


def transpose_pairs(pe, tp, x, ident, rows=D2):
    for c in range(NPAIR):
        last = pe.transpose(turned(tp, c)[0:rows, :], x[:, 2 * c:2 * c + 2, :].rearrange("p a f -> p (a f)"), ident)
    return last


def copy_turned(nc, xT, tp, rows=D2):
    n = min(4, NPAIR) * P
    nc.scalar.copy(xT[0:rows, 0:n], tp[0:rows, 0, 0:n])
    return nc.scalar.copy(xT[0:rows, n:NPAIR * P], tp[0:rows, 1, 0:NPAIR * P - n])


def multiply_pairs(pe, mm, pairs):
    for c in range(NPAIR):
        for k, (xT, w, rows) in enumerate(pairs):
            last = pe.matmul(product(mm, c), xT[0:rows, c * P:(c + 1) * P], w,
                             start=(k == 0), stop=(k == len(pairs) - 1))
    return last


def layernorm(dve, x, out, sq, st, var_ready, std_ready, count, relu=True):
    total, mean, rstd = st[:, 0, :], st[:, 1, :], st[:, 2, :]
    dve.reduce_sum(total, x, AX)
    dve.drain()
    dve.tensor_scalar(mean, total, 1.0 / D, None, ALU.mult)
    dve.drain()
    dve.tensor_tensor(out, x, over_features(mean), ALU.subtract)
    dve.drain()
    dve.tensor_tensor(sq, out, out, ALU.mult)
    dve.drain()
    dve.reduce_sum(total, sq, AX)
    dve.drain()
    dve.tensor_scalar(st[:, 3, :], total, 1.0 / D, EPS, ALU.mult, ALU.add).then_inc(var_ready, 1)
    dve.wait_ge(std_ready, count)
    dve.reciprocal(rstd, st[:, 4, :])
    dve.drain()
    if relu:
        dve.scalar_tensor_tensor(out, out, 0.0, over_features(rstd), ALU.max, ALU.mult)
    else:
        dve.tensor_tensor(out, out, over_features(rstd), ALU.mult)
    dve.drain()


def take_std(act, nc, st, var_ready, std_ready, count):
    act.wait_ge(var_ready, count)
    nc.scalar.activation(st[:, 4, :], st[:, 3, :], ACT.Sqrt).then_inc(std_ready, 1)


class Names:
    pass


class Stage:

    def __init__(self, nc, name):
        self.nc, self.name, self.ctx, self.used = nc, name, ExitStack(), []

    def __enter__(self):
        return self

    def __exit__(self, *what):
        self.ctx.close()
        if self.used:
            self.nc.clear_and_free_semaphores(self.used)
            self.nc.all_engine_barrier()

    def sb(self, name, shape, dt=F32):
        return self.ctx.enter_context(self.nc.sbuf_tensor(f"{self.name}_{name}", shape, dt))

    def ps(self, name, shape, dt=F32):
        return self.ctx.enter_context(self.nc.psum_tensor(f"{self.name}_{name}", shape, dt))

    def sem(self, name):
        self.used.append(self.nc.alloc_semaphore(f"{self.name}_{name}"))
        return self.used[-1]

    def sems(self, name, n=2):
        return [self.sem(f"{name}{i}") for i in range(n)]


def gather_rows(pool, table, idx, idx_now, rows, w, slot_free, landed, idx_staged, begun):
    with pool.Fori(0, IT) as i:
        for h in range(2):
            pool.wait_ge(slot_free[h], i + 1)
            pool.tensor_copy(idx_now[:, h * BS:(h + 1) * BS], idx[:, bass.ds((2 * i + h) * BS, BS)]).then_inc(idx_staged, 1)
            pool.wait_ge(idx_staged, 2 * i + h + 1)
            pool.sem_inc(begun, 1)
            for u in range(BS):
                pool.indirect_dma_start(
                    out=rows[:, h, u, 0:w], out_offset=None, in_=table,
                    in_offset=bass.IndirectOffsetOnAxis(ap=idx_now[:, h * BS + u:h * BS + u + 1], axis=0),
                ).then_inc(landed[h], 16)



def count_stage(nc, io, g, nodes):
    with Stage(nc, "cnt") as s:
        src, dst = s.sb("src", [P, COLS], I32), s.sb("dst", [P, COLS], I32)
        srcf, dstf = s.sb("srcf", [P, COLS]), s.sb("dstf", [P, COLS])
        HI_D, LO_D, HI_S, LO_S, KEEP = range(5)
        split = s.sb("split", [P, NB, 5, BS])
        now = s.sb("now", [P, 2, 5, BS])
        one = s.sb("one", [P, 2, BS, 2 * (P + COLS)], F16)
        iota_i, iota_f, iota_h = s.sb("iota_i", [P, COLS], I32), s.sb("iota_f", [P, COLS]), s.sb("iota_h", [P, COLS], F16)
        zero_h = s.sb("zero_h", [P, P + COLS], F16)
        pid_i, pid = s.sb("pid_i", [P, 1], I32), s.sb("pid", [P, 1])
        diag, upper = s.sb("diag", [P, P]), s.sb("upper", [P, P])
        ones = s.sb("ones", [P, P])
        zi = s.sb("zi", [P, COLS], I32)
        t = [s.sb(f"t{i}", [P, COLS]) for i in range(5)]
        zrow = s.sb("zrow", [1, D2])
        ndeg_in, ndeg_out = s.ps("deg_in", [P, 512]), s.ps("deg_out", [P, 512])
        pcol = s.ps("pcol", [P, 512])
        srcT = s.sb("srcT", [P, 4, P])
        pT = s.ps("pT", [P, 4, P])

        loaded = s.sem("loaded")
        consts = s.sem("consts")
        const_step = s.sem("const_step")
        split_ready = s.sem("split_ready")
        now_free, now_ready = s.sems("now_free"), s.sem("now_ready")
        one_free, one_ready = s.sems("one_free"), s.sem("one_ready")
        counted = s.sem("counted")
        totals_ready, offsets_ready = s.sem("totals_ready"), s.sem("offsets_ready")
        deg_ready, root_ready = s.sem("deg_ready"), s.sem("root_ready")
        diag_ready, row_ready = s.sem("diag_ready"), s.sem("row_ready")
        turned_ready, srct_ready, stored = s.sem("turned_ready"), s.sem("srct_ready"), s.sem("stored")
        zero_ready = s.sem("zero_ready")
        block = s.ctx.enter_context(nc.Block())

        @block.sync
        def _(sp):
            sp.dma_start(dst[:, :], io.dst.rearrange("(p c) -> p c", p=P)).then_inc(loaded, 16)
            sp.dma_start(src[:, :], io.src.rearrange("(p c) -> p c", p=P)).then_inc(loaded, 16)
            sp.dma_start(zi[:, :], io.node_type.rearrange("(p c) -> p c", p=P)).then_inc(loaded, 16)
            sp.dma_start(t[4][:, :], io.node_vec.rearrange("(p c) -> p c", p=P)).then_inc(loaded, 16)
            sp.wait_ge(zero_ready, 1)
            for table, w in g.sum_tables:
                sp.dma_start(table[ZROW:ZROW + 1, :], zrow[:, 0:w]).then_inc(stored, 16)
            sp.wait_ge(srct_ready, 1)
            for k in range(-(-COLS // P)):
                n = min(P, COLS - k * P)
                sp.dma_start(g.src_cols[k * P:k * P + n, :], srcT[0:n, k, :]).then_inc(stored, 16)
            sp.wait_ge(stored, 16 * (len(g.sum_tables) + -(-COLS // P)))

        @block.gpsimd
        def _(pool):
            pool.memset(g.ident[:, :], 0.0).then_inc(const_step, 1)
            pool.memset(upper[:, :], 1.0).then_inc(const_step, 1)
            pool.memset(g.lower[:, :], 1.0).then_inc(const_step, 1)
            pool.memset(ones[:, :], 1.0)
            pool.iota(iota_i[:, :], pattern=[[1, COLS]], base=0, channel_multiplier=0)
            pool.iota(pid_i[:, :], pattern=[[0, 1]], base=0, channel_multiplier=1)
            pool.wait_ge(const_step, 3)
            pool.affine_select(out=g.ident[:, :], in_=g.ident[:, :], compare_op=ALU.not_equal, fill=1.0,
                               base=0, pattern=[[-1, P]], channel_multiplier=1)
            pool.affine_select(out=upper[:, :], in_=upper[:, :], compare_op=ALU.is_gt, fill=0.0,
                               base=0, pattern=[[1, P]], channel_multiplier=-1)
            pool.affine_select(out=g.lower[:, :], in_=g.lower[:, :], compare_op=ALU.is_gt, fill=0.0,
                               base=0, pattern=[[-1, P]], channel_multiplier=1).then_inc(consts, 1)

        @block.vector
        def _(dve):
            dve.sem_inc(now_free[0], 1)
            dve.sem_inc(now_free[1], 1)
            dve.memset(zrow[:, :], 0.0).then_inc(zero_ready, 1)
            dve.memset(zero_h[:, :], 0.0)
            dve.wait_ge(consts, 1)
            dve.tensor_copy(iota_f[:, :], iota_i[:, :])
            dve.tensor_copy(iota_h[:, :], iota_i[:, :])
            dve.tensor_copy(pid[:, :], pid_i[:, :])
            dve.drain()
            dve.tensor_copy(g.iota[:, :], iota_f[:, 0:P])
            dve.wait_ge(loaded, 64)
            dve.tensor_copy(srcf[:, :], src[:, :])
            dve.tensor_copy(dstf[:, :], dst[:, :])
            dve.tensor_copy(g.src_idx[:, :], src[:, :])
            dve.tensor_copy(g.dst_idx[:, :], dst[:, :])
            dve.drain()
            for x, hi, lo in ((dstf, HI_D, LO_D), (srcf, HI_S, LO_S)):
                dve.tensor_scalar(t[0][:, :], x[:, :], 0.5, 1.0 / COLS, ALU.add, ALU.mult)
                dve.drain()
                dve.tensor_scalar(t[1][:, :], t[0][:, :], -0.5, ROUND, ALU.add, ALU.add)
                dve.drain()
                dve.tensor_scalar(t[0][:, :], t[1][:, :], -ROUND, None, ALU.add)
                dve.drain()
                dve.tensor_copy(split[:, :, hi, :], t[0][:, :].rearrange("p (b c) -> p b c", c=BS))
                dve.scalar_tensor_tensor(split[:, :, lo, :], t[0][:, :].rearrange("p (b c) -> p b c", c=BS), -float(COLS),
                                         x[:, :].rearrange("p (b c) -> p b c", c=BS), ALU.mult, ALU.add)
                dve.drain()
            dve.tensor_tensor(t[0][:, :], srcf[:, :], dstf[:, :], ALU.not_equal)
            dve.drain()
            by_block = t[0][:, :].rearrange("p (b c) -> p b c", c=BS)
            dve.memset(g.sc[:, :, :, :], 0.0)
            dve.drain()
            dve.tensor_copy(g.sc[:, :, EW, :], by_block)
            dve.tensor_copy(split[:, :, KEEP, :], by_block).then_inc(split_ready, 1)
            dve.drain()
            dve.memset(t[0][:, 0:1], 0.0)
            dve.tensor_tensor(t[0][:, 1:COLS], dstf[:, 1:COLS], dstf[:, 0:COLS - 1], ALU.is_equal)
            dve.tensor_scalar(t[1][:, :], dstf[:, :], dstf[:, 0:1], None, ALU.is_equal)
            dve.drain()
            dve.tensor_copy(g.sc[:, :, SAME, :], by_block)
            dve.tensor_copy(g.sc[:, :, FIRST, :], t[1][:, :].rearrange("p (b c) -> p b c", c=BS))
            dve.tensor_scalar(diag[:, :], g.ident[:, :], dstf[:, 0:1], None, ALU.mult).then_inc(diag_ready, 1)
            dve.wait_ge(row_ready, 1)
            dve.scalar_tensor_tensor(g.carries[:, :], pcol[:, 0:P], dstf[:, COLS - 1:COLS], upper[:, :],
                                     ALU.is_equal, ALU.mult)
            dve.wait_ge(turned_ready, 1)
            for k in range(-(-COLS // P)):
                n = min(P, COLS - k * P)
                last = dve.tensor_copy(srcT[0:n, k, :], pT[0:n, k, :])
            last.then_inc(srct_ready, 1)

            with dve.Fori(0, IT) as i:
                for h in range(2):
                    dve.wait_ge(now_ready, 2 * i + h + 1)
                    dve.wait_ge(one_free[h], i + 1)
                    for c in range(BS):
                        o = one[:, h, c, :]
                        dve.tensor_scalar(o[:, 0:P], iota_h[:, 0:P], now[:, h, HI_D, c:c + 1], None, ALU.is_equal)
                        dve.tensor_scalar(o[:, P:P + COLS], iota_h[:, :], now[:, h, LO_D, c:c + 1], None, ALU.is_equal)
                        dve.tensor_scalar(o[:, P + COLS:2 * P + COLS], iota_h[:, 0:P], now[:, h, HI_S, c:c + 1],
                                          now[:, h, KEEP, c:c + 1], ALU.is_equal, ALU.mult)
                        last = dve.tensor_scalar(o[:, 2 * P + COLS:], iota_h[:, :], now[:, h, LO_S, c:c + 1], None, ALU.is_equal)
                    last.then_inc(one_ready, 1)
                    dve.drain()
                    dve.sem_inc(now_free[h], 1)

            dve.wait_ge(counted, 1)
            deg_in, has, last_edge, first, tmp = (x[:, :] for x in t)
            ex = nodes.ex
            dve.tensor_copy(ex[:, :, 4], tmp)
            dve.tensor_copy(ex[:, :, 3], zi[:, :])
            dve.tensor_copy(deg_in, ndeg_in[:, 0:COLS])
            dve.tensor_copy(first, ndeg_out[:, 0:COLS])
            dve.drain()
            dve.tensor_scalar(iota_f[:, :], deg_in, 1.0, None, ALU.max)
            dve.tensor_scalar(tmp, first, 1.0, None, ALU.max).then_inc(deg_ready, 1)
            dve.wait_ge(root_ready, 1)
            dve.reciprocal(dstf[:, :], dstf[:, :])
            dve.reciprocal(srcf[:, :], srcf[:, :])
            dve.tensor_scalar(has, deg_in, 0.0, None, ALU.is_gt)
            dve.tensor_scalar(first, first, 0.0, None, ALU.is_gt)
            dve.drain()
            dve.tensor_tensor(ex[:, :, 0], srcf[:, :], first, ALU.mult)
            dve.tensor_tensor(ex[:, :, 1], dstf[:, :], has, ALU.mult)
            dve.memset(iota_f[:, :], 1.0)
            dve.drain()
            dve.tensor_tensor_scan(last_edge, iota_f[:, :], deg_in, 0.0, ALU.mult, ALU.add)
            dve.drain()
            dve.tensor_copy(diag[:, 0:1], last_edge[:, COLS - 1:COLS]).then_inc(totals_ready, 1)
            dve.wait_ge(offsets_ready, 1)
            dve.tensor_copy(diag[:, 1:2], pcol[:, P:P + 1])
            dve.drain()
            dve.tensor_scalar(last_edge, last_edge, diag[:, 1:2], -1.0, ALU.add, ALU.add)
            dve.drain()
            dve.scalar_tensor_tensor(deg_in, deg_in, -1.0, last_edge, ALU.mult, ALU.add)
            dve.tensor_scalar(tmp, last_edge, 0.5, 1.0 / COLS, ALU.add, ALU.mult)
            dve.drain()
            dve.tensor_scalar(first, tmp, -0.5, ROUND, ALU.add, ALU.add)
            dve.drain()
            dve.tensor_scalar(tmp, first, -ROUND, None, ALU.add)
            dve.drain()
            dve.scalar_tensor_tensor(first, tmp, float(COLS), deg_in, ALU.mult, ALU.is_gt)
            dve.tensor_scalar(tmp, tmp, float(NPAD), None, ALU.add)
            dve.drain()
            dve.tensor_tensor(tmp, tmp, last_edge, ALU.subtract)
            dve.drain()
            dve.tensor_tensor(tmp, tmp, first, ALU.mult)
            dve.drain()
            dve.tensor_tensor(last_edge, last_edge, tmp, ALU.add)
            dve.drain()
            dve.scalar_tensor_tensor(last_edge, last_edge, -float(ZROW), has, ALU.add, ALU.mult)
            dve.drain()
            dve.tensor_scalar(ex[:, :, 2], last_edge, float(ZROW), None, ALU.add)
            dve.drain()
            dve.tensor_copy(g.last_node[:, :], ex[:, :, 2])

        @block.scalar
        def _(act):
            act.wait_ge(split_ready, 1)
            with act.Fori(0, IT) as i:
                for h in range(2):
                    act.wait_ge(now_free[h], i + 1)
                    nc.scalar.copy(now[:, h, :, :].rearrange("p k c -> p (k c)"),
                                   split[:, :, :, :].rearrange("p b k c -> p (b k c)")[:, bass.ds((2 * i + h) * (5 * BS), 5 * BS)]
                                   ).then_inc(now_ready, 1)
            act.wait_ge(deg_ready, 1)
            nc.scalar.activation(dstf[:, :], iota_f[:, :], ACT.Sqrt)
            nc.scalar.activation(srcf[:, :], t[4][:, :], ACT.Sqrt).then_inc(root_ready, 1)

        @block.tensor
        def _(pe):
            pe.sem_inc(one_free[0], 1)
            pe.sem_inc(one_free[1], 1)
            pe.wait_ge(diag_ready, 1)
            pe.matmul(pcol[:, 0:P], ones[:, :], diag[:, :], start=True, stop=True).then_inc(row_ready, 1)
            for k in range(-(-COLS // P)):
                n = min(P, COLS - k * P)
                last = pe.transpose(pT[0:n, k, :], srcf[:, k * P:k * P + n], g.ident[:, :])
            last.then_inc(turned_ready, 1)
            for acc in (ndeg_in, ndeg_out):
                pe.matmul(acc[:, 0:COLS], zero_h[:, 0:P], zero_h[:, P:], start=True, stop=False, skip_group_check=True)
            with pe.Fori(0, IT) as i:
                for h in range(2):
                    pe.wait_ge(one_ready, 2 * i + h + 1)
                    for c in range(BS):
                        o = one[:, h, c, :]
                        pe.matmul(ndeg_in[:, 0:COLS], o[:, 0:P], o[:, P:P + COLS], start=False, stop=False,
                                  skip_group_check=True)
                        last = pe.matmul(ndeg_out[:, 0:COLS], o[:, P + COLS:2 * P + COLS], o[:, 2 * P + COLS:],
                                         start=False, stop=False, skip_group_check=True)
                    last.then_inc(one_free[h], 1)
            for acc in (ndeg_in, ndeg_out):
                last = pe.matmul(acc[:, 0:COLS], zero_h[:, 0:P], zero_h[:, P:], start=False, stop=True, skip_group_check=True)
            last.then_inc(counted, 1)
            pe.wait_ge(totals_ready, 1)
            pe.matmul(pcol[:, P:P + 1], upper[:, :], diag[:, 0:1], start=True, stop=True).then_inc(offsets_ready, 1)



def weight_stage(nc, io, g):
    with Stage(nc, "wts") as s:
        raw = [s.sb(f"raw{k}", [D2, D2]) for k in range(4)]
        lap, mf, coef = s.sb("lap", [P, K1 + 1]), s.sb("mf", [P, K1 + 1]), s.sb("coef", [P, K1 + 3])
        embT, adT, cmat = s.sb("embT", [EMB, NZ]), s.sb("adT", [EMB, EMB]), s.sb("cmat", [EMB, NZ])
        pm = s.ps("pm", [P, 512])
        zeroed, loaded, tanhed = s.sem("zeroed"), s.sem("loaded"), s.sem("tanhed")
        c_ready, c_copied, m_ready = s.sem("c_ready"), s.sem("c_copied"), s.sem("m_ready")
        bd = [(raw[k], io.w0[k], D) for k in range(4)] + [
            (g.w_rel1, io.w_rel1, D), (g.w_root1, io.w_root1, D), (g.w_rel2, io.w_rel2, D), (g.w_root2, io.w_root2, D),
            (g.W1, io.W1.rearrange("h r -> r h"), R), (g.W2, io.W2.rearrange("h k -> k h"), D)]
        n_dma = 2 * len(bd) + 10
        block = s.ctx.enter_context(nc.Block())

        @block.sync
        def _(sp):
            sp.wait_ge(zeroed, 1)
            with nc.allow_non_contiguous_dma(reason="small transposed weights, once"):
                for to, of, k in bd:
                    for half in range(2):
                        sp.dma_start(to[half * k:(half + 1) * k, half * D:(half + 1) * D], of).then_inc(loaded, 16)
                for to, of in ((g.bias0, io.bias0), (g.b2, io.b2), (g.gamma, io.gamma), (g.beta, io.beta),
                               (g.b_l1, io.b_l1), (g.b_l2, io.b_l2)):
                    sp.dma_start(to[:, :], of.partition_broadcast(P)).then_inc(loaded, 16)
                sp.dma_start(lap[:, :], io.lap.partition_broadcast(P)).then_inc(loaded, 16)
                sp.dma_start(mf[:, :], io.mf.rearrange("a k b -> (a k b)").partition_broadcast(P)).then_inc(loaded, 16)
                sp.dma_start(embT[:, :], io.emb.rearrange("z g -> g z")).then_inc(loaded, 16)
                sp.dma_start(adT[:, :], io.adaptW.rearrange("g k -> k g")).then_inc(loaded, 16)
                for half in range(2):
                    sp.dma_start(g.b1[half * D:(half + 1) * D, :], io.b1.unsqueeze(1)).then_inc(loaded, 16)
            sp.wait_ge(loaded, 16 * (n_dma + 2))

        @block.vector
        def _(dve):
            for k, (to, _, _) in enumerate(bd):
                last = dve.memset(to[:, :], 0.0)
            last.then_inc(zeroed, 1)
            dve.wait_ge(loaded, 16 * (n_dma + 2))
            dve.tensor_tensor(g.wh[:, :], raw[0][:, :], raw[2][:, :], ALU.subtract)
            dve.tensor_tensor(g.wu[0][:, :], raw[1][:, :], raw[3][:, :], ALU.subtract)
            dve.tensor_scalar(g.wu[1][:, :], raw[2][:, :], 2.0, None, ALU.mult)
            dve.tensor_scalar(g.wu[2][:, :], raw[3][:, :], 2.0, None, ALU.mult)
            dve.wait_ge(tanhed, 1)
            for k in range(1, K1):
                dve.tensor_tensor(lap[:, k:k + 1], lap[:, k:k + 1], lap[:, k - 1:k], ALU.mult)
                dve.drain()
            dve.memset(coef[:, :], 0.0)
            dve.drain()
            dve.tensor_copy(coef[:, 0:1], mf[:, 0:1])
            dve.tensor_tensor(coef[:, 1:K1 + 1], mf[:, 1:K1 + 1], lap[:, 0:K1], ALU.mult)
            dve.drain()
            for k, norm in enumerate(jacobi_norms()):
                dve.tensor_scalar(coef[:, k:k + 1], coef[:, k:k + 1], 1.0 / norm, None, ALU.mult)
            dve.drain()
            for k in range(K1 - 2, -1, -1):
                dve.scalar_tensor_tensor(coef[:, k:k + 1], coef[:, k + 2:k + 3], jacobi(k + 2)[1], coef[:, k:k + 1],
                                         ALU.mult, ALU.add)
                dve.drain()
            dve.tensor_copy(g.p0w[:, :], coef[:, 0:1])
            for k in range(K1):
                dve.tensor_scalar(g.omega[:, k:k + 1], coef[:, k + 1:k + 2], SCALE[k + 1], None, ALU.mult)
            dve.wait_ge(c_ready, 1)
            dve.tensor_copy(cmat[:, :], pm[0:EMB, 0:NZ]).then_inc(c_copied, 1)
            dve.wait_ge(m_ready, 1)
            dve.tensor_copy(g.pair_term[:, :], pm[0:NZ, P:P + NZ])

        @block.scalar
        def _(act):
            act.wait_ge(loaded, 16 * (n_dma + 2))
            nc.scalar.activation(lap[:, :], lap[:, :], ACT.Tanh).then_inc(tanhed, 1)

        @block.tensor
        def _(pe):
            pe.wait_ge(loaded, 16 * (n_dma + 2))
            pe.matmul(pm[0:EMB, 0:NZ], adT[:, :], embT[:, :], start=True, stop=True).then_inc(c_ready, 1)
            pe.wait_ge(c_copied, 1)
            pe.matmul(pm[0:NZ, P:P + NZ], embT[:, :], cmat[:, :], start=True, stop=True).then_inc(m_ready, 1)



def node_stage_in(nc, io, g, nodes):
    with Stage(nc, "nin") as s:
        x, row = s.sb("x", [P, 2, BS, D]), s.sb("row", [P, 2, BS, W1ROW])
        hh, sq, st, hT = s.sb("hh", [P, BS, D]), s.sb("sq", [P, BS, D]), s.sb("st", [P, 5, BS]), s.sb("hT", [P, NPAIR * P])
        exs = s.sb("exs", [P, 2, BS * 5])
        tp, mm = s.ps("tp", [P, 2, 512]), s.ps("mm", [P, 2, 512])
        x_landed, x_free = s.sems("x_landed"), s.sems("x_free")
        row_ready, row_free, row_stored = s.sems("row_ready"), s.sems("row_free"), s.sems("row_stored")
        var_ready, std_ready = s.sem("var_ready"), s.sem("std_ready")
        h_ready, tp_ready, hT_ready, mm_ready = s.sem("h_ready"), s.sem("tp_ready"), s.sem("hT_ready"), s.sem("mm_ready")
        ex_ready = s.sem("ex_ready")
        block = s.ctx.enter_context(nc.Block())

        @block.sync
        def _(sp):
            with sp.Fori(0, IT) as i:
                for h in range(2):
                    sp.wait_ge(x_free[h], i + 1)
                    sp.dma_start(x[:, h, :, :], block_of(io.x, i, h, D)).then_inc(x_landed[h], 16)

        @block.gpsimd
        def _(pool):
            pool.sem_inc(row_free[0], 1)
            pool.sem_inc(row_free[1], 1)
            with pool.Fori(0, IT) as i:
                for h in range(2):
                    pool.wait_ge(row_ready[h], i + 1)
                    pool.dma_start(block_of(g.tab_in, i, h, W1ROW), row[:, h, :, :]).then_inc(row_stored[h], 16)
                    pool.wait_ge(row_stored[h], (i + 1) * 16)
                    pool.sem_inc(row_free[h], 1)

        @block.vector
        def _(dve):
            dve.memset(row[:, :, :, EX + 5:W1ROW], 0.0)
            dve.sem_inc(x_free[0], 1)
            dve.sem_inc(x_free[1], 1)
            with dve.Fori(0, IT) as i:
                for h in range(2):
                    dve.wait_ge(x_landed[h], (i + 1) * 16)
                    layernorm(dve, x[:, h, :, :], hh[:, :, :], sq[:, :, :], st, var_ready, std_ready, 2 * i + h + 1)
                    dve.sem_inc(h_ready, 1)
                    dve.wait_ge(row_free[h], i + 1)
                    dve.tensor_copy(row[:, h, :, D:2 * D], hh[:, :, :])
                    dve.tensor_tensor(row[:, h, :, 0:D], x[:, h, :, :], over_columns(g.bias0[:, :]), ALU.add)
                    dve.wait_ge(ex_ready, 2 * i + h + 1)
                    dve.tensor_copy(row[:, h, :, EX:EX + 5], exs[:, h, :].rearrange("p (c k) -> p c k", k=5))
                    dve.drain()
                    dve.wait_ge(mm_ready, 2 * i + h + 1)
                    for c, piece in products(mm):
                        last = dve.tensor_tensor(row[:, h, c, 0:D], row[:, h, c, 0:D], piece, ALU.add)
                    last.then_inc(row_ready[h], 1)
                    dve.drain()
                    dve.sem_inc(x_free[h], 1)

        @block.scalar
        def _(act):
            with act.Fori(0, IT) as i:
                for h in range(2):
                    take_std(act, nc, st, var_ready, std_ready, 2 * i + h + 1)
                    nc.scalar.copy(exs[:, h, :], nodes.ex[:, :, :].rearrange("p c k -> p (c k)")[:, bass.ds((2 * i + h) * (5 * BS), 5 * BS)]
                                   ).then_inc(ex_ready, 1)
                    act.wait_ge(tp_ready, 2 * i + h + 1)
                    copy_turned(nc, hT, tp).then_inc(hT_ready, 1)

        @block.tensor
        def _(pe):
            with pe.Fori(0, IT) as i:
                for h in range(2):
                    pe.wait_ge(h_ready, 2 * i + h + 1)
                    transpose_pairs(pe, tp, hh, g.ident[:, :]).then_inc(tp_ready, 1)
                    pe.wait_ge(hT_ready, 2 * i + h + 1)
                    multiply_pairs(pe, mm, [(hT, g.wh[:, :], D2)]).then_inc(mm_ready, 1)


def node_stage_mid(nc, io, g):
    with Stage(nc, "mid") as s:
        rows, idx_now = s.sb("rows", [P, 2, BS, D2]), s.sb("idx_now", [P, 2 * BS], I32)
        own = s.sb("own", [P, 2, BS, W1ROW])
        x1, h1, sq, st = s.sb("x1", [P, BS, D]), s.sb("h1", [P, BS, D]), s.sb("sq", [P, BS, D]), s.sb("st", [P, 5, BS])
        x2, h2 = s.sb("x2", [P, 2, BS, D]), s.sb("h2", [P, 2, BS, H2ROW])
        hl = s.sb("hl", [P, BS, D])
        slot_free, landed, idx_staged, begun = s.sems("slot_free"), s.sems("landed"), s.sem("idx_staged"), s.sem("begun")
        own_landed, own_free = s.sems("own_landed"), s.sems("own_free")
        out_ready, out_free, out_stored = s.sems("out_ready"), s.sems("out_free"), s.sems("out_stored")
        var_ready, std_ready = s.sem("var_ready"), s.sem("std_ready")
        block = s.ctx.enter_context(nc.Block())

        @block.gpsimd
        def _(pool):
            gather_rows(pool, g.tab_both, g.last_node, idx_now, rows, D2, slot_free, landed, idx_staged, begun)

        @block.scalar
        def _(act):
            with act.Fori(0, IT) as i:
                for h in range(2):
                    act.wait_ge(own_free[h], i + 1)
                    act.dma_start(own[:, h, :, :], block_of(g.tab_in, i, h, W1ROW)).then_inc(own_landed[h], 16)
                    take_std(act, nc, st, var_ready, std_ready, (2 * i + h) * 2 + 1)
                    take_std(act, nc, st, var_ready, std_ready, (2 * i + h) * 2 + 2)

        @block.sync
        def _(sp):
            sp.sem_inc(out_free[0], 1)
            sp.sem_inc(out_free[1], 1)
            with sp.Fori(0, IT) as i:
                for h in range(2):
                    sp.wait_ge(out_ready[h], i + 1)
                    sp.dma_start(block_of(g.x2, i, h, D), x2[:, h, :, :]).then_inc(out_stored[h], 16)
                    sp.dma_start(block_of(g.tab_h2, i, h, H2ROW), h2[:, h, :, :]).then_inc(out_stored[h], 16)
                    sp.wait_ge(out_stored[h], (i + 1) * 32)
                    sp.sem_inc(out_free[h], 1)

        @block.vector
        def _(dve):
            dve.memset(h2[:, :, :, D + 2:H2ROW], 0.0)
            for q in slot_free + own_free:
                dve.sem_inc(q, 1)
            with dve.Fori(0, IT) as i:
                for h in range(2):
                    dve.wait_ge(landed[h], (i + 1) * (16 * BS))
                    dve.wait_ge(own_landed[h], (i + 1) * 16)
                    scal = own[:, h, :, EX:EX + 5]
                    dve.tensor_tensor(sq[:, :, :], rows[:, h, :, 0:D], over_features(scal[:, :, 0]), ALU.mult)
                    dve.wait_ge(out_free[h], i + 1)
                    dve.tensor_tensor(x2[:, h, :, :], rows[:, h, :, D:D2], over_features(scal[:, :, 1]), ALU.mult)
                    dve.drain()
                    dve.sem_inc(slot_free[h], 1)
                    dve.tensor_tensor(x1[:, :, :], own[:, h, :, 0:D], sq[:, :, :], ALU.subtract)
                    dve.drain()
                    layernorm(dve, x1[:, :, :], h1[:, :, :], sq[:, :, :], st, var_ready, std_ready, (2 * i + h) * 2 + 1)
                    dve.tensor_tensor(x1[:, :, :], x1[:, :, :], x2[:, h, :, :], ALU.add)
                    dve.drain()
                    dve.scalar_tensor_tensor(x2[:, h, :, :], h1[:, :, :], g.p0w[:, 0:1], x1[:, :, :], ALU.mult, ALU.add)
                    dve.drain()
                    layernorm(dve, x2[:, h, :, :], hl[:, :, :], sq[:, :, :], st, var_ready, std_ready, (2 * i + h) * 2 + 2)
                    dve.tensor_copy(h2[:, h, :, 0:D], hl[:, :, :])
                    dve.tensor_copy(h2[:, h, :, D:D + 2], scal[:, :, 3:5]).then_inc(out_ready[h], 1)
                    dve.drain()
                    dve.sem_inc(own_free[h], 1)


def node_stage_late(nc, io, g):
    with Stage(nc, "late") as s:
        x2, h2, agg = s.sb("x2", [P, 2, BS, D]), s.sb("h2", [P, 2, BS, H2ROW]), s.sb("agg", [P, 2, NAGG, BS, H2ROW])
        a, b, sq, st = s.sb("a", [P, BS, H2ROW]), s.sb("b", [P, BS, D]), s.sb("sq", [P, BS, D]), s.sb("st", [P, 5, BS])
        hh, hT = s.sb("hh", [P, BS, D]), s.sb("hT", [P, NPAIR * P])
        x3, row = s.sb("x3", [P, 2, BS, D]), s.sb("row", [P, 2, BS, D2])
        tp, mr, mo = s.ps("tp", [P, 2, 512]), s.ps("mr", [P, 2, 512]), s.ps("mo", [P, 2, 512])
        in_landed, in_free = s.sems("in_landed"), s.sems("in_free")
        out_ready, out_free, out_stored = s.sems("out_ready"), s.sems("out_free"), s.sems("out_stored")
        var_ready, std_ready = s.sem("var_ready"), s.sem("std_ready")
        h_ready, tp_ready, hT_ready, mm_ready = s.sem("h_ready"), s.sem("tp_ready"), s.sem("hT_ready"), s.sem("mm_ready")
        block = s.ctx.enter_context(nc.Block())

        @block.sync
        def _(sp):
            with sp.Fori(0, IT) as i:
                for h in range(2):
                    sp.wait_ge(in_free[h], i + 1)
                    sp.dma_start(x2[:, h, :, :], block_of(g.x2, i, h, D)).then_inc(in_landed[h], 16)
                    sp.dma_start(h2[:, h, :, :], block_of(g.tab_h2, i, h, H2ROW)).then_inc(in_landed[h], 16)
                    for q in range(NAGG):
                        sp.dma_start(agg[:, h, q, :, :], block_of(g.agg[q], i, h, H2ROW)).then_inc(in_landed[h], 16)

        @block.gpsimd
        def _(pool):
            pool.sem_inc(out_free[0], 1)
            pool.sem_inc(out_free[1], 1)
            with pool.Fori(0, IT) as i:
                for h in range(2):
                    pool.wait_ge(out_ready[h], i + 1)
                    pool.dma_start(block_of(g.x3, i, h, D), x3[:, h, :, :]).then_inc(out_stored[h], 16)
                    pool.dma_start(block_of(g.tab_h3, i, h, D2), row[:, h, :, :]).then_inc(out_stored[h], 16)
                    pool.wait_ge(out_stored[h], (i + 1) * 32)
                    pool.sem_inc(out_free[h], 1)

        @block.vector
        def _(dve):
            dve.sem_inc(in_free[0], 1)
            dve.sem_inc(in_free[1], 1)
            with dve.Fori(0, IT) as i:
                for h in range(2):
                    dve.wait_ge(in_landed[h], (i + 1) * (16 * (2 + NAGG)))
                    dve.tensor_tensor(a[:, :, :], agg[:, h, 0, :, :], agg[:, h, 1, :, :], ALU.add)
                    dve.tensor_tensor(agg[:, h, 2, :, :], agg[:, h, 2, :, :], agg[:, h, 3, :, :], ALU.add)
                    dve.drain()
                    dve.tensor_tensor(a[:, :, :], a[:, :, :], agg[:, h, 2, :, :], ALU.add)
                    dve.drain()
                    dve.tensor_scalar(st[:, 0, :], a[:, :, D], 1e-8, None, ALU.max)
                    dve.drain()
                    dve.reciprocal(st[:, 1, :], st[:, 0, :])
                    dve.drain()
                    dve.tensor_tensor(b[:, :, :], a[:, :, 0:D], over_features(st[:, 1, :]), ALU.mult)
                    dve.drain()
                    dve.tensor_tensor(b[:, :, :], b[:, :, :], h2[:, h, :, 0:D], ALU.add)
                    dve.drain()
                    layernorm(dve, b[:, :, :], hh[:, :, :], sq[:, :, :], st, var_ready, std_ready, (2 * i + h) * 2 + 1, relu=False)
                    dve.tensor_tensor(hh[:, :, :], hh[:, :, :], over_columns(g.gamma[:, :]), ALU.mult)
                    dve.tensor_tensor(b[:, :, :], x2[:, h, :, :], over_columns(g.beta[:, :]), ALU.add)
                    dve.drain()
                    dve.sem_inc(in_free[h], 1)
                    dve.wait_ge(out_free[h], i + 1)
                    dve.tensor_tensor(x3[:, h, :, :], hh[:, :, :], b[:, :, :], ALU.add)
                    dve.drain()
                    layernorm(dve, x3[:, h, :, :], hh[:, :, :], sq[:, :, :], st, var_ready, std_ready, (2 * i + h) * 2 + 2)
                    dve.sem_inc(h_ready, 1)
                    dve.wait_ge(mm_ready, 2 * i + h + 1)
                    for c, piece in products(mr):
                        dve.tensor_copy(row[:, h, c, 0:D], piece)
                    for c, piece in products(mo):
                        last = dve.tensor_tensor(row[:, h, c, D:D2], piece, over_columns(g.b_l1[:, :], c.stop - c.start), ALU.add)
                    last.then_inc(out_ready[h], 1)

        @block.scalar
        def _(act):
            with act.Fori(0, IT) as i:
                for h in range(2):
                    take_std(act, nc, st, var_ready, std_ready, (2 * i + h) * 2 + 1)
                    take_std(act, nc, st, var_ready, std_ready, (2 * i + h) * 2 + 2)
                    act.wait_ge(tp_ready, 2 * i + h + 1)
                    copy_turned(nc, hT, tp).then_inc(hT_ready, 1)

        @block.tensor
        def _(pe):
            with pe.Fori(0, IT) as i:
                for h in range(2):
                    pe.wait_ge(h_ready, 2 * i + h + 1)
                    transpose_pairs(pe, tp, hh, g.ident[:, :]).then_inc(tp_ready, 1)
                    pe.wait_ge(hT_ready, 2 * i + h + 1)
                    multiply_pairs(pe, mr, [(hT, g.w_rel1[:, :], D2)])
                    multiply_pairs(pe, mo, [(hT, g.w_root1[:, :], D2)]).then_inc(mm_ready, 1)


def node_stage_out(nc, io, g):
    with Stage(nc, "out") as s:
        rows, idx_now = s.sb("rows", [P, 2, BS, D2]), s.sb("idx_now", [P, 2 * BS], I32)
        x3, own = s.sb("x3", [P, 2, BS, D]), s.sb("own", [P, 2, BS, D2])
        ab = s.sb("ab", [P, 2, BS, D])
        aT, bT = s.sb("aT", [P, NPAIR * P]), s.sb("bT", [P, NPAIR * P])
        res = s.sb("res", [P, 2, BS, D])
        ta, tb, mm = s.ps("ta", [P, 2, 512]), s.ps("tb", [P, 2, 512]), s.ps("mm", [P, 2, 512])
        slot_free, landed, idx_staged, begun = s.sems("slot_free"), s.sems("landed"), s.sem("idx_staged"), s.sem("begun")
        in_landed, in_free = s.sems("in_landed"), s.sems("in_free")
        ab_ready, tp_ready, xT_ready, mm_ready = s.sem("ab_ready"), s.sem("tp_ready"), s.sem("xT_ready"), s.sem("mm_ready")
        out_ready, out_free, out_stored = s.sems("out_ready"), s.sems("out_free"), s.sems("out_stored")
        block = s.ctx.enter_context(nc.Block())

        @block.gpsimd
        def _(pool):
            gather_rows(pool, g.tab_both2, g.last_node, idx_now, rows, D2, slot_free, landed, idx_staged, begun)

        @block.scalar
        def _(act):
            with act.Fori(0, IT) as i:
                for h in range(2):
                    act.wait_ge(in_free[h], i + 1)
                    act.dma_start(x3[:, h, :, :], block_of(g.x3, i, h, D)).then_inc(in_landed[h], 16)
                    act.dma_start(own[:, h, :, :], block_of(g.tab_h3, i, h, D2)).then_inc(in_landed[h], 16)
                    act.wait_ge(tp_ready, 2 * i + h + 1)
                    copy_turned(nc, aT, ta)
                    copy_turned(nc, bT, tb).then_inc(xT_ready, 1)

        @block.sync
        def _(sp):
            sp.sem_inc(out_free[0], 1)
            sp.sem_inc(out_free[1], 1)
            with sp.Fori(0, IT) as i:
                for h in range(2):
                    sp.wait_ge(out_ready[h], i + 1)
                    sp.dma_start(block_of(io.out, i, h, D), res[:, h, :, :]).then_inc(out_stored[h], 16)
                    sp.wait_ge(out_stored[h], (i + 1) * 16)
                    sp.sem_inc(out_free[h], 1)

        @block.vector
        def _(dve):
            for q in slot_free + in_free:
                dve.sem_inc(q, 1)
            with dve.Fori(0, IT) as i:
                for h in range(2):
                    dve.wait_ge(landed[h], (i + 1) * (16 * BS))
                    dve.wait_ge(in_landed[h], (i + 1) * 32)
                    dve.tensor_tensor(ab[:, 1, :, :], rows[:, h, :, 0:D], own[:, h, :, D:D2], ALU.add)
                    dve.tensor_copy(ab[:, 0, :, :], rows[:, h, :, D:D2])
                    dve.drain()
                    dve.sem_inc(slot_free[h], 1)
                    dve.tensor_scalar(ab[:, 1, :, :], ab[:, 1, :, :], 0.0, None, ALU.max).then_inc(ab_ready, 1)
                    dve.wait_ge(out_free[h], i + 1)
                    dve.tensor_tensor(res[:, h, :, :], x3[:, h, :, :], over_columns(g.b_l2[:, :]), ALU.add)
                    dve.drain()
                    dve.wait_ge(mm_ready, 2 * i + h + 1)
                    for c, piece in products(mm):
                        last = dve.tensor_tensor(res[:, h, c, :], res[:, h, c, :], piece, ALU.add)
                    last.then_inc(out_ready[h], 1)
                    dve.drain()
                    dve.sem_inc(in_free[h], 1)

        @block.tensor
        def _(pe):
            with pe.Fori(0, IT) as i:
                for h in range(2):
                    pe.wait_ge(ab_ready, 2 * i + h + 1)
                    transpose_pairs(pe, ta, ab[:, 0, :, :], g.ident[:, :])
                    transpose_pairs(pe, tb, ab[:, 1, :, :], g.ident[:, :]).then_inc(tp_ready, 1)
                    pe.wait_ge(xT_ready, 2 * i + h + 1)
                    multiply_pairs(pe, mm, [(aT, g.w_rel2[:, :], D2), (bT, g.w_root2[:, :], D2)]).then_inc(mm_ready, 1)



def propagate(nc, g, name, kind, table, w, idx, to, u_old=None, u_new=None, k=0, acc_in=None, acc_out=None,
              merge=None):
    wide = D2 if merge is not None else D
    with Stage(nc, name) as s:
        rows, idx_now = s.sb("rows", [P, 2, BS, w]), s.sb("idx_now", [P, 2 * BS], I32)
        sc = s.sb("sc", [P, 2, NSC * BS])
        val, tmp = s.sb("val", [P, 2, BS, D]), s.sb("tmp", [P, BS, D])
        sums = s.sb("sums", [P, 2, BS, wide])
        fix, part, fixed = s.sb("fix", [P, D]), s.sb("part", [P, D]), s.sb("fixed", [P, wide])
        pfix = s.ps("pfix", [P, 512])
        has_acc = acc_in is not None or acc_out is not None
        acc = s.sb("acc", [P, 2, BS, D]) if has_acc else None
        slot_free, landed, idx_staged, begun = s.sems("slot_free"), s.sems("landed"), s.sem("idx_staged"), s.sem("begun")
        sc_free, sc_ready = s.sems("sc_free"), s.sem("sc_ready")
        in_landed = s.sems("in_landed")
        out_ready, out_free, out_stored = s.sems("out_ready"), s.sems("out_free"), s.sems("out_stored")
        fix_ready, fix_done, fix_copied, fix_stored, old_fix = (
            s.sem("fix_ready"), s.sem("fix_done"), s.sem("fix_copied"), s.sem("fix_stored"), s.sem("old_fix"))
        if kind == "jacobi_first":
            sq, st = s.sb("sq", [P, BS, D]), s.sb("st", [P, 5, BS])
            var_ready, std_ready = s.sem("var_ready"), s.sem("std_ready")
        if kind == "cheb_last":
            xu = [s.sb(f"xu{q}", [P, BS, D]) for q in range(2)]
            uT = [s.sb(f"uT{q}", [P, NPAIR * P]) for q in range(3)]
            tp = [s.ps(f"tp{q}", [P, 2, 512]) for q in range(2)]
            mm = s.ps("mm", [P, 2, 512])
            xu_ready, xu_turned, xu_copied, v_ready, v_turned, v_copied, mm_ready = (
                s.sem(n) for n in ("xu_ready", "xu_turned", "xu_copied", "v_ready", "v_turned", "v_copied", "mm_ready"))
        n_in = (acc_in is not None) + (merge is not None)
        n_out = 1 + (acc_out is not None)
        def staged(h, kind_of_scalar):
            return sc[:, h, kind_of_scalar * BS:(kind_of_scalar + 1) * BS]
        block = s.ctx.enter_context(nc.Block())

        @block.gpsimd
        def _(pool):
            gather_rows(pool, table, idx, idx_now, rows, w, slot_free, landed, idx_staged, begun)

        @block.scalar
        def _(act):
            flat = g.sc[:, :, :, :].rearrange("p b k c -> p (b k c)")
            with act.Fori(0, IT) as i:
                for h in range(2):
                    act.wait_ge(sc_free[h], i + 1)
                    nc.scalar.copy(sc[:, h, :], flat[:, bass.ds((2 * i + h) * (NSC * BS), NSC * BS)]).then_inc(sc_ready, 1)
                    if n_in:
                        act.wait_ge(out_free[h], i + 1)
                    if acc_in is not None:
                        act.dma_start(acc[:, h, :, :], block_of(acc_in, i, h, D)).then_inc(in_landed[h], 16)
                    if merge is not None:
                        act.dma_start(sums[:, h, :, 0:D], block_of(merge, i, h, D)).then_inc(in_landed[h], 16)
                    if kind == "jacobi_first":
                        take_std(act, nc, st, var_ready, std_ready, 2 * i + h + 1)
                    if kind == "cheb_last":
                        for q, u in enumerate((u_old, u_new)):
                            last = nc.scalar.copy(xu[q][:, :, :], u[:, bass.ds((2 * i + h) * BS, BS), :])
                        last.then_inc(xu_ready, 1)
                        act.wait_ge(xu_turned, 2 * i + h + 1)
                        for q in range(2):
                            last = copy_turned(nc, uT[q], tp[q])
                        last.then_inc(xu_copied, 1)
                        act.wait_ge(v_turned, 2 * i + h + 1)
                        copy_turned(nc, uT[2], tp[0]).then_inc(v_copied, 1)
            if merge is not None:
                act.dma_start(fixed[:, 0:D], merge[NPAD:NPAD + P, :]).then_inc(old_fix, 16)
            act.wait_ge(fix_done, 1)
            nc.scalar.copy(fixed[:, wide - D:wide], pfix[:, 0:D]).then_inc(fix_copied, 1)
            act.wait_ge(fix_copied, 1)
            if merge is not None:
                act.wait_ge(old_fix, 16)
            act.dma_start(to[NPAD:NPAD + P, :], fixed[:, :]).then_inc(fix_stored, 16)
            act.wait_ge(fix_stored, 16)

        @block.sync
        def _(sp):
            sp.sem_inc(out_free[0], 1)
            sp.sem_inc(out_free[1], 1)
            with sp.Fori(0, IT) as i:
                for h in range(2):
                    sp.wait_ge(out_ready[h], i + 1)
                    sp.dma_start(block_of(to, i, h, wide), sums[:, h, :, :]).then_inc(out_stored[h], 16)
                    if acc_out is not None:
                        sp.dma_start(block_of(acc_out, i, h, D), acc[:, h, :, :]).then_inc(out_stored[h], 16)
                    sp.wait_ge(out_stored[h], (i + 1) * (16 * n_out))
                    sp.sem_inc(out_free[h], 1)

        @block.tensor
        def _(pe):
            if kind == "cheb_last":
                with pe.Fori(0, IT) as i:
                    for h in range(2):
                        pe.wait_ge(xu_ready, 2 * i + h + 1)
                        for q in range(2):
                            last = transpose_pairs(pe, tp[q], xu[q], g.ident[:, :])
                        last.then_inc(xu_turned, 1)
                        pe.wait_ge(v_ready, 2 * i + h + 1)
                        pe.wait_ge(xu_copied, 2 * i + h + 1)
                        transpose_pairs(pe, tp[0], val[:, h, :, :], g.ident[:, :]).then_inc(v_turned, 1)
                        pe.wait_ge(v_copied, 2 * i + h + 1)
                        multiply_pairs(pe, mm, [(uT[q], g.wu[q][:, :], D2) for q in range(3)]).then_inc(mm_ready, 1)
            pe.wait_ge(fix_ready, 1)
            pe.matmul(pfix[:, 0:D], g.carries[:, :], part[:, :], start=True, stop=False)
            pe.matmul(pfix[:, 0:D], g.ident[:, :], fix[:, :], start=False, stop=True).then_inc(fix_done, 1)

        @block.vector
        def _(dve):
            dve.memset(fix[:, :], 0.0)
            dve.memset(sums[:, 1, BS - 1, :], 0.0)
            dve.drain()
            for q in slot_free + sc_free:
                dve.sem_inc(q, 1)
            with dve.Fori(0, IT) as i:
                for h in range(2):
                    here = bass.ds((2 * i + h) * BS, BS)
                    got, v = rows[:, h, :, :], val[:, h, :, :]
                    dve.wait_ge(sc_ready, 2 * i + h + 1)
                    dve.wait_ge(landed[h], (i + 1) * (16 * BS))
                    if kind == "cheb_first":
                        t1 = tmp[:, 0, 0:BS]
                        def put(which):
                            return g.sc[:, :, :, :].rearrange("p b k c -> p (b k c)")[
                                :, bass.ds((2 * i + h) * (NSC * BS) + which * BS, BS)]
                        dis, dinv = got[:, :, EX], got[:, :, EX + 1]
                        dve.tensor_tensor(t1, staged(h, EW), dis, ALU.mult)
                        dve.tensor_tensor(put(D1), dinv, dinv, ALU.mult)
                        dve.tensor_scalar(put(NDIS), dis, -1.0, None, ALU.mult)
                        dve.tensor_copy(put(DINV), dinv)
                        dve.tensor_copy(put(ZSRC), got[:, :, EX + 3])
                        dve.tensor_copy(g.last_src[:, here], got[:, :, EX + 2])
                        dve.drain()
                        dve.scalar_tensor_tensor(put(D0), t1, -1.0, dis, ALU.mult, ALU.mult)
                        dve.tensor_tensor(v, got[:, :, D:2 * D], over_features(t1), ALU.mult)
                        dve.wait_ge(out_free[h], i + 1)
                        dve.tensor_copy(acc[:, h, :, :], got[:, :, 0:D])
                        dve.drain()
                    elif kind == "cheb":
                        dve.tensor_tensor(v, got[:, :, 0:D], over_features(staged(h, D0)), ALU.mult)
                        dve.drain()
                    elif kind == "cheb_last":
                        dve.tensor_tensor(tmp[:, :, :], got[:, :, 0:D], over_features(staged(h, D0)), ALU.mult)
                        dve.drain()
                        dve.scalar_tensor_tensor(v, tmp[:, :, :], 2.0, u_old[:, here, :], ALU.mult, ALU.subtract).then_inc(v_ready, 1)
                        dve.wait_ge(mm_ready, 2 * i + h + 1)
                        for c, piece in products(mm):
                            dve.tensor_copy(v[:, c, :], piece)
                        dve.drain()
                    elif kind == "jacobi_first":
                        dve.tensor_tensor(tmp[:, :, :], got[:, :, 0:D], over_features(staged(h, NDIS)), ALU.mult)
                        dve.drain()
                        dve.wait_ge(in_landed[h], (i + 1) * (16 * n_in))
                        dve.tensor_tensor(tmp[:, :, :], acc[:, h, :, :], tmp[:, :, :], ALU.add)
                        dve.drain()
                        layernorm(dve, tmp[:, :, :], v, sq[:, :, :], st, var_ready, std_ready, 2 * i + h + 1)
                        dve.tensor_tensor(v, v, over_features(staged(h, DINV)), ALU.mult)
                        dve.drain()
                        dve.tensor_scalar(acc[:, h, :, :], v, g.omega[:, 0:1], None, ALU.mult)
                    elif kind == "jacobi":
                        if k == 1:
                            dve.tensor_tensor(v, got[:, :, 0:D], over_features(staged(h, D1)), ALU.mult)
                        else:
                            dve.tensor_tensor(tmp[:, :, :], got[:, :, 0:D], over_features(staged(h, D1)), ALU.mult)
                            dve.drain()
                            dve.scalar_tensor_tensor(v, u_old[:, here, :], BETA[k], tmp[:, :, :], ALU.mult, ALU.add)
                        dve.drain()
                        dve.wait_ge(in_landed[h], (i + 1) * (16 * n_in))
                        to_acc = v if k == K1 - 1 else acc[:, h, :, :]
                        dve.scalar_tensor_tensor(to_acc, v, g.omega[:, k:k + 1], acc[:, h, :, :], ALU.mult, ALU.add)
                    elif kind == "conv_first":
                        dve.tensor_copy(v, got[:, :, 0:D])
                        dve.wait_ge(out_free[h], i + 1)
                        dve.tensor_copy(acc[:, h, :, :], got[:, :, D:D2])
                    elif kind == "conv_last":
                        dve.wait_ge(in_landed[h], (i + 1) * (16 * n_in))
                        dve.tensor_tensor(tmp[:, :, :], got[:, :, 0:D], acc[:, h, :, :], ALU.add)
                        dve.drain()
                        dve.tensor_scalar(v, tmp[:, :, :], 0.0, None, ALU.max)
                    dve.drain()
                    dve.sem_inc(slot_free[h], 1)
                    if u_new is not None and kind != "cheb_last":
                        dve.tensor_copy(u_new[:, here, :], v)
                    dve.wait_ge(out_free[h], i + 1)
                    for f in range(D):
                        last = dve.tensor_tensor_scan(sums[:, h, :, wide - D + f], staged(h, SAME), v[:, :, f],
                                                      sums[:, 1 - h, BS - 1, wide - D + f:wide - D + f + 1], ALU.mult, ALU.add)
                    last.then_inc(out_ready[h], 1)
                    dve.tensor_tensor(tmp[:, :, :], v, over_features(staged(h, FIRST)), ALU.mult)
                    dve.drain()
                    dve.sem_inc(sc_free[h], 1)
                    dve.reduce_sum(part[:, :], tmp[:, :, :].rearrange("p c f -> p f c"), AX)
                    dve.drain()
                    dve.tensor_tensor(fix[:, :], fix[:, :], part[:, :], ALU.add)
                    dve.drain()
            dve.tensor_copy(part[:, :], sums[:, 1, BS - 1, wide - D:wide]).then_inc(fix_ready, 1)



def message_stage(nc, io, g):
    with Stage(nc, "msg") as s:
        rows, idx_now = s.sb("rows", [P, 2, BS, H2ROW]), s.sb("idx_now", [P, 2 * BS], I32)
        cw, dist = s.sb("cw", [P, COLS]), s.sb("dist", [P, COLS])
        sc = s.sb("sc", [P, 2, 2 * BS])
        attr, aT, g1 = s.sb("attr", [P, 2, BS, R]), s.sb("aT", [P, NPAIR * P]), s.sb("g1", [P, NPAIR * P])
        one, oneT = s.sb("one", [P, BS, P], F16), s.sb("oneT", [P, BS, P])
        ident_h = s.sb("ident_h", [P, P], F16)
        gate, junk, adapt, wgt = s.sb("gate", [P, BS, D]), s.sb("junk", [P, P]), s.sb("adapt", [P, BS]), s.sb("wgt", [P, BS])
        msg = s.sb("msg", [P, 2, BS, H2ROW])
        half_pi = s.sb("half_pi", [P, 1])
        zeros = s.sb("zeros", [P, BS * H2ROW])
        tp, ph = s.ps("tp", [P, 2, 512]), s.ps("ph", [P, 2, 512])
        pone, pterm = s.ps("pone", [P, 2, 1024], F16), s.ps("pterm", [P, 2, 512])
        HB = BS // 2
        slot_free, landed, idx_staged, begun = s.sems("slot_free"), s.sems("landed"), s.sem("idx_staged"), s.sem("begun")
        dist_landed, dist_ready, cos_ready, cw_ready, zeroed = (s.sem(n) for n in (
            "dist_landed", "dist_ready", "cos_ready", "cw_ready", "zeroed"))
        sc_free, sc_ready = s.sems("sc_free"), s.sem("sc_ready")
        attr_landed, attr_free = s.sems("attr_landed"), s.sem("attr_free")
        attr_turned, attr_copied, hid_ready, silu_done, gate_ready, gate_read = (s.sem(n) for n in (
            "attr_turned", "attr_copied", "hid_ready", "silu_done", "gate_ready", "gate_read"))
        one_ready, one_turned, one_copied, term_ready, term_read = (s.sem(n) for n in (
            "one_ready", "one_turned", "one_copied", "term_ready", "term_read"))
        out_ready, out_free, out_stored = s.sems("out_ready"), s.sems("out_free"), s.sems("out_stored")
        cleared = s.sem("cleared")
        block = s.ctx.enter_context(nc.Block())

        @block.gpsimd
        def _(pool):
            gather_rows(pool, g.tab_h2, g.dst_idx, idx_now, rows, H2ROW, slot_free, landed, idx_staged, begun)

        @block.sync
        def _(sp):
            sp.dma_start(dist[:, :], io.edge_weight.rearrange("(p c) -> p c", p=P)).then_inc(dist_landed, 16)
            sp.sem_inc(out_free[0], 1)
            sp.sem_inc(out_free[1], 1)
            sp.wait_ge(zeroed, 1)
            for q in range(NAGG):
                sp.dma_start(g.agg[q][0:NPAD, :].rearrange("(p b c) w -> p b (c w)", p=P, c=BS),
                             zeros[:, :].unsqueeze(1).broadcast_to([P, NB, BS * H2ROW])).then_inc(cleared, 16)
                sp.dma_start(g.agg[q][NPAD:NPAD + P, :], zeros[:, 0:H2ROW]).then_inc(cleared, 16)
            with sp.Fori(0, IT) as i:
                for h in range(2):
                    sp.wait_ge(out_ready[h], i + 1)
                    sp.dma_start(block_of(g.msg, i, h, H2ROW), msg[:, h, :, :]).then_inc(out_stored[h], 16)
                    sp.wait_ge(out_stored[h], (i + 1) * 16)
                    sp.sem_inc(out_free[h], 1)
            sp.wait_ge(cleared, 32 * NAGG)

        @block.scalar
        def _(act):
            act.wait_ge(dist_ready, 1)
            nc.scalar.activation(cw[:, :], dist[:, :], ACT.Sin, bias=half_pi[:, 0:1], scale=-math.pi / CUTOFF
                                 ).then_inc(cos_ready, 1)
            act.wait_ge(cw_ready, 1)
            flat = g.sc[:, :, :, :].rearrange("p b k c -> p (b k c)")
            with act.Fori(0, IT) as i:
                for h in range(2):
                    act.wait_ge(sc_free[h], i + 1)
                    nc.scalar.copy(sc[:, h, 0:BS], cw[:, bass.ds((2 * i + h) * BS, BS)])
                    nc.scalar.copy(sc[:, h, BS:2 * BS], flat[:, bass.ds((2 * i + h) * (NSC * BS) + ZSRC * BS, BS)]
                                   ).then_inc(sc_ready, 1)
                    act.wait_ge(attr_free, 2 * i + h + 1)
                    act.dma_start(attr[:, h, :, :], block_of(io.edge_attr, i, h, R)).then_inc(attr_landed[h], 16)
                    act.wait_ge(attr_turned, 2 * i + h + 1)
                    copy_turned(nc, aT, tp, 2 * R).then_inc(attr_copied, 1)
                    act.wait_ge(hid_ready, 2 * i + h + 1)
                    n = 4 * P
                    nc.scalar.activation(g1[0:D2, 0:n], ph[0:D2, 0, 0:n], ACT.Silu, bias=g.b1[:, 0:1])
                    nc.scalar.activation(g1[0:D2, n:NPAIR * P], ph[0:D2, 1, 0:NPAIR * P - n], ACT.Silu,
                                         bias=g.b1[:, 0:1]).then_inc(silu_done, 1)
                    act.wait_ge(one_turned, 2 * i + h + 1)
                    nc.scalar.copy(oneT[:, 0:8, :].rearrange("p c e -> p (c e)"), pone[:, 0, :])
                    nc.scalar.copy(oneT[:, 8:BS, :].rearrange("p c e -> p (c e)"), pone[:, 1, 0:(BS - 8) * P]).then_inc(one_copied, 1)

        @block.tensor
        def _(pe):
            pe.sem_inc(attr_free, 2)
            with pe.Fori(0, IT) as i:
                for h in range(2):
                    n = 2 * i + h + 1
                    pe.wait_ge(one_ready, n)
                    for c in range(BS):
                        last = pe.transpose(pone[:, c // 8, (c % 8) * P:(c % 8 + 1) * P], one[:, c, :], ident_h[:, :])
                    last.then_inc(one_turned, 1)
                    pe.wait_ge(attr_landed[h], (i + 1) * 16)
                    pe.wait_ge(gate_read, n)
                    transpose_pairs(pe, tp, attr[:, h, :, :], g.ident[:, :], 2 * R).then_inc(attr_turned, 1)
                    pe.wait_ge(attr_copied, n)
                    pe.sem_inc(attr_free, 1)
                    pe.matmul(ph[0:D2, 0, :], g.W1[:, :], aT[0:2 * R, 0:4 * P], start=True, stop=True)
                    pe.matmul(ph[0:D2, 1, 0:(NPAIR - 4) * P], g.W1[:, :], aT[0:2 * R, 4 * P:NPAIR * P], start=True,
                              stop=True).then_inc(hid_ready, 1)
                    pe.wait_ge(silu_done, n)
                    multiply_pairs(pe, tp, [(g1, g.W2[:, :], D2)]).then_inc(gate_ready, 1)
                    pe.wait_ge(one_copied, n)
                    for half in range(2):
                        pe.wait_ge(term_read, (2 * i + h) * 2 + half + 1)
                        for c in range(HB):
                            last = pe.matmul(pterm[:, c // 4, (c % 4) * P:(c % 4) * P + NZ], oneT[0:NZ, half * HB + c, :],
                                             g.pair_term[:, :], start=True, stop=True)
                        last.then_inc(term_ready, 1)

        @block.vector
        def _(dve):
            dve.memset(zeros[:, :], 0.0).then_inc(zeroed, 1)
            dve.memset(half_pi[:, :], math.pi / 2)
            dve.memset(msg[:, :, :, D + 1:H2ROW], 0.0)
            dve.tensor_copy(ident_h[:, :], g.ident[:, :])
            dve.wait_ge(dist_landed, 16)
            dve.tensor_scalar(cw[:, :], dist[:, :], CUTOFF, 0.5, ALU.is_lt, ALU.mult)
            dve.drain()
            dve.tensor_copy(g.half_keep[:, :], cw[:, :])
            dve.scalar_tensor_tensor(dist[:, :], dist[:, :], -1.0, dist[:, :], ALU.mult, ALU.max)
            dve.drain()
            dve.tensor_scalar(dist[:, :], dist[:, :], CUTOFF, None, ALU.min)
            dve.drain()
            dve.sem_inc(dist_ready, 1)
            dve.wait_ge(cos_ready, 1)
            dve.scalar_tensor_tensor(cw[:, :], cw[:, :], 1.0, g.half_keep[:, :], ALU.add, ALU.mult).then_inc(cw_ready, 1)
            for q in slot_free + sc_free:
                dve.sem_inc(q, 1)
            dve.sem_inc(gate_read, 1)
            dve.sem_inc(term_read, 1)
            with dve.Fori(0, IT) as i:
                for h in range(2):
                    n = 2 * i + h + 1
                    got, m = rows[:, h, :, :], msg[:, h, :, :]
                    dve.wait_ge(sc_ready, n)
                    for c in range(BS):
                        last = dve.tensor_scalar(one[:, c, :], g.iota[:, :], sc[:, h, BS + c:BS + c + 1], None, ALU.is_equal)
                    last.then_inc(one_ready, 1)
                    dve.wait_ge(gate_ready, n)
                    for c, piece in products(tp):
                        last = dve.tensor_tensor(gate[:, c, :], piece, over_columns(g.b2[:, :], c.stop - c.start), ALU.add)
                    last.then_inc(gate_read, 1)
                    dve.wait_ge(landed[h], (i + 1) * (16 * BS))
                    dve.tensor_tensor(wgt[:, :], sc[:, h, 0:BS], got[:, :, D + 1], ALU.mult)
                    for half in range(2):
                        dve.wait_ge(term_ready, (2 * i + h) * 2 + half + 1)
                        for c in range(HB):
                            cc = half * HB + c
                            last = dve.scalar_tensor_tensor(
                                junk[:, 0:NZ], g.iota[:, 0:NZ], got[:, cc, D:D + 1],
                                pterm[:, c // 4, (c % 4) * P:(c % 4) * P + NZ],
                                ALU.is_equal, ALU.mult, accum_out=adapt[:, cc:cc + 1])
                            dve.drain()
                        dve.sem_inc(term_read, 1)
                    dve.tensor_tensor(gate[:, :, :], gate[:, :, :], over_features(adapt[:, :]), ALU.add)
                    dve.wait_ge(out_free[h], i + 1)
                    dve.tensor_tensor(m[:, :, 0:D], got[:, :, 0:D], over_features(wgt[:, :]), ALU.mult)
                    dve.tensor_copy(m[:, :, D], got[:, :, D + 1])
                    dve.drain()
                    dve.sem_inc(slot_free[h], 1)
                    dve.sem_inc(sc_free[h], 1)
                    dve.tensor_tensor(m[:, :, 0:D], m[:, :, 0:D], gate[:, :, :], ALU.mult).then_inc(out_ready[h], 1)
                    dve.drain()


def add_up_stage(nc, io, g):
    with Stage(nc, "add") as s:
        msg, out = s.sb("msg", [P, 2, BS, H2ROW]), s.sb("out", [P, 2, BS, H2ROW])
        src_row = s.sb("src_row", [P, 2, BS, P])
        srcs = s.sb("srcs", [P, 2, BS])
        same, junk, before = s.sb("same", [P, 2, BS, P]), s.sb("junk", [P, P]), s.sb("before", [P, BS])
        dump_i, dump = s.sb("dump_i", [P, 1], I32), s.sb("dump", [P, 1])
        where = s.sb("where", [P, 2, BS], I32)
        t0 = s.sb("t0", [P, 2, BS])
        ps = [s.ps(f"ps{h}", [P, 2, 512]) for h in range(2)]
        HB = BS // 2
        in_landed, in_free = s.sems("in_landed"), s.sems("in_free")
        dump_ready = s.sem("dump_ready")
        same_ready, summed, copied = s.sem("same_ready"), s.sem("summed"), s.sem("copied")
        where_ready = s.sem("where_ready")
        slot_done = s.sems("slot_done")
        srcs_ready, srcs_free = s.sem("srcs_ready"), s.sems("srcs_free")
        added, begun = s.sems("added", NAGG), s.sem("begun")
        block = s.ctx.enter_context(nc.Block())

        @block.sync
        def _(sp):
            with sp.Fori(0, IT) as i:
                for h in range(2):
                    sp.wait_ge(in_free[h], i + 1)
                    sp.dma_start(msg[:, h, :, :], block_of(g.msg, i, h, H2ROW)).then_inc(in_landed[h], 16)
                    sp.dma_start(src_row[:, h, :, :].rearrange("p c e -> p (c e)"),
                                 g.src_cols[bass.ds((2 * i + h) * BS, BS), :].rearrange("c e -> (c e)").partition_broadcast(P)
                                 ).then_inc(in_landed[h], 16)

        @block.scalar
        def _(act):
            with act.Fori(0, IT) as i:
                for h in range(2):
                    act.wait_ge(srcs_free[h], i + 1)
                    nc.scalar.copy(srcs[:, h, :], g.src_idx[:, bass.ds((2 * i + h) * BS, BS)]).then_inc(srcs_ready, 1)
                    act.wait_ge(summed, 2 * i + h + 1)
                    act.wait_ge(slot_done[h], i + 1)
                    for q in range(2):
                        last = nc.scalar.copy(out[:, h, q * HB:(q + 1) * HB, :].rearrange("p c w -> p (c w)"), ps[h][:, q, 0:HB * H2ROW])
                    last.then_inc(copied, 1)

        @block.tensor
        def _(pe):
            with pe.Fori(0, IT) as i:
                for h in range(2):
                    pe.wait_ge(same_ready, 2 * i + h + 1)
                    pe.wait_ge(slot_done[h], i + 1)
                    for c in range(BS):
                        last = pe.matmul(ps[h][:, c // HB, (c % HB) * H2ROW:(c % HB + 1) * H2ROW], same[:, h, c, :],
                                         msg[:, h, c, :], start=True, stop=True)
                    last.then_inc(summed, 1)
                    pe.wait_ge(summed, 2 * i + h + 1)
                    pe.sem_inc(in_free[h], 1)

        @block.vector
        def _(dve):
            for q in in_free + srcs_free:
                dve.sem_inc(q, 1)
            dve.wait_ge(dump_ready, 1)
            dve.tensor_copy(dump[:, :], dump_i[:, :])
            dve.drain()
            with dve.Fori(0, IT) as i:
                for h in range(2):
                    dve.wait_ge(in_landed[h], (i + 1) * 32)
                    dve.wait_ge(srcs_ready, 2 * i + h + 1)
                    for c in range(BS):
                        dve.tensor_scalar(same[:, h, c, :], src_row[:, h, c, :], srcs[:, h, c:c + 1], None, ALU.is_equal)
                    for c in range(BS):
                        dve.scalar_tensor_tensor(junk[:, :], src_row[:, h, c, :], srcs[:, h, c:c + 1], g.lower[:, :],
                                                 ALU.is_equal, ALU.mult, accum_out=before[:, c:c + 1])
                        dve.drain()
                    dve.sem_inc(same_ready, 1)
                    dve.tensor_scalar(t0[:, 0, :], before[:, :], 0.5, None, ALU.is_lt)
                    dve.tensor_scalar(t0[:, 1, :], srcs[:, h, :], dump[:, 0:1], None, ALU.subtract)
                    dve.drain()
                    dve.sem_inc(srcs_free[h], 1)
                    dve.tensor_tensor(t0[:, 1, :], t0[:, 1, :], t0[:, 0, :], ALU.mult)
                    dve.drain()
                    dve.wait_ge(slot_done[h], i + 1)
                    dve.tensor_scalar(where[:, h, :], t0[:, 1, :], dump[:, 0:1], None, ALU.add).then_inc(where_ready, 1)

        @block.gpsimd
        def _(pool):
            pool.iota(dump_i[:, :], pattern=[[0, 1]], base=NPAD, channel_multiplier=1).then_inc(dump_ready, 1)
            pool.sem_inc(slot_done[0], 1)
            pool.sem_inc(slot_done[1], 1)
            per = 2 * BS // NAGG
            with pool.Fori(0, IT) as i:
                for h in range(2):
                    pool.wait_ge(copied, 2 * i + h + 1)
                    pool.wait_ge(where_ready, 2 * i + h + 1)
                    pool.sem_inc(begun, 1)
                    for c in range(BS):
                        n = h * BS + c
                        if n >= NAGG:
                            pool.wait_ge(added[n % NAGG], i * (16 * per) + 16 * (n // NAGG))
                            pool.sem_inc(begun, 1)
                        pool.indirect_dma_start(
                            out=g.agg[n % NAGG], out_offset=bass.IndirectOffsetOnAxis(ap=where[:, h, c:c + 1], axis=0),
                            in_=out[:, h, c, :], in_offset=None, compute_op=ALU.add,
                        ).then_inc(added[n % NAGG], 16)
                for q in range(NAGG):
                    pool.wait_ge(added[q], (i + 1) * (16 * per))
                pool.sem_inc(slot_done[0], 1)
                pool.sem_inc(slot_done[1], 1)


def gnn_program(nc, args, out):
    with Stage(nc, "all") as s:
        io = Names()
        io.x, io.src, io.dst, io.edge_attr = args["x"], args["src"], args["dst"], args["edge_attr"]
        io.edge_weight, io.node_type, io.node_vec, io.w0 = args["edge_weight"], args["node_type"], args["node_vec"], args["w0"]
        io.bias0, io.lap, io.mf, io.W1 = args["bias0"], args["lap"], args["mf"], args["W1"]
        io.b1, io.W2, io.b2, io.emb = args["b1"], args["W2"], args["b2"], args["emb"]
        io.adaptW, io.gamma, io.beta, io.w_rel1 = args["adaptW"], args["gamma"], args["beta"], args["w_rel1"]
        io.w_root1, io.b_l1, io.w_rel2, io.w_root2 = args["w_root1"], args["b_l1"], args["w_rel2"], args["w_root2"]
        io.b_l2 = args["b_l2"]
        io.out = out
        g = Names()
        dram = lambda name, rows, w: nc.dram_tensor(name, [rows, w], F32).ap()
        g.tab_in = dram("tab_in", NPAD, W1ROW)
        g.tab_s = [dram("tab_s0", ROWS, D), dram("tab_s1", ROWS, D)]
        g.tab_a0, g.tab_a2 = dram("tab_a0", ROWS, D), dram("tab_a2", ROWS, D)
        g.tab_both, g.tab_both2 = dram("tab_both", ROWS, D2), dram("tab_both2", ROWS, D2)
        g.sum_tables = [(g.tab_s[0], D), (g.tab_s[1], D), (g.tab_a0, D), (g.tab_a2, D), (g.tab_both, D2), (g.tab_both2, D2)]
        g.edge_r, g.edge_acc, g.edge_q = dram("edge_r", NPAD, D), dram("edge_acc", NPAD, D), dram("edge_q", NPAD, D)
        g.x2, g.x3, g.tab_h2, g.tab_h3 = dram("x2", NPAD, D), dram("x3", NPAD, D), dram("tab_h2", NPAD, H2ROW), dram("tab_h3", NPAD, D2)
        g.msg = dram("msg", NPAD, H2ROW)
        g.agg = [dram(f"agg{q}", NPAD + P, H2ROW) for q in range(NAGG)]
        g.src_cols = dram("src_cols", COLS, P)

        g.ident, g.lower, g.carries, g.iota = s.sb("ident", [P, P]), s.sb("lower", [P, P]), s.sb("carries", [P, P]), s.sb("iota", [P, P])
        g.src_idx, g.dst_idx = s.sb("src_idx", [P, COLS], I32), s.sb("dst_idx", [P, COLS], I32)
        g.last_src, g.last_node = s.sb("last_src", [P, COLS], I32), s.sb("last_node", [P, COLS], I32)
        g.sc = s.sb("sc", [P, NB, NSC, BS])
        g.wh, g.wu = s.sb("wh", [D2, D2]), [s.sb(f"wu{k}", [D2, D2]) for k in range(3)]
        g.w_rel1, g.w_root1 = s.sb("w_rel1", [D2, D2]), s.sb("w_root1", [D2, D2])
        g.w_rel2, g.w_root2 = s.sb("w_rel2", [D2, D2]), s.sb("w_root2", [D2, D2])
        g.W1, g.W2, g.b1 = s.sb("W1", [2 * R, D2]), s.sb("W2", [D2, D2]), s.sb("b1", [D2, 1])
        g.bias0, g.b2, g.b_l1, g.b_l2 = s.sb("bias0", [P, D]), s.sb("b2", [P, D]), s.sb("b_l1", [P, D]), s.sb("b_l2", [P, D])
        g.gamma, g.beta = s.sb("gamma", [P, D]), s.sb("beta", [P, D])
        g.omega, g.p0w, g.pair_term = s.sb("omega", [P, K1]), s.sb("p0w", [P, 1]), s.sb("pair_term", [NZ, NZ])

        weight_stage(nc, io, g)
        with Stage(nc, "nodes") as ns:
            nodes = Names()
            nodes.ex = ns.sb("ex", [P, COLS, 5])
            count_stage(nc, io, g, nodes)
            node_stage_in(nc, io, g, nodes)
        with Stage(nc, "values") as vs:
            ua, ub = vs.sb("ua", [P, COLS, D]), vs.sb("ub", [P, COLS, D])
            s0, s1 = g.tab_s
            propagate(nc, g, "c0", "cheb_first", g.tab_in, W1ROW, g.src_idx, s0, u_new=ua, acc_out=g.edge_r)
            propagate(nc, g, "c1", "cheb", s0, D, g.last_src, s1, u_new=ub)
            propagate(nc, g, "c2", "cheb_last", s1, D, g.last_src, g.tab_a0, u_old=ua, u_new=ub)
            propagate(nc, g, "j0", "jacobi_first", g.tab_a0, D, g.last_src, s0, u_new=ua, acc_in=g.edge_r, acc_out=g.edge_acc)
            u, tab = (ua, ub), (s0, s1)
            for k in range(1, K1):
                end = k == K1 - 1
                propagate(nc, g, f"j{k}", "jacobi", tab[(k - 1) % 2], D, g.last_src, g.tab_both if end else tab[k % 2],
                          u_old=u[k % 2], u_new=None if end else u[k % 2], k=k, acc_in=g.edge_acc,
                          acc_out=None if end else g.edge_acc, merge=g.tab_a0 if end else None)
        node_stage_mid(nc, io, g)
        g.half_keep = s.sb("half_keep", [P, COLS])
        message_stage(nc, io, g)
        add_up_stage(nc, io, g)
        node_stage_late(nc, io, g)
        propagate(nc, g, "g0", "conv_first", g.tab_h3, D2, g.src_idx, g.tab_a2, acc_out=g.edge_q)
        propagate(nc, g, "g1", "conv_last", g.tab_a2, D, g.last_src, g.tab_both2, acc_in=g.edge_q, merge=g.tab_a2)
        node_stage_out(nc, io, g)


def kernel(**inputs):
    import numpy as np
    import concourse.bacc as bacc
    from concourse.bass_utils import run_bass_kernel_spmd

    def padded(name, value=0):
        a = np.asarray(inputs[name])
        out = np.full((NPAD,) + a.shape[1:], value, a.dtype)
        out[:N] = a
        return out

    arrays = {"x": padded("x"), "src": padded("src", NPAD - 1), "dst": padded("dst", NPAD - 1),
              "edge_attr": padded("edge_attr_40"), "edge_weight": padded("edge_weight"),
              "node_type": padded("node_type_119"), "node_vec": padded("node_vec")}
    for name, of in (("w0", "L0_gnn_weight"), ("bias0", "L0_gnn_bias"), ("lap", "L1_gnn_lap_coefs"),
                     ("mf", "L1_gnn_mf_weights"), ("W1", "L2_gnn_W1"), ("b1", "L2_gnn_b1"), ("W2", "L2_gnn_W2"),
                     ("b2", "L2_gnn_b2"), ("emb", "L2_gnn_emb"), ("adaptW", "L2_gnn_adaptW"), ("gamma", "L2_gnn_gamma"),
                     ("beta", "L2_gnn_beta"), ("w_rel1", "L3_gnn_w_rel1"), ("w_root1", "L3_gnn_w_root1"),
                     ("b_l1", "L3_gnn_b1"), ("w_rel2", "L3_gnn_w_rel2"), ("w_root2", "L3_gnn_w_root2"), ("b_l2", "L3_gnn_b2")):
        arrays[name] = np.ascontiguousarray(inputs[of])
    nc = bacc.Bacc("TRN2", target_bir_lowering=False, num_devices=1)
    args = {name: nc.dram_tensor(f"in_{name}", a.shape, mybir.dt.from_np(a.dtype), kind="ExternalInput").ap()
            for name, a in arrays.items()}
    out = nc.dram_tensor("out_x", [NPAD, D], F32, kind="ExternalOutput").ap()
    gnn_program(nc, args, out)
    r = run_bass_kernel_spmd(nc, [{f"in_{name}": a for name, a in arrays.items()}], core_ids=[0])
    return np.ascontiguousarray(r.results[0]["out_x"][:N])
```

```python
from contextlib import ExitStack
import math

import concourse.bass as bass
from concourse import mybir

ALU = mybir.AluOpType
ACT = mybir.ActivationFunctionType
AX = mybir.AxisListType.X
F32 = mybir.dt.float32
F16 = mybir.dt.float16
I32 = mybir.dt.int32

P = 128
N = 50000
D = 48
R = 40
NZ = 119
EMB = 32
BS = 14
COLS = 2 * BS * -(-N // (P * 2 * BS))
NB = COLS // BS
IT = NB // 2
NPAD = P * COLS
ZROW = NPAD + P
ROWS = NPAD + P + 1
NPAIR = BS // 2
D2 = 2 * D
W1ROW = 104
EX = 2 * D
H2ROW = 52
NAGG = 4
K1 = 10
CUTOFF = 6.0
EPS = 1e-5
ROUND = 12582912.0

SAME, FIRST, D0, D1, NDIS, DINV, ZSRC = range(7)
EW = D0
NSC = 7


def jacobi(n):
    if n == 1:
        return 2.0, 0.0
    m = 2 * n + 2
    return (m * (m - 1) * (m - 2) / (2 * n * (m - n) * (m - 2)),
            -2.0 * n * n * m / (2 * n * (m - n) * (m - 2)))


def jacobi_norms():
    out = []
    for i in range(K1 + 1):
        t1 = math.pow(2.0, 3.0) / (2 * i + 3.0)
        t2 = math.exp(math.lgamma(i + 2.0) - math.lgamma(i + 3.0))
        t3 = math.exp(math.lgamma(i + 2.0) - math.lgamma(i + 1.0))
        out.append(math.sqrt(t1 * t2 * t3))
    return out


SCALE = [1.0]
for _k in range(1, K1 + 1):
    SCALE.append(SCALE[-1] * jacobi(_k)[0])
BETA = [0.0, 0.0] + [jacobi(k)[1] * SCALE[k - 2] / SCALE[k] for k in range(2, K1 + 1)]


def over_features(scalars, w=D):
    return scalars.unsqueeze(2).broadcast_to([P, BS, w])


def over_columns(row, n=BS):
    return row.unsqueeze(1).broadcast_to([P, n, D])


def block_of(table, i, h, w):
    return table[0:NPAD, :].rearrange("(p c) w -> p c w", p=P)[:, bass.ds((2 * i + h) * BS, BS), 0:w]


def turned(tp, c):
    return tp[:, c // 4, (c % 4) * P:(c % 4 + 1) * P]


def product(mm, c):
    return mm[:, c // 5, (c % 5) * D2:(c % 5 + 1) * D2]


def products(mm):
    n = min(5, NPAIR)
    out = [(slice(0, 2 * n), mm[:, 0, 0:n * D2].rearrange("p (c f) -> p c f", f=D))]
    if NPAIR > n:
        out.append((slice(2 * n, BS), mm[:, 1, 0:(NPAIR - n) * D2].rearrange("p (c f) -> p c f", f=D)))
    return out


def transpose_pairs(pe, tp, x, ident, rows=D2):
    for c in range(NPAIR):
        last = pe.transpose(turned(tp, c)[0:rows, :], x[:, 2 * c:2 * c + 2, :].rearrange("p a f -> p (a f)"), ident)
    return last


def copy_turned(nc, xT, tp, rows=D2):
    n = min(4, NPAIR) * P
    nc.scalar.copy(xT[0:rows, 0:n], tp[0:rows, 0, 0:n])
    return nc.scalar.copy(xT[0:rows, n:NPAIR * P], tp[0:rows, 1, 0:NPAIR * P - n])


def multiply_pairs(pe, mm, pairs):
    for c in range(NPAIR):
        for k, (xT, w, rows) in enumerate(pairs):
            last = pe.matmul(product(mm, c), xT[0:rows, c * P:(c + 1) * P], w,
                             start=(k == 0), stop=(k == len(pairs) - 1))
    return last


def centre(dve, x, out, st):
    total, mean = st[:, 0, :], st[:, 1, :]
    dve.reduce_sum(total, x, AX)
    dve.drain()
    dve.tensor_scalar(mean, total, 1.0 / D, None, ALU.mult)
    dve.drain()
    return dve.tensor_tensor(out, x, over_features(mean), ALU.subtract)


def variance(dve, sq, st):
    total = st[:, 2, :]
    dve.reduce_sum(total, sq, AX)
    dve.drain()
    return dve.tensor_scalar(st[:, 3, :], total, 1.0 / D, EPS, ALU.mult, ALU.add)


def normalised(dve, x, out, st, relu=True):
    rstd = st[:, 2, :]
    dve.reciprocal(rstd, st[:, 4, :])
    dve.drain()
    if relu:
        return dve.scalar_tensor_tensor(out, x, 0.0, over_features(rstd), ALU.max, ALU.mult)
    return dve.tensor_tensor(out, x, over_features(rstd), ALU.mult)


def layernorm(dve, x, out, sq, st, var_ready, std_ready, count, relu=True):
    centre(dve, x, out, st)
    dve.drain()
    dve.tensor_tensor(sq, out, out, ALU.mult)
    dve.drain()
    variance(dve, sq, st).then_inc(var_ready, 1)
    dve.wait_ge(std_ready, count)
    normalised(dve, out, out, st, relu)
    dve.drain()


def take_std(act, nc, st, var_ready, std_ready, count):
    act.wait_ge(var_ready, count)
    nc.scalar.activation(st[:, 4, :], st[:, 3, :], ACT.Sqrt).then_inc(std_ready, 1)


class Names:
    pass


class Stage:

    def __init__(self, nc, name):
        self.nc, self.name, self.ctx, self.used = nc, name, ExitStack(), []

    def __enter__(self):
        return self

    def __exit__(self, *what):
        self.ctx.close()
        if self.used:
            self.nc.clear_and_free_semaphores(self.used)
            self.nc.all_engine_barrier()

    def sb(self, name, shape, dt=F32):
        return self.ctx.enter_context(self.nc.sbuf_tensor(f"{self.name}_{name}", shape, dt))

    def ps(self, name, shape, dt=F32):
        return self.ctx.enter_context(self.nc.psum_tensor(f"{self.name}_{name}", shape, dt))

    def sem(self, name):
        self.used.append(self.nc.alloc_semaphore(f"{self.name}_{name}"))
        return self.used[-1]

    def sems(self, name, n=2):
        return [self.sem(f"{name}{i}") for i in range(n)]


def skewed(engine, prepare, consume):
    prepare(0, 0)
    with engine.Fori(0, IT - 1) as i:
        prepare(i, 1)
        consume(i, 0)
        prepare(i + 1, 0)
        consume(i, 1)
    prepare(IT - 1, 1)
    consume(IT - 1, 0)
    consume(IT - 1, 1)


def gather_rows(pool, table, idx, idx_now, rows, w, slot_free, landed, idx_staged, begun):
    with pool.Fori(0, IT) as i:
        for h in range(2):
            pool.wait_ge(slot_free[h], i + 1)
            pool.tensor_copy(idx_now[:, h * BS:(h + 1) * BS], idx[:, bass.ds((2 * i + h) * BS, BS)]).then_inc(idx_staged, 1)
            pool.wait_ge(idx_staged, 2 * i + h + 1)
            pool.sem_inc(begun, 1)
            for u in range(BS):
                pool.indirect_dma_start(
                    out=rows[:, h, u, 0:w], out_offset=None, in_=table,
                    in_offset=bass.IndirectOffsetOnAxis(ap=idx_now[:, h * BS + u:h * BS + u + 1], axis=0),
                ).then_inc(landed[h], 16)



def node_stage_in(nc, io, g):
    with Stage(nc, "nin") as s:
        HB = BS // 2
        src, dst = s.sb("src", [P, COLS], I32), s.sb("dst", [P, COLS], I32)
        srcf, dstf = s.sb("srcf", [P, COLS]), s.sb("dstf", [P, COLS])
        HI_D, LO_D, HI_S, LO_S, KEEP, MINUS_LO_S = range(6)
        NK = 6
        split = s.sb("split", [P, NB, NK, BS])
        now = s.sb("now", [P, 2, NK, BS])
        one = s.sb("one", [P, 2, HB, 2 * (P + COLS)], F16)
        away = s.sb("away", [P, 2, COLS], F16)
        BY_ACT = 5
        iota_i, iota_f, iota_h = s.sb("iota_i", [P, COLS], I32), s.sb("iota_f", [P, COLS]), s.sb("iota_h", [P, COLS], F16)
        zero_h = s.sb("zero_h", [P, P + COLS], F16)
        diag, upper, ones = s.sb("diag", [P, P]), s.sb("upper", [P, P]), s.sb("ones", [P, P])
        zi = s.sb("zi", [P, COLS], I32)
        t = [s.sb(f"t{i}", [P, COLS]) for i in range(4)] + [s.sb("vec", [P, COLS])]
        ex = s.sb("ex", [P, COLS, 5])
        zrow = s.sb("zrow", [1, D2])
        srcT = s.sb("srcT", [P, 4, P])
        x, hh = s.sb("x", [P, 2, BS, D]), s.sb("hh", [P, COLS, D])
        xc, sq, st = s.sb("xc", [P, BS, D]), s.sb("sq", [P, BS, D]), s.sb("st", [P, 5, BS])
        ndeg_in, ndeg_out = s.ps("deg_in", [P, 512]), s.ps("deg_out", [P, 512])
        pcol, pT = s.ps("pcol", [P, 512]), s.ps("pT", [P, 4, P])

        loaded, consts, const_step, split_ready = s.sem("loaded"), s.sem("consts"), s.sem("const_step"), s.sem("split_ready")
        now_free, now_ready = s.sems("now_free"), s.sem("now_ready")
        one_free, one_ready, act_one_ready = s.sems("one_free"), s.sem("one_ready"), s.sem("act_one_ready")
        away_ready, iota_ready = s.sem("away_ready"), s.sem("iota_ready")
        counted = s.sem("counted")
        totals_ready, offsets_ready = s.sem("totals_ready"), s.sem("offsets_ready")
        deg_ready, root_ready = s.sem("deg_ready"), s.sem("root_ready")
        diag_ready, row_ready = s.sem("diag_ready"), s.sem("row_ready")
        turned_ready, srct_ready, stored, zero_ready = s.sem("turned_ready"), s.sem("srct_ready"), s.sem("stored"), s.sem("zero_ready")
        x_landed, x_free = s.sems("x_landed"), s.sems("x_free")
        xc_ready, sq_ready, var_ready, std_ready = s.sem("xc_ready"), s.sem("sq_ready"), s.sem("var_ready"), s.sem("std_ready")
        counting = ExitStack()
        block = counting.enter_context(nc.Block())

        @block.sync
        def _(sp):
            sp.dma_start(dst[:, :], io.dst.rearrange("(p c) -> p c", p=P)).then_inc(loaded, 16)
            sp.dma_start(src[:, :], io.src.rearrange("(p c) -> p c", p=P)).then_inc(loaded, 16)
            sp.dma_start(zi[:, :], io.node_type.rearrange("(p c) -> p c", p=P)).then_inc(loaded, 16)
            sp.dma_start(t[4][:, :], io.node_vec.rearrange("(p c) -> p c", p=P)).then_inc(loaded, 16)
            with sp.Fori(0, IT) as i:
                for h in range(2):
                    sp.wait_ge(x_free[h], i + 1)
                    sp.dma_start(x[:, h, :, :], block_of(io.x, i, h, D)).then_inc(x_landed[h], 16)
            sp.wait_ge(zero_ready, 1)
            for table, w in g.sum_tables:
                sp.dma_start(table[ZROW:ZROW + 1, :], zrow[:, 0:w]).then_inc(stored, 16)
            sp.wait_ge(srct_ready, 1)
            for k in range(-(-COLS // P)):
                n = min(P, COLS - k * P)
                sp.dma_start(g.src_cols[k * P:k * P + n, :], srcT[0:n, k, :]).then_inc(stored, 16)
            sp.wait_ge(stored, 16 * (len(g.sum_tables) + -(-COLS // P)))

        @block.gpsimd
        def _(pool):
            pool.memset(g.ident[:, :], 0.0).then_inc(const_step, 1)
            pool.memset(upper[:, :], 1.0).then_inc(const_step, 1)
            pool.memset(g.lower[:, :], 1.0).then_inc(const_step, 1)
            pool.memset(ones[:, :], 1.0)
            pool.iota(iota_i[:, :], pattern=[[1, COLS]], base=0, channel_multiplier=0)
            pool.wait_ge(const_step, 3)
            pool.affine_select(out=g.ident[:, :], in_=g.ident[:, :], compare_op=ALU.not_equal, fill=1.0,
                               base=0, pattern=[[-1, P]], channel_multiplier=1)
            pool.affine_select(out=upper[:, :], in_=upper[:, :], compare_op=ALU.is_gt, fill=0.0,
                               base=0, pattern=[[1, P]], channel_multiplier=-1)
            pool.affine_select(out=g.lower[:, :], in_=g.lower[:, :], compare_op=ALU.is_gt, fill=0.0,
                               base=0, pattern=[[-1, P]], channel_multiplier=1).then_inc(consts, 1)

        @block.vector
        def _(dve):
            for q in now_free + x_free:
                dve.sem_inc(q, 1)
            dve.memset(zrow[:, :], 0.0).then_inc(zero_ready, 1)
            dve.memset(zero_h[:, :], 0.0)
            dve.wait_ge(consts, 1)
            dve.tensor_copy(iota_f[:, :], iota_i[:, :])
            dve.tensor_copy(iota_h[:, :], iota_i[:, :])
            dve.drain()
            dve.tensor_copy(g.iota[:, :], iota_f[:, 0:P]).then_inc(iota_ready, 1)
            dve.wait_ge(loaded, 64)
            dve.tensor_copy(srcf[:, :], src[:, :])
            dve.tensor_copy(dstf[:, :], dst[:, :])
            dve.tensor_copy(g.src_idx[:, :], src[:, :])
            dve.tensor_copy(g.dst_idx[:, :], dst[:, :])
            dve.drain()
            for of, hi, lo in ((dstf, HI_D, LO_D), (srcf, HI_S, LO_S)):
                dve.tensor_scalar(t[0][:, :], of[:, :], 0.5, 1.0 / COLS, ALU.add, ALU.mult)
                dve.drain()
                dve.tensor_scalar(t[1][:, :], t[0][:, :], -0.5, ROUND, ALU.add, ALU.add)
                dve.drain()
                dve.tensor_scalar(t[0][:, :], t[1][:, :], -ROUND, None, ALU.add)
                dve.drain()
                dve.tensor_copy(split[:, :, hi, :], t[0][:, :].rearrange("p (b c) -> p b c", c=BS))
                dve.scalar_tensor_tensor(split[:, :, lo, :], t[0][:, :].rearrange("p (b c) -> p b c", c=BS), -float(COLS),
                                         of[:, :].rearrange("p (b c) -> p b c", c=BS), ALU.mult, ALU.add)
                dve.drain()
            dve.tensor_scalar(split[:, :, MINUS_LO_S, :], split[:, :, LO_S, :], -1.0, None, ALU.mult)
            dve.tensor_tensor(t[0][:, :], srcf[:, :], dstf[:, :], ALU.not_equal)
            dve.drain()
            by_block = t[0][:, :].rearrange("p (b c) -> p b c", c=BS)
            dve.tensor_copy(split[:, :, KEEP, :], by_block).then_inc(split_ready, 1)
            dve.memset(g.sc[:, :, :, :], 0.0)
            dve.drain()
            dve.tensor_copy(g.sc[:, :, EW, :], by_block)
            dve.drain()
            dve.memset(t[0][:, 0:1], 0.0)
            dve.tensor_tensor(t[0][:, 1:COLS], dstf[:, 1:COLS], dstf[:, 0:COLS - 1], ALU.is_equal)
            dve.tensor_scalar(t[1][:, :], dstf[:, :], dstf[:, 0:1], None, ALU.is_equal)
            dve.drain()
            dve.tensor_copy(g.sc[:, :, SAME, :], by_block)
            dve.tensor_copy(g.sc[:, :, FIRST, :], t[1][:, :].rearrange("p (b c) -> p b c", c=BS))
            dve.tensor_scalar(diag[:, :], g.ident[:, :], dstf[:, 0:1], None, ALU.mult).then_inc(diag_ready, 1)
            dve.wait_ge(row_ready, 1)
            dve.scalar_tensor_tensor(g.carries[:, :], pcol[:, 0:P], dstf[:, COLS - 1:COLS], upper[:, :],
                                     ALU.is_equal, ALU.mult)
            dve.wait_ge(turned_ready, 1)
            for k in range(-(-COLS // P)):
                n = min(P, COLS - k * P)
                last = dve.tensor_copy(srcT[0:n, k, :], pT[0:n, k, :])
            last.then_inc(srct_ready, 1)

            def one_hots(i, h, half):
                dve.wait_ge(one_free[half], 2 * i + h + 1)
                for cc in range(HB):
                    c = half * HB + cc
                    o = one[:, half, cc, :]
                    dve.tensor_scalar(o[:, 0:P], iota_h[:, 0:P], now[:, h, HI_D, c:c + 1], None, ALU.is_equal)
                    dve.tensor_scalar(o[:, P:P + COLS], iota_h[:, :], now[:, h, LO_D, c:c + 1], None, ALU.is_equal)
                    if cc >= BY_ACT:
                        dve.tensor_scalar(o[:, 2 * P + COLS:], iota_h[:, :], now[:, h, LO_S, c:c + 1], None, ALU.is_equal)
                    last = dve.tensor_scalar(o[:, P + COLS:2 * P + COLS], iota_h[:, 0:P], now[:, h, HI_S, c:c + 1],
                                             now[:, h, KEEP, c:c + 1], ALU.is_equal, ALU.mult)
                last.then_inc(one_ready, 1)

            with dve.Fori(0, IT) as i:
                for h in range(2):
                    n = 2 * i + h + 1
                    dve.wait_ge(x_landed[h], (i + 1) * 16)
                    centre(dve, x[:, h, :, :], xc[:, :, :], st).then_inc(xc_ready, 1)
                    dve.drain()
                    dve.sem_inc(x_free[h], 1)
                    dve.wait_ge(now_ready, n)
                    one_hots(i, h, 0)
                    dve.wait_ge(sq_ready, n)
                    variance(dve, sq[:, :, :], st).then_inc(var_ready, 1)
                    one_hots(i, h, 1)
                    dve.drain()
                    dve.sem_inc(now_free[h], 1)
                    dve.wait_ge(std_ready, n)
                    normalised(dve, xc[:, :, :], hh[:, bass.ds((2 * i + h) * BS, BS), :], st)
                    dve.drain()

            dve.wait_ge(counted, 1)
            deg_in, has, last_edge, first, tmp = (q[:, :] for q in t)
            dve.tensor_copy(ex[:, :, 4], tmp)
            dve.tensor_copy(ex[:, :, 3], zi[:, :])
            dve.tensor_copy(deg_in, ndeg_in[:, 0:COLS])
            dve.tensor_copy(first, ndeg_out[:, 0:COLS])
            dve.drain()
            dve.tensor_scalar(iota_f[:, :], deg_in, 1.0, None, ALU.max)
            dve.tensor_scalar(tmp, first, 1.0, None, ALU.max).then_inc(deg_ready, 1)
            dve.wait_ge(root_ready, 1)
            dve.reciprocal(dstf[:, :], dstf[:, :])
            dve.reciprocal(srcf[:, :], srcf[:, :])
            dve.tensor_scalar(has, deg_in, 0.0, None, ALU.is_gt)
            dve.tensor_scalar(first, first, 0.0, None, ALU.is_gt)
            dve.drain()
            dve.tensor_tensor(ex[:, :, 0], srcf[:, :], first, ALU.mult)
            dve.tensor_tensor(ex[:, :, 1], dstf[:, :], has, ALU.mult)
            dve.memset(iota_f[:, :], 1.0)
            dve.drain()
            dve.tensor_tensor_scan(last_edge, iota_f[:, :], deg_in, 0.0, ALU.mult, ALU.add)
            dve.drain()
            dve.tensor_copy(diag[:, 0:1], last_edge[:, COLS - 1:COLS]).then_inc(totals_ready, 1)
            dve.wait_ge(offsets_ready, 1)
            dve.tensor_copy(diag[:, 1:2], pcol[:, P:P + 1])
            dve.drain()
            dve.tensor_scalar(last_edge, last_edge, diag[:, 1:2], -1.0, ALU.add, ALU.add)
            dve.drain()
            dve.scalar_tensor_tensor(deg_in, deg_in, -1.0, last_edge, ALU.mult, ALU.add)
            dve.tensor_scalar(tmp, last_edge, 0.5, 1.0 / COLS, ALU.add, ALU.mult)
            dve.drain()
            dve.tensor_scalar(first, tmp, -0.5, ROUND, ALU.add, ALU.add)
            dve.drain()
            dve.tensor_scalar(tmp, first, -ROUND, None, ALU.add)
            dve.drain()
            dve.scalar_tensor_tensor(first, tmp, float(COLS), deg_in, ALU.mult, ALU.is_gt)
            dve.tensor_scalar(tmp, tmp, float(NPAD), None, ALU.add)
            dve.drain()
            dve.tensor_tensor(tmp, tmp, last_edge, ALU.subtract)
            dve.drain()
            dve.tensor_tensor(tmp, tmp, first, ALU.mult)
            dve.drain()
            dve.tensor_tensor(last_edge, last_edge, tmp, ALU.add)
            dve.drain()
            dve.scalar_tensor_tensor(last_edge, last_edge, -float(ZROW), has, ALU.add, ALU.mult)
            dve.drain()
            dve.tensor_scalar(ex[:, :, 2], last_edge, float(ZROW), None, ALU.add)
            dve.drain()
            dve.tensor_copy(g.last_node[:, :], ex[:, :, 2])

        @block.scalar
        def _(act):
            act.wait_ge(split_ready, 1)
            act.wait_ge(iota_ready, 1)
            act.sem_inc(act_one_ready, 2)
            flat = split[:, :, :, :].rearrange("p b k c -> p (b k c)")

            def prepare(i, h):
                act.wait_ge(now_free[h], 2 * i + 1)
                nc.scalar.copy(now[:, h, :, :].rearrange("p k c -> p (k c)"),
                               flat[:, bass.ds((2 * i + h) * (NK * BS), NK * BS)]).then_inc(now_ready, 1)

            def one_hots(i, h, half):
                n = 2 * i + h + 1
                act.wait_ge(now_ready, n)
                act.wait_ge(one_free[half], n)
                for cc in range(BY_ACT):
                    c = half * HB + cc
                    k = (n - 1) * (2 * BY_ACT) + half * BY_ACT + cc
                    act.wait_ge(act_one_ready, k + 1)
                    nc.scalar.activation(away[:, (half * BY_ACT + cc) % 2, :], iota_h[:, :], ACT.Abs, bias=now[:, h, MINUS_LO_S, c:c + 1]
                                         ).then_inc(away_ready, 1)
                    act.wait_ge(away_ready, k + 1)
                    nc.scalar.activation(one[:, half, cc, 2 * P + COLS:], away[:, (half * BY_ACT + cc) % 2, :], ACT.Relu,
                                         bias=1.0, scale=-1.0).then_inc(act_one_ready, 1)

            def consume(i, h):
                n = 2 * i + h + 1
                act.wait_ge(xc_ready, n)
                nc.scalar.activation(sq[:, :, :], xc[:, :, :], ACT.Square).then_inc(sq_ready, 1)
                one_hots(i, h, 0)
                take_std(act, nc, st, var_ready, std_ready, n)
                one_hots(i, h, 1)
                act.wait_ge(act_one_ready, 2 * n * BY_ACT + 2)
                act.sem_inc(now_free[h], 1)

            skewed(act, prepare, consume)
            act.wait_ge(deg_ready, 1)
            nc.scalar.activation(dstf[:, :], iota_f[:, :], ACT.Sqrt)
            nc.scalar.activation(srcf[:, :], t[4][:, :], ACT.Sqrt).then_inc(root_ready, 1)

        @block.tensor
        def _(pe):
            pe.sem_inc(one_free[0], 1)
            pe.sem_inc(one_free[1], 1)
            pe.wait_ge(diag_ready, 1)
            pe.matmul(pcol[:, 0:P], ones[:, :], diag[:, :], start=True, stop=True).then_inc(row_ready, 1)
            for k in range(-(-COLS // P)):
                n = min(P, COLS - k * P)
                last = pe.transpose(pT[0:n, k, :], srcf[:, k * P:k * P + n], g.ident[:, :])
            last.then_inc(turned_ready, 1)
            for acc in (ndeg_in, ndeg_out):
                pe.matmul(acc[:, 0:COLS], zero_h[:, 0:P], zero_h[:, P:], start=True, stop=False, skip_group_check=True)
            with pe.Fori(0, IT) as i:
                for h in range(2):
                    for half in range(2):
                        n = (2 * i + h) * 2 + half + 1
                        pe.wait_ge(one_ready, n)
                        pe.wait_ge(act_one_ready, n * BY_ACT + 2)
                        for c in range(HB):
                            o = one[:, half, c, :]
                            pe.matmul(ndeg_in[:, 0:COLS], o[:, 0:P], o[:, P:P + COLS], start=False, stop=False,
                                      skip_group_check=True)
                            last = pe.matmul(ndeg_out[:, 0:COLS], o[:, P + COLS:2 * P + COLS], o[:, 2 * P + COLS:],
                                             start=False, stop=False, skip_group_check=True)
                        last.then_inc(one_free[half], 1)
            for acc in (ndeg_in, ndeg_out):
                last = pe.matmul(acc[:, 0:COLS], zero_h[:, 0:P], zero_h[:, P:], start=False, stop=True, skip_group_check=True)
            last.then_inc(counted, 1)
            pe.wait_ge(totals_ready, 1)
            pe.matmul(pcol[:, P:P + 1], upper[:, :], diag[:, 0:1], start=True, stop=True).then_inc(offsets_ready, 1)

        counting.close()
        row = s.sb("row", [P, 2, BS, W1ROW])
        with Stage(nc, "row") as r:
            row_ready, row_free, row_stored = r.sems("row_ready"), r.sems("row_free"), r.sems("row_stored")
            x_landed, x_free = r.sems("x_landed"), r.sems("x_free")
            h_copied = r.sems("h_copied")
            block = r.ctx.enter_context(nc.Block())

            @block.sync
            def _(sp):
                def prepare(i, h):
                    sp.wait_ge(x_free[h], i + 1)
                    sp.dma_start(x[:, h, :, :], block_of(io.x, i, h, D)).then_inc(x_landed[h], 16)

                def consume(i, h):
                    sp.wait_ge(row_ready[h], i + 1)
                    sp.wait_ge(h_copied[h], i + 1)
                    sp.dma_start(block_of(g.tab_in, i, h, W1ROW), row[:, h, :, :]).then_inc(row_stored[h], 16)

                skewed(sp, prepare, consume)
                for h in range(2):
                    sp.wait_ge(row_stored[h], 16 * IT)

            @block.vector
            def _(dve):
                dve.memset(row[:, :, :, EX + 5:W1ROW], 0.0)
                for q in x_free + row_free:
                    dve.sem_inc(q, 1)
                with dve.Fori(0, IT) as i:
                    for h in range(2):
                        dve.wait_ge(x_landed[h], (i + 1) * 16)
                        dve.wait_ge(row_free[h], i + 1)
                        dve.tensor_tensor(row[:, h, :, 0:D], x[:, h, :, :], over_columns(g.bias0[:, :]), ALU.add)
                        dve.tensor_copy(row[:, h, :, EX:EX + 5], ex[:, bass.ds((2 * i + h) * BS, BS), :]).then_inc(row_ready[h], 1)
                        dve.drain()
                        dve.sem_inc(x_free[h], 1)

            @block.scalar
            def _(act):
                with act.Fori(0, IT) as i:
                    for h in range(2):
                        act.wait_ge(row_free[h], i + 1)
                        nc.scalar.copy(row[:, h, :, D:2 * D], hh[:, bass.ds((2 * i + h) * BS, BS), :]).then_inc(h_copied[h], 1)

            @block.gpsimd
            def _(pool):
                with pool.Fori(0, IT) as i:
                    for h in range(2):
                        pool.wait_ge(row_stored[h], (i + 1) * 16)
                        pool.sem_inc(row_free[h], 1)



def weight_stage(nc, io, g):
    with Stage(nc, "wts") as s:
        raw = [s.sb(f"raw{k}", [D2, D2]) for k in range(4)]
        lap, mf, coef = s.sb("lap", [P, K1 + 1]), s.sb("mf", [P, K1 + 1]), s.sb("coef", [P, K1 + 3])
        embT, adT, cmat = s.sb("embT", [EMB, NZ]), s.sb("adT", [EMB, EMB]), s.sb("cmat", [EMB, NZ])
        pm = s.ps("pm", [P, 512])
        zeroed, loaded, tanhed = s.sem("zeroed"), s.sem("loaded"), s.sem("tanhed")
        c_ready, c_copied, m_ready = s.sem("c_ready"), s.sem("c_copied"), s.sem("m_ready")
        bd = [(raw[k], io.w0[k], D) for k in range(4)] + [
            (g.w_rel1, io.w_rel1, D), (g.w_root1, io.w_root1, D), (g.w_rel2, io.w_rel2, D), (g.w_root2, io.w_root2, D),
            (g.W1, io.W1.rearrange("h r -> r h"), R), (g.W2, io.W2.rearrange("h k -> k h"), D)]
        n_dma = 2 * len(bd) + 13
        block = s.ctx.enter_context(nc.Block())

        @block.sync
        def _(sp):
            sp.wait_ge(zeroed, 1)
            with nc.allow_non_contiguous_dma(reason="small transposed weights, once"):
                for to, of, k in bd:
                    for half in range(2):
                        sp.dma_start(to[half * k:(half + 1) * k, half * D:(half + 1) * D], of).then_inc(loaded, 16)
                for to, of in ((g.bias0, io.bias0), (g.gamma, io.gamma), (g.beta, io.beta),
                               (g.b_l1, io.b_l1), (g.b_l2, io.b_l2)):
                    sp.dma_start(to[:, :], of.partition_broadcast(P)).then_inc(loaded, 16)
                sp.dma_start(lap[:, :], io.lap.partition_broadcast(P)).then_inc(loaded, 16)
                sp.dma_start(mf[:, :], io.mf.rearrange("a k b -> (a k b)").partition_broadcast(P)).then_inc(loaded, 16)
                sp.dma_start(embT[:, :], io.emb.rearrange("z g -> g z")).then_inc(loaded, 16)
                sp.dma_start(adT[:, :], io.adaptW.rearrange("g k -> k g")).then_inc(loaded, 16)
                for half in range(2):
                    sp.dma_start(g.W2[D2:D2 + 1, half * D:(half + 1) * D], io.b2.unsqueeze(0)).then_inc(loaded, 16)
                    sp.dma_start(g.b1[half * D:(half + 1) * D, :], io.b1.unsqueeze(1)).then_inc(loaded, 16)
            sp.wait_ge(loaded, 16 * n_dma)

        @block.vector
        def _(dve):
            for k, (to, _, _) in enumerate(bd):
                last = dve.memset(to[:, :], 0.0)
            last.then_inc(zeroed, 1)
            dve.wait_ge(loaded, 16 * n_dma)
            dve.tensor_tensor(g.wh[:, :], raw[0][:, :], raw[2][:, :], ALU.subtract)
            dve.tensor_tensor(g.wu[0][:, :], raw[1][:, :], raw[3][:, :], ALU.subtract)
            dve.tensor_scalar(g.wu[1][:, :], raw[2][:, :], 2.0, None, ALU.mult)
            dve.tensor_scalar(g.wu[2][:, :], raw[3][:, :], 2.0, None, ALU.mult)
            dve.wait_ge(tanhed, 1)
            for k in range(1, K1):
                dve.tensor_tensor(lap[:, k:k + 1], lap[:, k:k + 1], lap[:, k - 1:k], ALU.mult)
                dve.drain()
            dve.memset(coef[:, :], 0.0)
            dve.drain()
            dve.tensor_copy(coef[:, 0:1], mf[:, 0:1])
            dve.tensor_tensor(coef[:, 1:K1 + 1], mf[:, 1:K1 + 1], lap[:, 0:K1], ALU.mult)
            dve.drain()
            for k, norm in enumerate(jacobi_norms()):
                dve.tensor_scalar(coef[:, k:k + 1], coef[:, k:k + 1], 1.0 / norm, None, ALU.mult)
            dve.drain()
            for k in range(K1 - 2, -1, -1):
                dve.scalar_tensor_tensor(coef[:, k:k + 1], coef[:, k + 2:k + 3], jacobi(k + 2)[1], coef[:, k:k + 1],
                                         ALU.mult, ALU.add)
                dve.drain()
            dve.tensor_copy(g.p0w[:, :], coef[:, 0:1])
            for k in range(K1):
                dve.memset(g.betas[:, k:k + 1], BETA[k])
            for k in range(K1):
                dve.tensor_scalar(g.omega[:, k:k + 1], coef[:, k + 1:k + 2], SCALE[k + 1], None, ALU.mult)
            dve.wait_ge(c_ready, 1)
            dve.tensor_copy(cmat[:, :], pm[0:EMB, 0:NZ]).then_inc(c_copied, 1)
            dve.wait_ge(m_ready, 1)
            dve.tensor_copy(g.pair_term[:, :], pm[0:NZ, P:P + NZ])

        @block.scalar
        def _(act):
            act.wait_ge(loaded, 16 * n_dma)
            nc.scalar.activation(lap[:, :], lap[:, :], ACT.Tanh).then_inc(tanhed, 1)

        @block.tensor
        def _(pe):
            pe.wait_ge(loaded, 16 * n_dma)
            pe.matmul(pm[0:EMB, 0:NZ], adT[:, :], embT[:, :], start=True, stop=True).then_inc(c_ready, 1)
            pe.wait_ge(c_copied, 1)
            pe.matmul(pm[0:NZ, P:P + NZ], embT[:, :], cmat[:, :], start=True, stop=True).then_inc(m_ready, 1)



def layernorm_apart(dve, x, xc, out, st, sq, xc_ready, sq_ready, var_ready, std_ready, count, relu=True):
    centre(dve, x, xc, st).then_inc(xc_ready, 1)
    dve.wait_ge(sq_ready, count)
    variance(dve, sq, st).then_inc(var_ready, 1)
    dve.wait_ge(std_ready, count)
    return normalised(dve, xc, out, st, relu)


def take_squares(act, nc, xc, sq, xc_ready, sq_ready, count):
    act.wait_ge(xc_ready, count)
    nc.scalar.activation(sq, xc, ACT.Square).then_inc(sq_ready, 1)


def next_block(i, h):
    return (i, 1) if h == 0 else (i + 1, 0)


def with_next(engine, body):
    with engine.Fori(0, IT - 1) as i:
        body(i, 0, False)
        body(i, 1, False)
    body(IT - 1, 0, False)
    body(IT - 1, 1, True)


def node_stage_mid(nc, io, g):
    with Stage(nc, "mid") as s:
        rows, idx_now = s.sb("rows", [P, 2, BS, D2]), s.sb("idx_now", [P, 2 * BS], I32)
        own = s.sb("own", [P, 2, BS, W1ROW])
        left, leftT = s.sb("left", [P, BS, D]), s.sb("leftT", [P, NPAIR * P])
        x1, xc, h1, sq, st = s.sb("x1", [P, BS, D]), s.sb("xc", [P, BS, D]), s.sb("h1", [P, BS, D]), s.sb("sq", [P, BS, D]), s.sb("st", [P, 5, BS])
        a0 = s.sb("a0", [P, BS, D])
        x2, h2 = s.sb("x2", [P, 2, BS, D]), s.sb("h2", [P, 2, BS, H2ROW])
        tp, mm = s.ps("tp", [P, 2, 512]), s.ps("mm", [P, 2, 512])
        slot_free, landed, idx_staged, begun = s.sems("slot_free"), s.sems("landed"), s.sem("idx_staged"), s.sem("begun")
        own_landed, own_free = s.sems("own_landed"), s.sems("own_free")
        out_ready, out_free, out_stored = s.sems("out_ready"), s.sems("out_free"), s.sems("out_stored")
        xc_ready, sq_ready, var_ready, std_ready = s.sem("xc_ready"), s.sem("sq_ready"), s.sem("var_ready"), s.sem("std_ready")
        left_ready, left_turned, left_copied, mm_ready, mm_read = (
            s.sem(n) for n in ("left_ready", "left_turned", "left_copied", "mm_ready", "mm_read"))
        block = s.ctx.enter_context(nc.Block())

        @block.gpsimd
        def _(pool):
            gather_rows(pool, g.tab_both, g.last_node, idx_now, rows, D2, slot_free, landed, idx_staged, begun)

        @block.scalar
        def _(act):
            def own_h(i, h):
                act.wait_ge(own_landed[h], (i + 1) * 16)
                nc.scalar.copy(left[:, :, :], own[:, h, :, D:2 * D]).then_inc(left_ready, 1)

            def own_h_turned(i, h):
                act.wait_ge(left_turned, 2 * i + h + 1)
                copy_turned(nc, leftT, tp).then_inc(left_copied, 1)

            def body(i, h, last):
                n = (2 * i + h) * 2
                take_squares(act, nc, xc[:, :, :], sq[:, :, :], xc_ready, sq_ready, n + 1)
                take_std(act, nc, st, var_ready, std_ready, n + 1)
                if not last:
                    own_h(*next_block(i, h))
                    own_h_turned(*next_block(i, h))
                take_squares(act, nc, xc[:, :, :], sq[:, :, :], xc_ready, sq_ready, n + 2)
                take_std(act, nc, st, var_ready, std_ready, n + 2)

            own_h(0, 0)
            own_h_turned(0, 0)
            with_next(act, body)

        @block.tensor
        def _(pe):
            with pe.Fori(0, IT) as i:
                for h in range(2):
                    n = 2 * i + h + 1
                    pe.wait_ge(left_ready, n)
                    transpose_pairs(pe, tp, left, g.ident[:, :]).then_inc(left_turned, 1)
                    pe.wait_ge(left_copied, n)
                    pe.wait_ge(mm_read, n)
                    for c in range(NPAIR):
                        pe.matmul(product(mm, c), leftT[0:D2, c * P:(c + 1) * P], g.wh[:, :], start=True, stop=False)
                        last = pe.matmul(product(mm, c), g.ident[:, :], own[:, h, 2 * c:2 * c + 2, 0:D], start=False, stop=True)
                    last.then_inc(mm_ready, 1)

        @block.sync
        def _(sp):
            def prepare(i, h):
                sp.wait_ge(own_free[h], i + 1)
                sp.dma_start(own[:, h, :, :], block_of(g.tab_in, i, h, W1ROW)).then_inc(own_landed[h], 16)

            def consume(i, h):
                sp.wait_ge(out_ready[h], i + 1)
                sp.dma_start(block_of(g.x2, i, h, D), x2[:, h, :, :]).then_inc(out_stored[h], 16)
                sp.dma_start(block_of(g.tab_h2, i, h, H2ROW), h2[:, h, :, :]).then_inc(out_stored[h], 16)
                sp.wait_ge(out_stored[h], (i + 1) * 32)
                sp.sem_inc(out_free[h], 1)

            sp.sem_inc(out_free[0], 1)
            sp.sem_inc(out_free[1], 1)
            skewed(sp, prepare, consume)

        @block.vector
        def _(dve):
            dve.memset(h2[:, :, :, D + 2:H2ROW], 0.0)
            for q in slot_free + own_free + [mm_read]:
                dve.sem_inc(q, 1)
            with dve.Fori(0, IT) as i:
                for h in range(2):
                    n = 2 * i + h + 1
                    dve.wait_ge(landed[h], (i + 1) * (16 * BS))
                    dve.wait_ge(own_landed[h], (i + 1) * 16)
                    scal = own[:, h, :, EX:EX + 5]
                    dve.scalar_tensor_tensor(a0[:, :, :], rows[:, h, :, 0:D], -1.0, over_features(scal[:, :, 0]), ALU.mult, ALU.mult)
                    dve.wait_ge(out_free[h], i + 1)
                    dve.tensor_tensor(x2[:, h, :, :], rows[:, h, :, D:D2], over_features(scal[:, :, 1]), ALU.mult)
                    dve.drain()
                    dve.sem_inc(slot_free[h], 1)
                    dve.wait_ge(mm_ready, n)
                    for c, piece in products(mm):
                        dve.tensor_tensor(x1[:, c, :], a0[:, c, :], piece, ALU.add)
                    dve.drain()
                    dve.sem_inc(mm_read, 1)
                    layernorm_apart(dve, x1[:, :, :], xc[:, :, :], h1[:, :, :], st, sq[:, :, :], xc_ready, sq_ready,
                                    var_ready, std_ready, 2 * n - 1)
                    dve.tensor_tensor(x1[:, :, :], x1[:, :, :], x2[:, h, :, :], ALU.add)
                    dve.drain()
                    dve.scalar_tensor_tensor(x2[:, h, :, :], h1[:, :, :], g.p0w[:, 0:1], x1[:, :, :], ALU.mult, ALU.add)
                    dve.drain()
                    layernorm_apart(dve, x2[:, h, :, :], xc[:, :, :], h2[:, h, :, 0:D], st, sq[:, :, :], xc_ready, sq_ready,
                                    var_ready, std_ready, 2 * n)
                    dve.tensor_copy(h2[:, h, :, D:D + 2], scal[:, :, 3:5])
                    dve.drain()
                    dve.sem_inc(out_ready[h], 1)
                    dve.sem_inc(own_free[h], 1)


def node_stage_late(nc, io, g):
    with Stage(nc, "late") as s:
        x2, h2, agg = s.sb("x2", [P, 2, BS, D]), s.sb("h2", [P, 2, BS, H2ROW]), s.sb("agg", [P, 2, NAGG, BS, H2ROW])
        total, x2b = s.sb("total", [P, 2, BS, H2ROW]), s.sb("x2b", [P, 2, BS, D])
        y, xc, sq, st = s.sb("y", [P, BS, D]), s.sb("xc", [P, BS, D]), s.sb("sq", [P, BS, D]), s.sb("st", [P, 5, BS])
        x3 = s.sb("x3", [P, 2, BS, D])
        agg_landed, agg_free, h2_landed, h2_free = s.sems("agg_landed"), s.sems("agg_free"), s.sems("h2_landed"), s.sems("h2_free")
        total_ready, total_free, half_ready = s.sem("total_ready"), s.sems("total_free"), s.sem("half_ready")
        out_ready, out_free, out_stored = s.sems("out_ready"), s.sems("out_free"), s.sems("out_stored")
        xc_ready, sq_ready, var_ready, std_ready = s.sem("xc_ready"), s.sem("sq_ready"), s.sem("var_ready"), s.sem("std_ready")
        block = s.ctx.enter_context(nc.Block())

        @block.sync
        def _(sp):
            with sp.Fori(0, IT) as i:
                for h in range(2):
                    sp.wait_ge(agg_free[h], i + 1)
                    for q in range(NAGG):
                        sp.dma_start(agg[:, h, q, :, :], block_of(g.agg[q], i, h, H2ROW)).then_inc(agg_landed[h], 16)
                    sp.dma_start(x2[:, h, :, :], block_of(g.x2, i, h, D)).then_inc(agg_landed[h], 16)
                    sp.wait_ge(h2_free[h], i + 1)
                    sp.dma_start(h2[:, h, :, :], block_of(g.tab_h2, i, h, H2ROW)).then_inc(h2_landed[h], 16)

        @block.tensor
        def _(pe):
            pe.sem_inc(out_free[0], 1)
            pe.sem_inc(out_free[1], 1)
            with pe.Fori(0, IT) as i:
                for h in range(2):
                    pe.wait_ge(out_stored[h], (i + 1) * 16)
                    pe.sem_inc(out_free[h], 1)

        @block.gpsimd
        def _(pool):
            pool.sem_inc(agg_free[0], 1)
            pool.sem_inc(agg_free[1], 1)
            with pool.Fori(0, IT) as i:
                for h in range(2):
                    pool.wait_ge(agg_landed[h], (i + 1) * (16 * (NAGG + 1)))
                    pool.tensor_tensor(agg[:, h, 0, :, :], agg[:, h, 0, :, :], agg[:, h, 1, :, :], ALU.add)
                    pool.tensor_tensor(agg[:, h, 2, :, :], agg[:, h, 2, :, :], agg[:, h, 3, :, :], ALU.add).then_inc(half_ready, 1)
                    pool.wait_ge(total_free[h], i + 1)
                    pool.wait_ge(half_ready, 2 * i + h + 1)
                    pool.tensor_tensor(x2b[:, h, :, :], x2[:, h, :, :], over_columns(g.beta[:, :]), ALU.add)
                    pool.tensor_tensor(total[:, h, :, :], agg[:, h, 0, :, :], agg[:, h, 2, :, :], ALU.add).then_inc(total_ready, 1)
                    pool.wait_ge(total_ready, 2 * i + h + 1)
                    pool.sem_inc(agg_free[h], 1)

        @block.scalar
        def _(act):
            with act.Fori(0, IT) as i:
                for h in range(2):
                    take_squares(act, nc, xc[:, :, :], sq[:, :, :], xc_ready, sq_ready, 2 * i + h + 1)
                    take_std(act, nc, st, var_ready, std_ready, 2 * i + h + 1)
                    act.wait_ge(out_ready[h], i + 1)
                    act.dma_start(block_of(g.x3, i, h, D), x3[:, h, :, :]).then_inc(out_stored[h], 16)

        @block.vector
        def _(dve):
            for q in h2_free + total_free:
                dve.sem_inc(q, 1)
            with dve.Fori(0, IT) as i:
                for h in range(2):
                    n = 2 * i + h + 1
                    a = total[:, h, :, :]
                    dve.wait_ge(total_ready, n)
                    dve.wait_ge(h2_landed[h], (i + 1) * 16)
                    dve.tensor_scalar(st[:, 0, :], a[:, :, D], 1e-8, None, ALU.max)
                    dve.drain()
                    dve.reciprocal(st[:, 1, :], st[:, 0, :])
                    dve.drain()
                    dve.tensor_tensor(y[:, :, :], a[:, :, 0:D], over_features(st[:, 1, :]), ALU.mult)
                    dve.drain()
                    dve.tensor_tensor(y[:, :, :], y[:, :, :], h2[:, h, :, 0:D], ALU.add)
                    dve.drain()
                    dve.sem_inc(h2_free[h], 1)
                    layernorm_apart(dve, y[:, :, :], xc[:, :, :], xc[:, :, :], st, sq[:, :, :], xc_ready, sq_ready,
                                    var_ready, std_ready, n, relu=False)
                    dve.drain()
                    dve.tensor_tensor(xc[:, :, :], xc[:, :, :], over_columns(g.gamma[:, :]), ALU.mult)
                    dve.drain()
                    dve.wait_ge(out_free[h], i + 1)
                    dve.tensor_tensor(x3[:, h, :, :], xc[:, :, :], x2b[:, h, :, :], ALU.add).then_inc(out_ready[h], 1)
                    dve.drain()
                    dve.sem_inc(total_free[h], 1)


def node_stage_out(nc, io, g):
    with Stage(nc, "out") as s:
        rows, idx_now = s.sb("rows", [P, 2, BS, D2]), s.sb("idx_now", [P, 2 * BS], I32)
        x3, xc, sq, st = s.sb("x3", [P, 2, BS, D]), s.sb("xc", [P, BS, D]), s.sb("sq", [P, BS, D]), s.sb("st", [P, 5, BS])
        h3, h3T = s.sb("h3", [P, BS, D]), s.sb("h3T", [P, NPAIR * P])
        a3, h4 = s.sb("a3", [P, BS, D]), s.sb("h4", [P, BS, D])
        aT, hT = s.sb("aT", [P, NPAIR * P]), s.sb("hT", [P, NPAIR * P])
        res = s.sb("res", [P, 2, BS, D])
        ta, tb, mq, mm = s.ps("ta", [P, 2, 512]), s.ps("tb", [P, 2, 512]), s.ps("mq", [P, 2, 512]), s.ps("mm", [P, 2, 512])
        slot_free, landed, idx_staged, begun = s.sems("slot_free"), s.sems("landed"), s.sem("idx_staged"), s.sem("begun")
        x3_landed, x3_free = s.sems("x3_landed"), s.sems("x3_free")
        xc_ready, sq_ready, var_ready, std_ready = s.sem("xc_ready"), s.sem("sq_ready"), s.sem("var_ready"), s.sem("std_ready")
        h3_ready, h3_turned, h3_copied, mq_ready, mq_read = (
            s.sem(n) for n in ("h3_ready", "h3_turned", "h3_copied", "mq_ready", "mq_read"))
        a3_ready, a3_turned, h4_ready, h4_turned, both_copied, mm_ready = (
            s.sem(n) for n in ("a3_ready", "a3_turned", "h4_ready", "h4_turned", "both_copied", "mm_ready"))
        out_ready, out_free, out_stored = s.sems("out_ready"), s.sems("out_free"), s.sems("out_stored")
        block = s.ctx.enter_context(nc.Block())

        @block.gpsimd
        def _(pool):
            gather_rows(pool, g.tab_both2, g.last_node, idx_now, rows, D2, slot_free, landed, idx_staged, begun)

        @block.sync
        def _(sp):
            def prepare(i, h):
                sp.wait_ge(x3_free[h], i + 1)
                sp.dma_start(x3[:, h, :, :], block_of(g.x3, i, h, D)).then_inc(x3_landed[h], 16)

            def consume(i, h):
                sp.wait_ge(out_ready[h], i + 1)
                sp.dma_start(block_of(io.out, i, h, D), res[:, h, :, :]).then_inc(out_stored[h], 16)
                sp.wait_ge(out_stored[h], (i + 1) * 16)
                sp.sem_inc(out_free[h], 1)

            sp.sem_inc(out_free[0], 1)
            sp.sem_inc(out_free[1], 1)
            skewed(sp, prepare, consume)

        @block.scalar
        def _(act):
            def own_turned(i, h):
                act.wait_ge(h3_turned, 2 * i + h + 1)
                copy_turned(nc, h3T, ta).then_inc(h3_copied, 1)

            def body(i, h, last):
                n = 2 * i + h + 1
                act.wait_ge(landed[h], (i + 1) * (16 * BS))
                nc.scalar.copy(a3[:, :, :], rows[:, h, :, D:D2]).then_inc(a3_ready, 1)
                act.wait_ge(a3_turned, n)
                copy_turned(nc, aT, ta)
                if not last:
                    take_squares(act, nc, xc[:, :, :], sq[:, :, :], xc_ready, sq_ready, n + 1)
                act.wait_ge(h4_turned, n)
                copy_turned(nc, hT, tb).then_inc(both_copied, 1)
                if not last:
                    take_std(act, nc, st, var_ready, std_ready, n + 1)
                    own_turned(*next_block(i, h))

            take_squares(act, nc, xc[:, :, :], sq[:, :, :], xc_ready, sq_ready, 1)
            take_std(act, nc, st, var_ready, std_ready, 1)
            own_turned(0, 0)
            with_next(act, body)

        @block.tensor
        def _(pe):
            def own(i, h):
                n = 2 * i + h + 1
                pe.wait_ge(h3_ready, n)
                transpose_pairs(pe, ta, h3, g.ident[:, :]).then_inc(h3_turned, 1)
                pe.wait_ge(h3_copied, n)
                pe.wait_ge(mq_read, n)
                multiply_pairs(pe, mq, [(h3T, g.w_root1[:, :], D2)]).then_inc(mq_ready, 1)

            def body(i, h, last):
                n = 2 * i + h + 1
                pe.wait_ge(a3_ready, n)
                transpose_pairs(pe, ta, a3, g.ident[:, :]).then_inc(a3_turned, 1)
                pe.wait_ge(h4_ready, n)
                transpose_pairs(pe, tb, h4, g.ident[:, :]).then_inc(h4_turned, 1)
                pe.wait_ge(both_copied, n)
                multiply_pairs(pe, mm, [(aT, g.w_rel2[:, :], D2), (hT, g.w_root2[:, :], D2)]).then_inc(mm_ready, 1)
                if not last:
                    own(*next_block(i, h))

            own(0, 0)
            with_next(pe, body)

        @block.vector
        def _(dve):
            def own(i, h):
                n = 2 * i + h + 1
                dve.wait_ge(x3_landed[h], (i + 1) * 16)
                layernorm_apart(dve, x3[:, h, :, :], xc[:, :, :], h3[:, :, :], st, sq[:, :, :], xc_ready, sq_ready,
                                var_ready, std_ready, n).then_inc(h3_ready, 1)

            def body(i, h, last):
                n = 2 * i + h + 1
                dve.wait_ge(landed[h], (i + 1) * (16 * BS))
                dve.wait_ge(out_free[h], i + 1)
                dve.tensor_tensor(h4[:, :, :], rows[:, h, :, 0:D], over_columns(g.b_l1[:, :]), ALU.add)
                dve.tensor_tensor(res[:, h, :, :], x3[:, h, :, :], over_columns(g.b_l2[:, :]), ALU.add)
                dve.drain()
                dve.sem_inc(x3_free[h], 1)
                dve.wait_ge(mq_ready, n)
                for c, piece in products(mq):
                    dve.tensor_tensor(h4[:, c, :], h4[:, c, :], piece, ALU.add)
                dve.drain()
                dve.sem_inc(mq_read, 1)
                dve.tensor_scalar(h4[:, :, :], h4[:, :, :], 0.0, None, ALU.max).then_inc(h4_ready, 1)
                dve.wait_ge(a3_ready, n)
                dve.sem_inc(slot_free[h], 1)
                if not last:
                    own(*next_block(i, h))
                dve.wait_ge(mm_ready, n)
                for c, piece in products(mm):
                    last_add = dve.tensor_tensor(res[:, h, c, :], res[:, h, c, :], piece, ALU.add)
                last_add.then_inc(out_ready[h], 1)
                dve.drain()

            for q in slot_free + x3_free + [mq_read]:
                dve.sem_inc(q, 1)
            own(0, 0)
            with_next(dve, body)



def propagate(nc, g, name, kind, table, w, idx, to, u_old=None, u_new=None, k=None, acc_in=None, acc_out=None,
              r_out=None, merge=None, zero=None):
    wide = D2 if merge is not None else D
    cheb = kind in ("cheb_first", "cheb", "cheb_last")
    conv = kind == "conv_first"
    product_of = cheb or conv
    normed = kind in ("jacobi_first", "conv_first")
    by_feature = kind in ("jacobi", "jacobi_last")
    with Stage(nc, name) as s:
        rows, idx_now = s.sb("rows", [P, 2, BS, w]), s.sb("idx_now", [P, 2 * BS], I32)
        sc = s.sb("sc", [P, 2, NSC * BS])
        same = s.sb("same", [P, 2, D, BS + 1], F16)
        val, run = s.sb("val", [P, D, BS + 1]), s.sb("run", [P, D, BS + 1])
        tmp = s.sb("tmp", [P, D, BS])
        sums = s.sb("sums", [P, 2, BS, wide])
        fix, part, fixed = s.sb("fix", [P, D]), s.sb("part", [P, D]), s.sb("fixed", [P, wide])
        pfix = s.ps("pfix", [P, 512])
        has_acc = acc_in is not None or acc_out is not None
        acc = s.sb("acc", [P, 2, BS, D]) if has_acc else None
        res = s.sb("res", [P, 2, BS, D]) if r_out is not None else None
        slot_free, landed, idx_staged, begun = s.sems("slot_free"), s.sems("landed"), s.sem("idx_staged"), s.sem("begun")
        sc_free, sc_ready = s.sems("sc_free"), s.sem("sc_ready")
        in_landed = s.sems("in_landed")
        val_ready, val_read, run_ready, run_read = s.sem("val_ready"), s.sem("val_read"), s.sem("run_ready"), s.sem("run_read")
        sums_ready, side_ready, out_free, out_stored = s.sems("sums_ready"), s.sems("side_ready"), s.sems("out_free"), s.sems("out_stored")
        fix_ready, fix_done, fix_copied, fix_stored, old_fix = (
            s.sem("fix_ready"), s.sem("fix_done"), s.sem("fix_copied"), s.sem("fix_stored"), s.sem("old_fix"))
        if normed:
            sq, st = s.sb("sq", [P, BS, D]), s.sb("st", [P, 5, BS])
            var_ready, std_ready = s.sem("var_ready"), s.sem("std_ready")
        if kind == "jacobi_first":
            x1 = s.sb("x1", [P, BS, D])
        if kind in ("jacobi", "jacobi_last"):
            beta, omega = s.sb("beta", [P, 1]), s.sb("omega", [P, 1])
        if product_of:
            left, leftT = s.sb("left", [P, 1 + conv, BS, D]), s.sb("leftT", [P, NPAIR * P])
            tp, mm, mm2 = s.ps("tp", [P, 2, 512]), s.ps("mm", [P, 2, 512]), s.ps("mm2", [P, 2, 512])
            left_ready, left_turned, left_copied, mm_ready, mm_read = (
                s.sem(n) for n in ("left_ready", "left_turned", "left_copied", "mm_ready", "mm_read"))
            wu = {"cheb_first": g.wu[0], "cheb": g.wu[1], "cheb_last": g.wu[2], "conv_first": g.w_rel1}[kind]
            wh = {"cheb_first": g.wh, "conv_first": g.w_root1}.get(kind)
        if kind == "cheb_first":
            t1 = s.sb("t1", [P, 2, BS])
        n_in = (acc_in is not None) + (merge is not None)
        n_out = 1 + (acc_out is not None) + (r_out is not None)
        has_side = n_out > 1

        def staged(h, which):
            return sc[:, h, which * BS:(which + 1) * BS]

        def rows_of(x):
            return x.rearrange("p f c -> p c f")

        def u_block(u, i, h):
            return u[:, bass.ds((2 * i + h) * (D * BS), D * BS)].rearrange("p (f c) -> p f c", c=BS)

        v = val[:, :, 1:BS + 1]
        block = s.ctx.enter_context(nc.Block())

        @block.gpsimd
        def _(pool):
            gather_rows(pool, table, idx, idx_now, rows, w, slot_free, landed, idx_staged, begun)

        @block.scalar
        def _(act):
            flat = g.sc[:, :, :, :].rearrange("p b k c -> p (b k c)")

            def prepare(i, h):
                at = (2 * i + h) * (NSC * BS)
                act.wait_ge(sc_free[h], i + 1)
                nc.scalar.copy(sc[:, h, :], flat[:, bass.ds(at, NSC * BS)])
                nc.scalar.copy(same[:, h, :, 1:BS + 1], flat[:, bass.ds(at + SAME * BS, BS)].unsqueeze(1).broadcast_to([P, D, BS])
                               ).then_inc(sc_ready, 1)

            def consume(i, h, last_block=False):
                n = 2 * i + h + 1
                if kind in ("cheb", "cheb_last"):
                    act.wait_ge(val_ready, n)
                    nc.scalar.copy(left[:, 0, :, :], rows_of(v)).then_inc(left_ready, 1)
                if kind == "jacobi_first":
                    take_std(act, nc, st, var_ready, std_ready, n)
                if product_of:
                    act.wait_ge(left_turned, n)
                    copy_turned(nc, leftT, tp).then_inc(left_copied, 1)
                if u_new is not None:
                    act.wait_ge(val_ready, n)
                    nc.scalar.copy(u_block(u_new, i, h), v).then_inc(val_read, 1)
                if conv and not last_block:
                    take_std(act, nc, st, var_ready, std_ready, n + 1)
                act.wait_ge(run_ready, n)
                act.wait_ge(out_free[h], i + 1)
                if merge is not None:
                    act.wait_ge(in_landed[h], (i + 1) * (16 * n_in))
                nc.scalar.copy(sums[:, h, :, wide - D:wide], rows_of(run[:, :, 1:BS + 1])).then_inc(sums_ready[h], 1)
                act.wait_ge(sums_ready[h], i + 1)
                act.sem_inc(run_read, 1)

            if conv:
                prepare(0, 0)
                take_std(act, nc, st, var_ready, std_ready, 1)
                with act.Fori(0, IT - 1) as i:
                    prepare(i, 1)
                    consume(i, 0)
                    prepare(i + 1, 0)
                    consume(i, 1)
                prepare(IT - 1, 1)
                consume(IT - 1, 0)
                consume(IT - 1, 1, last_block=True)
            else:
                skewed(act, prepare, consume)
            if merge is not None:
                act.dma_start(fixed[:, 0:D], merge[NPAD:NPAD + P, :]).then_inc(old_fix, 16)
            act.wait_ge(fix_done, 1)
            nc.scalar.copy(fixed[:, wide - D:wide], pfix[:, 0:D]).then_inc(fix_copied, 1)
            act.wait_ge(fix_copied, 1)
            if merge is not None:
                act.wait_ge(old_fix, 16)
            act.dma_start(to[NPAD:NPAD + P, :], fixed[:, :]).then_inc(fix_stored, 16)
            act.wait_ge(fix_stored, 16)

        @block.sync
        def _(sp):
            def prepare(i, h):
                if n_in:
                    sp.wait_ge(out_free[h], i + 1)
                if acc_in is not None:
                    sp.dma_start(acc[:, h, :, :], block_of(acc_in, i, h, D)).then_inc(in_landed[h], 16)
                if merge is not None:
                    sp.dma_start(sums[:, h, :, 0:D], block_of(merge, i, h, D)).then_inc(in_landed[h], 16)

            def consume(i, h):
                if has_side:
                    sp.wait_ge(side_ready[h], i + 1)
                if acc_out is not None:
                    sp.dma_start(block_of(acc_out, i, h, D), acc[:, h, :, :]).then_inc(out_stored[h], 16)
                if r_out is not None:
                    sp.dma_start(block_of(r_out, i, h, D), res[:, h, :, :]).then_inc(out_stored[h], 16)
                sp.wait_ge(sums_ready[h], i + 1)
                sp.dma_start(block_of(to, i, h, wide), sums[:, h, :, :]).then_inc(out_stored[h], 16)
                sp.wait_ge(out_stored[h], (i + 1) * (16 * n_out))
                sp.sem_inc(out_free[h], 1)

            sp.sem_inc(out_free[0], 1)
            sp.sem_inc(out_free[1], 1)
            skewed(sp, prepare, consume)

        @block.tensor
        def _(pe):
            if product_of:
                with pe.Fori(0, IT) as i:
                    for h in range(2):
                        pe.wait_ge(left_ready, 2 * i + h + 1)
                        transpose_pairs(pe, tp, left[:, h * conv, :, :], g.ident[:, :]).then_inc(left_turned, 1)
                        pe.wait_ge(left_copied, 2 * i + h + 1)
                        if conv:
                            pe.wait_ge(mm_read, 2 * i + h + 1)
                        if wh is not None:
                            multiply_pairs(pe, mm2, [(leftT, wh[:, :], D2)])
                        multiply_pairs(pe, mm, [(leftT, wu[:, :], D2)]).then_inc(mm_ready, 1)
            pe.wait_ge(fix_ready, 1)
            pe.matmul(pfix[:, 0:D], g.carries[:, :], part[:, :], start=True, stop=False)
            pe.matmul(pfix[:, 0:D], g.ident[:, :], fix[:, :], start=False, stop=True).then_inc(fix_done, 1)

        @block.vector
        def _(dve):
            def values(i, h):
                n = 2 * i + h + 1
                got = rows[:, h, :, :]
                dve.wait_ge(sc_ready, n)
                dve.wait_ge(landed[h], (i + 1) * (16 * BS))
                if u_new is not None:
                    dve.wait_ge(val_read, n)
                if kind == "cheb_first":
                    at = (2 * i + h) * (NSC * BS)
                    flat = g.sc[:, :, :, :].rearrange("p b k c -> p (b k c)")

                    def put(which):
                        return flat[:, bass.ds(at + which * BS, BS)]

                    dis, dinv = got[:, :, EX], got[:, :, EX + 1]
                    dve.tensor_tensor(t1[:, h, :], staged(h, EW), dis, ALU.mult)
                    dve.tensor_copy(left[:, 0, :, :], got[:, :, D:2 * D]).then_inc(left_ready, 1)
                    dve.tensor_tensor(put(D1), dinv, dinv, ALU.mult)
                    dve.tensor_scalar(put(NDIS), dis, -1.0, None, ALU.mult)
                    dve.tensor_copy(put(DINV), dinv)
                    dve.tensor_copy(put(ZSRC), got[:, :, EX + 3])
                    dve.tensor_copy(g.last_src[:, bass.ds((2 * i + h) * BS, BS)], got[:, :, EX + 2])
                    dve.drain()
                    dve.scalar_tensor_tensor(put(D0), t1[:, h, :], -1.0, dis, ALU.mult, ALU.mult)
                    dve.tensor_tensor(rows_of(v), got[:, :, D:2 * D], over_features(t1[:, h, :]), ALU.mult).then_inc(val_ready, 1)
                    dve.wait_ge(out_free[h], i + 1)
                    dve.tensor_copy(res[:, h, :, :], got[:, :, 0:D])
                elif kind == "cheb":
                    dve.tensor_tensor(rows_of(v), got[:, :, 0:D], over_features(staged(h, D0)), ALU.mult).then_inc(val_ready, 1)
                elif kind == "cheb_last":
                    dve.tensor_tensor(rows_of(tmp[:, :, :]), got[:, :, 0:D], over_features(staged(h, D0)), ALU.mult)
                    dve.drain()
                    dve.sem_inc(slot_free[h], 1)
                    dve.scalar_tensor_tensor(v, tmp[:, :, :], 2.0, u_block(u_old, i, h), ALU.mult, ALU.subtract).then_inc(val_ready, 1)
                    dve.wait_ge(in_landed[h], (i + 1) * (16 * n_in))
                    dve.wait_ge(mm_ready, n)
                    for c, piece in products(mm):
                        dve.tensor_tensor(rows_of(v)[:, c, :], acc[:, h, c, :], piece, ALU.add)
                elif kind == "jacobi_first":
                    dve.tensor_tensor(x1[:, :, :], got[:, :, 0:D], over_features(staged(h, NDIS)), ALU.mult)
                    dve.drain()
                    dve.sem_inc(slot_free[h], 1)
                    dve.wait_ge(in_landed[h], (i + 1) * (16 * n_in))
                    dve.tensor_tensor(x1[:, :, :], acc[:, h, :, :], x1[:, :, :], ALU.add)
                    dve.drain()
                    layernorm(dve, x1[:, :, :], x1[:, :, :], sq[:, :, :], st, var_ready, std_ready, n)
                    dve.tensor_tensor(rows_of(v), x1[:, :, :], over_features(staged(h, DINV)), ALU.mult).then_inc(val_ready, 1)
                elif kind in ("jacobi", "jacobi_last"):
                    dve.tensor_tensor(rows_of(tmp[:, :, :]), got[:, :, 0:D], over_features(staged(h, D1)), ALU.mult)
                    dve.drain()
                    dve.sem_inc(slot_free[h], 1)
                    dve.scalar_tensor_tensor(v, u_block(u_old, i, h), beta[:, 0:1], tmp[:, :, :], ALU.mult, ALU.add).then_inc(val_ready, 1)
                elif kind == "conv_first":
                    dve.wait_ge(mm_ready, n)
                    dve.wait_ge(out_free[h], i + 1)
                    for c, piece in products(mm):
                        dve.tensor_copy(rows_of(v)[:, c, :], piece)
                    for c, piece in products(mm2):
                        last = dve.tensor_tensor(acc[:, h, c, :], piece, over_columns(g.b_l1[:, :], c.stop - c.start), ALU.add)
                    last.then_inc(side_ready[h], 1)
                    dve.drain()
                    dve.sem_inc(mm_read, 1)
                elif kind == "conv_last":
                    dve.wait_ge(in_landed[h], (i + 1) * (16 * n_in))
                    dve.tensor_tensor(rows_of(tmp[:, :, :]), got[:, :, 0:D], acc[:, h, :, :], ALU.add)
                    dve.drain()
                    dve.sem_inc(slot_free[h], 1)
                    dve.tensor_scalar(v, tmp[:, :, :], 0.0, None, ALU.max)

            def beside(i, h):
                n = 2 * i + h + 1
                if kind == "cheb_first":
                    dve.wait_ge(mm_ready, n)
                    for c, piece in products(mm2):
                        dve.tensor_tensor(res[:, h, c, :], res[:, h, c, :], piece, ALU.add)
                    for c, piece in products(mm):
                        last = dve.tensor_tensor(acc[:, h, c, :], piece, t1[:, h, c].unsqueeze(2).broadcast_to([P, c.stop - c.start, D]), ALU.mult)
                    last.then_inc(side_ready[h], 1)
                elif kind == "cheb":
                    dve.wait_ge(in_landed[h], (i + 1) * (16 * n_in))
                    dve.wait_ge(mm_ready, n)
                    for c, piece in products(mm):
                        last = dve.tensor_tensor(acc[:, h, c, :], acc[:, h, c, :], piece, ALU.add)
                    last.then_inc(side_ready[h], 1)
                elif kind == "jacobi_first":
                    dve.tensor_scalar(acc[:, h, :, :].rearrange("p c f -> p (c f)").rearrange("p (f c) -> p f c", c=BS), v,
                                      g.omega[:, 0:1], None, ALU.mult).then_inc(side_ready[h], 1)
                elif kind == "jacobi":
                    dve.wait_ge(in_landed[h], (i + 1) * (16 * n_in))
                    acc_f = acc[:, h, :, :].rearrange("p c f -> p (c f)").rearrange("p (f c) -> p f c", c=BS)
                    dve.scalar_tensor_tensor(acc_f, v, omega[:, 0:1], acc_f, ALU.mult, ALU.add).then_inc(side_ready[h], 1)

            def normalise(i, h):
                n = 2 * i + h + 1
                dve.wait_ge(landed[h], (i + 1) * (16 * BS))
                layernorm(dve, rows[:, h, :, :], left[:, h, :, :], sq[:, :, :], st, var_ready, std_ready, n)
                dve.sem_inc(slot_free[h], 1)
                dve.sem_inc(left_ready, 1)

            def scan(i, h):
                n = 2 * i + h + 1
                values(i, h)
                if kind == "jacobi_last":
                    dve.drain()
                    dve.wait_ge(in_landed[h], (i + 1) * (16 * n_in))
                    acc_f = acc[:, h, :, :].rearrange("p c f -> p (c f)").rearrange("p (f c) -> p f c", c=BS)
                    dve.scalar_tensor_tensor(v, v, omega[:, 0:1], acc_f, ALU.mult, ALU.add)
                dve.drain()
                if kind in ("cheb_first", "cheb"):
                    dve.sem_inc(slot_free[h], 1)
                dve.wait_ge(run_read, n)
                dve.tensor_tensor_scan(run[:, :, :].rearrange("p f c -> p (f c)"), same[:, h, :, :].rearrange("p f c -> p (f c)"),
                                       val[:, :, :].rearrange("p f c -> p (f c)"), 0.0, ALU.mult, ALU.add).then_inc(run_ready, 1)
                dve.tensor_tensor(tmp[:, :, :], v, staged(h, FIRST).unsqueeze(1).broadcast_to([P, D, BS]), ALU.mult)
                dve.drain()
                dve.tensor_copy(val[:, :, 0], run[:, :, BS])
                dve.reduce_sum(part[:, :], tmp[:, :, :], AX)
                dve.drain()
                dve.tensor_tensor(fix[:, :], fix[:, :], part[:, :], ALU.add)
                beside(i, h)
                dve.drain()
                dve.sem_inc(sc_free[h], 1)

            dve.memset(fix[:, :], 0.0)
            dve.memset(val[:, :, 0], 0.0)
            dve.memset(same[:, :, :, 0], 0.0)
            if kind in ("jacobi", "jacobi_last"):
                dve.tensor_copy(beta[:, :], g.betas[:, bass.ds(k, 1)])
                dve.tensor_copy(omega[:, :], g.omega[:, bass.ds(k, 1)])
            dve.drain()
            for q in slot_free + sc_free + [run_read, val_read]:
                dve.sem_inc(q, 1)
            if conv:
                dve.sem_inc(mm_read, 1)
            if zero is not None:
                dve.memset(zero[:, :], 0.0)
            if conv:
                skewed(dve, normalise, scan)
            else:
                with dve.Fori(0, IT) as i:
                    scan(i, 0)
                    scan(i, 1)
            dve.tensor_copy(part[:, :], run[:, :, BS]).then_inc(fix_ready, 1)



def message_stage(nc, io, g):
    with Stage(nc, "msg") as s:
        rows, idx_now = s.sb("rows", [P, 2, BS, H2ROW]), s.sb("idx_now", [P, 2 * BS], I32)
        cw, dist = s.sb("cw", [P, COLS]), s.sb("dist", [P, COLS])
        sc = s.sb("sc", [P, 2, 2 * BS])
        attr, aT, g1 = s.sb("attr", [P, 2, BS, R]), s.sb("aT", [P, NPAIR * P]), s.sb("g1", [D2 + 1, NPAIR * P])
        one, oneT = s.sb("one", [P, BS, P], F16), s.sb("oneT", [P, 2, BS, P])
        ident_h = s.sb("ident_h", [P, P], F16)
        gate, junk, adapt, wgt = s.sb("gate", [P, 2, BS, D]), s.sb("junk", [P, P]), s.sb("adapt", [P, BS]), s.sb("wgt", [P, BS])
        msg = s.sb("msg", [P, 2, BS, H2ROW])
        half_pi = s.sb("half_pi", [P, 1])
        zeros = s.sb("zeros", [P, BS * H2ROW])
        tp, ph = s.ps("tp", [P, 2, 512]), s.ps("ph", [P, 2, 512])
        pone, pterm = s.ps("pone", [P, 2, 1024], F16), s.ps("pterm", [P, 2, 512])
        HB = BS // 2
        slot_free, landed, idx_staged, begun = s.sems("slot_free"), s.sems("landed"), s.sem("idx_staged"), s.sem("begun")
        dist_landed, dist_ready, cos_ready, cw_ready, zeroed = (s.sem(n) for n in (
            "dist_landed", "dist_ready", "cos_ready", "cw_ready", "zeroed"))
        sc_free, sc_ready = s.sems("sc_free"), s.sem("sc_ready")
        attr_landed, attr_free = s.sems("attr_landed"), s.sems("attr_free")
        attr_turned, attr_copied, hid_ready, silu_done, gate_ready, gate_copied = (s.sem(n) for n in (
            "attr_turned", "attr_copied", "hid_ready", "silu_done", "gate_ready", "gate_copied"))
        one_ready, one_turned, one_copied, term_ready, term_read = (s.sem(n) for n in (
            "one_ready", "one_turned", "one_copied", "term_ready", "term_read"))
        oneT_free, ones_ready = s.sems("oneT_free"), s.sem("ones_ready")
        out_ready, out_free, out_stored = s.sems("out_ready"), s.sems("out_free"), s.sems("out_stored")
        cleared = s.sem("cleared")
        block = s.ctx.enter_context(nc.Block())

        @block.gpsimd
        def _(pool):
            gather_rows(pool, g.tab_h2, g.dst_idx, idx_now, rows, H2ROW, slot_free, landed, idx_staged, begun)

        @block.sync
        def _(sp):
            sp.dma_start(dist[:, :], io.edge_weight.rearrange("(p c) -> p c", p=P)).then_inc(dist_landed, 16)
            sp.sem_inc(out_free[0], 1)
            sp.sem_inc(out_free[1], 1)
            sp.wait_ge(zeroed, 1)
            for q in range(NAGG):
                sp.dma_start(g.agg[q][0:NPAD, :].rearrange("(p b c) w -> p b (c w)", p=P, c=BS),
                             zeros[:, :].unsqueeze(1).broadcast_to([P, NB, BS * H2ROW])).then_inc(cleared, 16)
                sp.dma_start(g.agg[q][NPAD:NPAD + P, :], zeros[:, 0:H2ROW]).then_inc(cleared, 16)

            def prepare(i, h):
                sp.wait_ge(attr_free[h], i + 1)
                sp.dma_start(attr[:, h, :, :], block_of(io.edge_attr, i, h, R)).then_inc(attr_landed[h], 16)

            def consume(i, h):
                sp.wait_ge(out_ready[h], i + 1)
                sp.dma_start(block_of(g.msg, i, h, H2ROW), msg[:, h, :, :]).then_inc(out_stored[h], 16)
                sp.wait_ge(out_stored[h], (i + 1) * 16)
                sp.sem_inc(out_free[h], 1)

            skewed(sp, prepare, consume)
            sp.wait_ge(cleared, 32 * NAGG)

        @block.scalar
        def _(act):
            act.wait_ge(dist_ready, 1)
            nc.scalar.activation(cw[:, :], dist[:, :], ACT.Sin, bias=half_pi[:, 0:1], scale=-math.pi / CUTOFF
                                 ).then_inc(cos_ready, 1)
            act.wait_ge(cw_ready, 1)
            flat = g.sc[:, :, :, :].rearrange("p b k c -> p (b k c)")

            def gates(i, h):
                n = 2 * i + h + 1
                act.wait_ge(sc_free[h], i + 1)
                nc.scalar.copy(sc[:, h, 0:BS], cw[:, bass.ds((2 * i + h) * BS, BS)])
                nc.scalar.copy(sc[:, h, BS:2 * BS], flat[:, bass.ds((2 * i + h) * (NSC * BS) + ZSRC * BS, BS)]
                               ).then_inc(sc_ready, 1)
                act.wait_ge(attr_turned, n)
                copy_turned(nc, aT, tp, 2 * R).then_inc(attr_copied, 1)
                act.wait_ge(one_turned, n)
                act.wait_ge(oneT_free[h], i + 1)
                nc.scalar.copy(oneT[:, h, 0:8, :].rearrange("p c e -> p (c e)"), pone[:, 0, :])
                nc.scalar.copy(oneT[:, h, 8:BS, :].rearrange("p c e -> p (c e)"), pone[:, 1, 0:(BS - 8) * P]).then_inc(one_copied, 1)
                act.wait_ge(hid_ready, n)
                q = 4 * P
                nc.scalar.activation(g1[0:D2, 0:q], ph[0:D2, 0, 0:q], ACT.Silu, bias=g.b1[:, 0:1])
                nc.scalar.activation(g1[0:D2, q:NPAIR * P], ph[0:D2, 1, 0:NPAIR * P - q], ACT.Silu,
                                     bias=g.b1[:, 0:1]).then_inc(silu_done, 1)
                act.wait_ge(gate_ready, n)
                for c, piece in products(tp):
                    last = nc.scalar.copy(gate[:, h, c, :], piece)
                last.then_inc(gate_copied, 1)

            with act.Fori(0, IT) as i:
                for h in range(2):
                    gates(i, h)

        @block.tensor
        def _(pe):
            def turn(i, h):
                n = 2 * i + h + 1
                pe.wait_ge(attr_landed[h], (i + 1) * 16)
                transpose_pairs(pe, tp, attr[:, h, :, :], g.ident[:, :], 2 * R).then_inc(attr_turned, 1)
                pe.wait_ge(one_ready, n)
                for c in range(BS):
                    last = pe.transpose(pone[:, c // 8, (c % 8) * P:(c % 8 + 1) * P], one[:, c, :], ident_h[:, :])
                last.then_inc(one_turned, 1)

            def hidden(i, h):
                n = 2 * i + h + 1
                pe.wait_ge(attr_copied, n)
                pe.sem_inc(attr_free[h], 1)
                pe.matmul(ph[0:D2, 0, :], g.W1[:, :], aT[0:2 * R, 0:4 * P], start=True, stop=True)
                pe.matmul(ph[0:D2, 1, 0:(NPAIR - 4) * P], g.W1[:, :], aT[0:2 * R, 4 * P:NPAIR * P], start=True,
                          stop=True).then_inc(hid_ready, 1)

            def second(i, h):
                pe.wait_ge(silu_done, 2 * i + h + 1)
                multiply_pairs(pe, tp, [(g1, g.W2[:, :], D2 + 1)]).then_inc(gate_ready, 1)

            def term(i, h, half):
                pe.wait_ge(term_read, (2 * i + h) * 2 + half + 1)
                for c in range(HB):
                    last = pe.matmul(pterm[:, c // 4, (c % 4) * P:(c % 4) * P + NZ], oneT[0:NZ, h, half * HB + c, :],
                                     g.pair_term[:, :], start=True, stop=True)
                last.then_inc(term_ready, 1)

            def body(i, h, last):
                n = 2 * i + h + 1
                pe.wait_ge(one_copied, n)
                term(i, h, 0)
                pe.wait_ge(gate_copied, n)
                if not last:
                    turn(*next_block(i, h))
                term(i, h, 1)
                pe.wait_ge(term_ready, 2 * n)
                pe.sem_inc(oneT_free[h], 1)
                if not last:
                    hidden(*next_block(i, h))
                    second(*next_block(i, h))

            for q in attr_free + oneT_free:
                pe.sem_inc(q, 1)
            pe.wait_ge(ones_ready, 1)
            turn(0, 0)
            hidden(0, 0)
            second(0, 0)
            with_next(pe, body)

        @block.vector
        def _(dve):
            dve.memset(zeros[:, :], 0.0).then_inc(zeroed, 1)
            dve.memset(half_pi[:, :], math.pi / 2)
            dve.memset(msg[:, :, :, D + 1:H2ROW], 0.0)
            dve.tensor_copy(ident_h[:, :], g.ident[:, :])
            dve.memset(g1[D2:D2 + 1, :], 1.0).then_inc(ones_ready, 1)
            dve.wait_ge(dist_landed, 16)
            dve.tensor_scalar(cw[:, :], dist[:, :], CUTOFF, 0.5, ALU.is_lt, ALU.mult)
            dve.drain()
            dve.tensor_copy(g.half_keep[:, :], cw[:, :])
            dve.scalar_tensor_tensor(dist[:, :], dist[:, :], -1.0, dist[:, :], ALU.mult, ALU.max)
            dve.drain()
            dve.tensor_scalar(dist[:, :], dist[:, :], CUTOFF, None, ALU.min)
            dve.drain()
            dve.sem_inc(dist_ready, 1)
            dve.wait_ge(cos_ready, 1)
            dve.scalar_tensor_tensor(cw[:, :], cw[:, :], 1.0, g.half_keep[:, :], ALU.add, ALU.mult).then_inc(cw_ready, 1)
            for q in slot_free + sc_free:
                dve.sem_inc(q, 1)
            dve.sem_inc(term_read, 1)

            def one_hots(i, h, first=False):
                n = 2 * i + h + 1
                dve.wait_ge(sc_ready, n)
                if not first:
                    dve.wait_ge(one_turned, n - 1)
                for c in range(BS):
                    last = dve.tensor_scalar(one[:, c, :], g.iota[:, :], sc[:, h, BS + c:BS + c + 1], None, ALU.is_equal)
                last.then_inc(one_ready, 1)

            def terms(i, h, half):
                dve.wait_ge(term_ready, (2 * i + h) * 2 + half + 1)
                for c in range(HB):
                    cc = half * HB + c
                    dve.scalar_tensor_tensor(
                        junk[:, 0:NZ], g.iota[:, 0:NZ], rows[:, h, cc, D:D + 1],
                        pterm[:, c // 4, (c % 4) * P:(c % 4) * P + NZ],
                        ALU.is_equal, ALU.mult, accum_out=adapt[:, cc:cc + 1])
                    dve.drain()
                dve.sem_inc(term_read, 1)

            def messages(i, h):
                n = 2 * i + h + 1
                got, m = rows[:, h, :, :], msg[:, h, :, :]
                dve.wait_ge(landed[h], (i + 1) * (16 * BS))
                dve.tensor_tensor(wgt[:, :], sc[:, h, 0:BS], got[:, :, D + 1], ALU.mult)
                terms(i, h, 0)
                dve.wait_ge(out_free[h], i + 1)
                dve.tensor_tensor(m[:, :, 0:D], got[:, :, 0:D], over_features(wgt[:, :]), ALU.mult)
                dve.tensor_copy(m[:, :, D], got[:, :, D + 1])
                terms(i, h, 1)
                dve.sem_inc(slot_free[h], 1)
                dve.wait_ge(gate_copied, n)
                dve.tensor_tensor(gate[:, h, :, :], gate[:, h, :, :], over_features(adapt[:, :]), ALU.add)
                dve.drain()
                dve.tensor_tensor(m[:, :, 0:D], m[:, :, 0:D], gate[:, h, :, :], ALU.mult).then_inc(out_ready[h], 1)
                dve.drain()
                dve.sem_inc(sc_free[h], 1)

            one_hots(0, 0, first=True)
            with dve.Fori(0, IT - 1) as i:
                one_hots(i, 1)
                messages(i, 0)
                one_hots(i + 1, 0)
                messages(i, 1)
            one_hots(IT - 1, 1)
            messages(IT - 1, 0)
            messages(IT - 1, 1)


def add_up_stage(nc, io, g):
    with Stage(nc, "add") as s:
        msg, out = s.sb("msg", [P, 2, BS, H2ROW]), s.sb("out", [P, 2, BS, H2ROW])
        src_row = s.sb("src_row", [P, 2, BS, P])
        srcs = s.sb("srcs", [P, 2, BS])
        same, junk, before = s.sb("same", [P, 2, BS, P]), s.sb("junk", [P, P]), s.sb("before", [P, BS])
        dump_i, dump = s.sb("dump_i", [P, 1], I32), s.sb("dump", [P, 1])
        where = s.sb("where", [P, 2, BS], I32)
        t0 = s.sb("t0", [P, 2, BS])
        ps = [s.ps(f"ps{h}", [P, 2, 512]) for h in range(2)]
        HB = BS // 2
        in_landed, in_free = s.sems("in_landed"), s.sems("in_free")
        dump_ready = s.sem("dump_ready")
        same_ready, summed, copied = s.sem("same_ready"), s.sem("summed"), s.sem("copied")
        where_ready = s.sem("where_ready")
        slot_done, sums_free = s.sems("slot_done"), s.sems("sums_free")
        srcs_ready, srcs_free = s.sem("srcs_ready"), s.sems("srcs_free")
        added, begun = s.sems("added", NAGG), s.sem("begun")
        block = s.ctx.enter_context(nc.Block())

        @block.sync
        def _(sp):
            with sp.Fori(0, IT) as i:
                for h in range(2):
                    sp.wait_ge(in_free[h], i + 1)
                    sp.dma_start(msg[:, h, :, :], block_of(g.msg, i, h, H2ROW)).then_inc(in_landed[h], 16)
                    sp.dma_start(src_row[:, h, :, :].rearrange("p c e -> p (c e)"),
                                 g.src_cols[bass.ds((2 * i + h) * BS, BS), :].rearrange("c e -> (c e)").partition_broadcast(P)
                                 ).then_inc(in_landed[h], 16)

        @block.scalar
        def _(act):
            with act.Fori(0, IT) as i:
                for h in range(2):
                    act.wait_ge(srcs_free[h], i + 1)
                    nc.scalar.copy(srcs[:, h, :], g.src_idx[:, bass.ds((2 * i + h) * BS, BS)]).then_inc(srcs_ready, 1)
                    act.wait_ge(summed, 2 * i + h + 1)
                    act.wait_ge(slot_done[h], i + 1)
                    for q in range(2):
                        last = nc.scalar.copy(out[:, h, q * HB:(q + 1) * HB, :].rearrange("p c w -> p (c w)"), ps[h][:, q, 0:HB * H2ROW])
                    last.then_inc(copied, 1)
                    act.wait_ge(copied, 2 * i + h + 1)
                    act.sem_inc(sums_free[h], 1)

        @block.tensor
        def _(pe):
            pe.sem_inc(sums_free[0], 1)
            pe.sem_inc(sums_free[1], 1)
            with pe.Fori(0, IT) as i:
                for h in range(2):
                    pe.wait_ge(same_ready, 2 * i + h + 1)
                    pe.wait_ge(sums_free[h], i + 1)
                    for c in range(BS):
                        last = pe.matmul(ps[h][:, c // HB, (c % HB) * H2ROW:(c % HB + 1) * H2ROW], same[:, h, c, :],
                                         msg[:, h, c, :], start=True, stop=True)
                    last.then_inc(summed, 1)
                    pe.wait_ge(summed, 2 * i + h + 1)
                    pe.sem_inc(in_free[h], 1)

        @block.vector
        def _(dve):
            for q in in_free + srcs_free:
                dve.sem_inc(q, 1)
            dve.wait_ge(dump_ready, 1)
            dve.tensor_copy(dump[:, :], dump_i[:, :])
            dve.drain()
            with dve.Fori(0, IT) as i:
                for h in range(2):
                    dve.wait_ge(in_landed[h], (i + 1) * 32)
                    dve.wait_ge(srcs_ready, 2 * i + h + 1)
                    for c in range(BS):
                        dve.tensor_scalar(same[:, h, c, :], src_row[:, h, c, :], srcs[:, h, c:c + 1], None, ALU.is_equal)
                    for c in range(BS):
                        dve.scalar_tensor_tensor(junk[:, :], src_row[:, h, c, :], srcs[:, h, c:c + 1], g.lower[:, :],
                                                 ALU.is_equal, ALU.mult, accum_out=before[:, c:c + 1])
                        dve.drain()
                    dve.sem_inc(same_ready, 1)
                    dve.tensor_scalar(t0[:, 0, :], before[:, :], 0.5, None, ALU.is_lt)
                    dve.tensor_scalar(t0[:, 1, :], srcs[:, h, :], dump[:, 0:1], None, ALU.subtract)
                    dve.drain()
                    dve.sem_inc(srcs_free[h], 1)
                    dve.tensor_tensor(t0[:, 1, :], t0[:, 1, :], t0[:, 0, :], ALU.mult)
                    dve.drain()
                    dve.wait_ge(slot_done[h], i + 1)
                    dve.tensor_scalar(where[:, h, :], t0[:, 1, :], dump[:, 0:1], None, ALU.add).then_inc(where_ready, 1)

        @block.gpsimd
        def _(pool):
            pool.iota(dump_i[:, :], pattern=[[0, 1]], base=NPAD, channel_multiplier=1).then_inc(dump_ready, 1)
            pool.sem_inc(slot_done[0], 1)
            pool.sem_inc(slot_done[1], 1)
            per = 2 * BS // NAGG

            def adds(i, h, first):
                pool.wait_ge(copied, 2 * i + h + 1)
                pool.wait_ge(where_ready, 2 * i + h + 1)
                pool.sem_inc(begun, 1)
                for c in range(BS):
                    n = h * BS + c
                    if n >= NAGG or not first:
                        pool.wait_ge(added[n % NAGG], i * (16 * per) + 16 * (n // NAGG))
                        pool.sem_inc(begun, 1)
                    if c == NAGG - 1 and not (first and h == 0):
                        pool.sem_inc(slot_done[1 - h], 1)
                    pool.indirect_dma_start(
                        out=g.agg[n % NAGG], out_offset=bass.IndirectOffsetOnAxis(ap=where[:, h, c:c + 1], axis=0),
                        in_=out[:, h, c, :], in_offset=None, compute_op=ALU.add,
                    ).then_inc(added[n % NAGG], 16)

            adds(0, 0, True)
            adds(0, 1, True)
            with pool.Fori(1, IT) as i:
                adds(i, 0, False)
                adds(i, 1, False)
            for q in range(NAGG):
                pool.wait_ge(added[q], IT * (16 * per))


def gnn_program(nc, args, out):
    with Stage(nc, "all") as s:
        io = Names()
        io.x, io.src, io.dst, io.edge_attr = args["x"], args["src"], args["dst"], args["edge_attr"]
        io.edge_weight, io.node_type, io.node_vec, io.w0 = args["edge_weight"], args["node_type"], args["node_vec"], args["w0"]
        io.bias0, io.lap, io.mf, io.W1 = args["bias0"], args["lap"], args["mf"], args["W1"]
        io.b1, io.W2, io.b2, io.emb = args["b1"], args["W2"], args["b2"], args["emb"]
        io.adaptW, io.gamma, io.beta, io.w_rel1 = args["adaptW"], args["gamma"], args["beta"], args["w_rel1"]
        io.w_root1, io.b_l1, io.w_rel2, io.w_root2 = args["w_root1"], args["b_l1"], args["w_rel2"], args["w_root2"]
        io.b_l2 = args["b_l2"]
        io.out = out
        g = Names()
        dram = lambda name, rows, w: nc.dram_tensor(name, [rows, w], F32).ap()
        g.tab_in = dram("tab_in", NPAD, W1ROW)
        g.tab_s = [dram("tab_s0", ROWS, D), dram("tab_s1", ROWS, D)]
        g.tab_a0, g.tab_a2 = dram("tab_a0", ROWS, D), dram("tab_a2", ROWS, D)
        g.tab_both, g.tab_both2 = dram("tab_both", ROWS, D2), dram("tab_both2", ROWS, D2)
        g.sum_tables = [(g.tab_s[0], D), (g.tab_s[1], D), (g.tab_a0, D), (g.tab_a2, D), (g.tab_both, D2), (g.tab_both2, D2)]
        g.edge_y, g.edge_r, g.edge_acc, g.edge_q = dram("edge_y", NPAD, D), dram("edge_r", NPAD, D), dram("edge_acc", NPAD, D), dram("edge_q", NPAD, D)
        g.x2, g.x3, g.tab_h2 = dram("x2", NPAD, D), dram("x3", NPAD, D), dram("tab_h2", NPAD, H2ROW)
        g.msg = dram("msg", NPAD, H2ROW)
        g.agg = [dram(f"agg{q}", NPAD + P, H2ROW) for q in range(NAGG)]
        g.src_cols = dram("src_cols", COLS, P)

        g.ident, g.lower, g.carries, g.iota = s.sb("ident", [P, P]), s.sb("lower", [P, P]), s.sb("carries", [P, P]), s.sb("iota", [P, P])
        g.src_idx, g.dst_idx = s.sb("src_idx", [P, COLS], I32), s.sb("dst_idx", [P, COLS], I32)
        g.last_src, g.last_node = s.sb("last_src", [P, COLS], I32), s.sb("last_node", [P, COLS], I32)
        g.sc = s.sb("sc", [P, NB, NSC, BS])
        g.wh, g.wu = s.sb("wh", [D2, D2]), [s.sb(f"wu{k}", [D2, D2]) for k in range(3)]
        g.w_rel1, g.w_root1 = s.sb("w_rel1", [D2, D2]), s.sb("w_root1", [D2, D2])
        g.w_rel2, g.w_root2 = s.sb("w_rel2", [D2, D2]), s.sb("w_root2", [D2, D2])
        g.W1, g.W2, g.b1 = s.sb("W1", [2 * R, D2]), s.sb("W2", [D2 + 1, D2]), s.sb("b1", [D2, 1])
        g.bias0, g.b_l1, g.b_l2 = s.sb("bias0", [P, D]), s.sb("b_l1", [P, D]), s.sb("b_l2", [P, D])
        g.gamma, g.beta = s.sb("gamma", [P, D]), s.sb("beta", [P, D])
        g.omega, g.betas, g.p0w, g.pair_term = s.sb("omega", [P, K1]), s.sb("betas", [P, K1]), s.sb("p0w", [P, 1]), s.sb("pair_term", [NZ, NZ])

        weight_stage(nc, io, g)
        node_stage_in(nc, io, g)
        s0, s1 = g.tab_s
        with Stage(nc, "values") as vs:
            ua = vs.sb("ua", [P, COLS * D])
            propagate(nc, g, "c0", "cheb_first", g.tab_in, W1ROW, g.src_idx, s0, u_new=ua, acc_out=g.edge_y, r_out=g.edge_r)
            propagate(nc, g, "c1", "cheb", s0, D, g.last_src, s1, acc_in=g.edge_y, acc_out=g.edge_y)
            propagate(nc, g, "c2", "cheb_last", s1, D, g.last_src, g.tab_a0, u_old=ua, acc_in=g.edge_y)
            ub = vs.sb("ub", [P, COLS * D])
            propagate(nc, g, "j0", "jacobi_first", g.tab_a0, D, g.last_src, s0, u_new=ua, acc_in=g.edge_r,
                      acc_out=g.edge_acc, zero=ub)
            with nc.Fori(0, (K1 - 2) // 2) as r:
                propagate(nc, g, "jo", "jacobi", s0, D, g.last_src, s1, u_old=ub, u_new=ub, k=2 * r + 1,
                          acc_in=g.edge_acc, acc_out=g.edge_acc)
                propagate(nc, g, "je", "jacobi", s1, D, g.last_src, s0, u_old=ua, u_new=ua, k=2 * r + 2,
                          acc_in=g.edge_acc, acc_out=g.edge_acc)
            propagate(nc, g, "j9", "jacobi_last", s0, D, g.last_src, g.tab_both, u_old=ub, k=K1 - 1,
                      acc_in=g.edge_acc, merge=g.tab_a0)
        node_stage_mid(nc, io, g)
        g.half_keep = s.sb("half_keep", [P, COLS])
        message_stage(nc, io, g)
        add_up_stage(nc, io, g)
        node_stage_late(nc, io, g)
        propagate(nc, g, "g0", "conv_first", g.x3, D, g.src_idx, g.tab_a2, acc_out=g.edge_q)
        propagate(nc, g, "g1", "conv_last", g.tab_a2, D, g.last_src, g.tab_both2, acc_in=g.edge_q, merge=g.tab_a2)
        node_stage_out(nc, io, g)


def kernel(**inputs):
    import numpy as np
    import concourse.bacc as bacc
    from concourse.bass_utils import run_bass_kernel_spmd

    def padded(name, value=0):
        a = np.asarray(inputs[name])
        out = np.full((NPAD,) + a.shape[1:], value, a.dtype)
        out[:N] = a
        return out

    arrays = {"x": padded("x"), "src": padded("src", NPAD - 1), "dst": padded("dst", NPAD - 1),
              "edge_attr": padded("edge_attr_40"), "edge_weight": padded("edge_weight"),
              "node_type": padded("node_type_119"), "node_vec": padded("node_vec")}
    for name, of in (("w0", "L0_gnn_weight"), ("bias0", "L0_gnn_bias"), ("lap", "L1_gnn_lap_coefs"),
                     ("mf", "L1_gnn_mf_weights"), ("W1", "L2_gnn_W1"), ("b1", "L2_gnn_b1"), ("W2", "L2_gnn_W2"),
                     ("b2", "L2_gnn_b2"), ("emb", "L2_gnn_emb"), ("adaptW", "L2_gnn_adaptW"), ("gamma", "L2_gnn_gamma"),
                     ("beta", "L2_gnn_beta"), ("w_rel1", "L3_gnn_w_rel1"), ("w_root1", "L3_gnn_w_root1"),
                     ("b_l1", "L3_gnn_b1"), ("w_rel2", "L3_gnn_w_rel2"), ("w_root2", "L3_gnn_w_root2"), ("b_l2", "L3_gnn_b2")):
        arrays[name] = np.ascontiguousarray(inputs[of])
    nc = bacc.Bacc("TRN2", target_bir_lowering=False, num_devices=1)
    args = {name: nc.dram_tensor(f"in_{name}", a.shape, mybir.dt.from_np(a.dtype), kind="ExternalInput").ap()
            for name, a in arrays.items()}
    out = nc.dram_tensor("out_x", [NPAD, D], F32, kind="ExternalOutput").ap()
    gnn_program(nc, args, out)
    r = run_bass_kernel_spmd(nc, [{f"in_{name}": a for name, a in arrays.items()}], core_ids=[0])
    return np.ascontiguousarray(r.results[0]["out_x"][:N])
```

```python
from contextlib import ExitStack
import math

import concourse.bass as bass
from concourse import mybir

ALU = mybir.AluOpType
ACT = mybir.ActivationFunctionType
AX = mybir.AxisListType.X
F32 = mybir.dt.float32
F16 = mybir.dt.float16
I32 = mybir.dt.int32

P = 128
N = 50000
D = 48
R = 40
NZ = 119
EMB = 32
BS = 14
COLS = 2 * BS * -(-N // (P * 2 * BS))
NB = COLS // BS
IT = NB // 2
NPAD = P * COLS
ZROW = NPAD + P
ROWS = NPAD + P + 1
NPAIR = BS // 2
D2 = 2 * D
W1ROW = 56
EX = D
H2ROW = 52
NAGG = 4
K1 = 10
CUTOFF = 6.0
EPS = 1e-5
ROUND = 12582912.0

SAME, FIRST, D0, D1, NDIS, DINV, ZSRC = range(7)
EW = D0
NSC = 7


def jacobi(n):
    if n == 1:
        return 2.0, 0.0
    m = 2 * n + 2
    return (m * (m - 1) * (m - 2) / (2 * n * (m - n) * (m - 2)),
            -2.0 * n * n * m / (2 * n * (m - n) * (m - 2)))


def jacobi_norms():
    out = []
    for i in range(K1 + 1):
        t1 = math.pow(2.0, 3.0) / (2 * i + 3.0)
        t2 = math.exp(math.lgamma(i + 2.0) - math.lgamma(i + 3.0))
        t3 = math.exp(math.lgamma(i + 2.0) - math.lgamma(i + 1.0))
        out.append(math.sqrt(t1 * t2 * t3))
    return out


SCALE = [1.0]
for _k in range(1, K1 + 1):
    SCALE.append(SCALE[-1] * jacobi(_k)[0])
BETA = [0.0, 0.0] + [jacobi(k)[1] * SCALE[k - 2] / SCALE[k] for k in range(2, K1 + 1)]


def over_features(scalars, w=D):
    return scalars.unsqueeze(2).broadcast_to([P, BS, w])


def over_columns(row, n=BS):
    return row.unsqueeze(1).broadcast_to([P, n, D])


def block_of(table, i, h, w):
    return table[0:NPAD, :].rearrange("(p c) w -> p c w", p=P)[:, bass.ds((2 * i + h) * BS, BS), 0:w]


def turned(tp, c):
    return tp[:, c // 4, (c % 4) * P:(c % 4 + 1) * P]


def product(mm, c):
    return mm[:, c // 5, (c % 5) * D2:(c % 5 + 1) * D2]


def products(mm):
    n = min(5, NPAIR)
    out = [(slice(0, 2 * n), mm[:, 0, 0:n * D2].rearrange("p (c f) -> p c f", f=D))]
    if NPAIR > n:
        out.append((slice(2 * n, BS), mm[:, 1, 0:(NPAIR - n) * D2].rearrange("p (c f) -> p c f", f=D)))
    return out


def transpose_pairs(pe, tp, x, ident, rows=D2):
    for c in range(NPAIR):
        last = pe.transpose(turned(tp, c)[0:rows, :], x[:, 2 * c:2 * c + 2, :].rearrange("p a f -> p (a f)"), ident)
    return last


def copy_turned(nc, xT, tp, rows=D2):
    n = min(4, NPAIR) * P
    nc.scalar.copy(xT[0:rows, 0:n], tp[0:rows, 0, 0:n])
    return nc.scalar.copy(xT[0:rows, n:NPAIR * P], tp[0:rows, 1, 0:NPAIR * P - n])


def multiply_pairs(pe, mm, pairs):
    for c in range(NPAIR):
        for k, (xT, w, rows) in enumerate(pairs):
            last = pe.matmul(product(mm, c), xT[0:rows, c * P:(c + 1) * P], w,
                             start=(k == 0), stop=(k == len(pairs) - 1))
    return last


def centre(dve, x, out, st):
    total, mean = st[:, 0, :], st[:, 1, :]
    dve.reduce_sum(total, x, AX)
    dve.drain()
    dve.tensor_scalar(mean, total, 1.0 / D, None, ALU.mult)
    dve.drain()
    return dve.tensor_tensor(out, x, over_features(mean), ALU.subtract)


def variance(dve, sq, st):
    total = st[:, 2, :]
    dve.reduce_sum(total, sq, AX)
    dve.drain()
    return dve.tensor_scalar(st[:, 3, :], total, 1.0 / D, EPS, ALU.mult, ALU.add)


def normalised(dve, x, out, st, relu=True):
    rstd = st[:, 2, :]
    dve.reciprocal(rstd, st[:, 4, :])
    dve.drain()
    if relu:
        return dve.scalar_tensor_tensor(out, x, 0.0, over_features(rstd), ALU.max, ALU.mult)
    return dve.tensor_tensor(out, x, over_features(rstd), ALU.mult)


def layernorm(dve, x, out, sq, st, var_ready, std_ready, count, relu=True):
    centre(dve, x, out, st)
    dve.drain()
    dve.tensor_tensor(sq, out, out, ALU.mult)
    dve.drain()
    variance(dve, sq, st).then_inc(var_ready, 1)
    dve.wait_ge(std_ready, count)
    normalised(dve, out, out, st, relu)
    dve.drain()


def take_std(act, nc, st, var_ready, std_ready, count):
    act.wait_ge(var_ready, count)
    nc.scalar.activation(st[:, 4, :], st[:, 3, :], ACT.Sqrt).then_inc(std_ready, 1)


class Names:
    pass


class Stage:

    def __init__(self, nc, name):
        self.nc, self.name, self.ctx, self.used = nc, name, ExitStack(), []

    def __enter__(self):
        return self

    def __exit__(self, *what):
        self.ctx.close()
        if self.used:
            self.nc.clear_and_free_semaphores(self.used)
            self.nc.all_engine_barrier()

    def sb(self, name, shape, dt=F32):
        return self.ctx.enter_context(self.nc.sbuf_tensor(f"{self.name}_{name}", shape, dt))

    def ps(self, name, shape, dt=F32):
        return self.ctx.enter_context(self.nc.psum_tensor(f"{self.name}_{name}", shape, dt))

    def sem(self, name):
        self.used.append(self.nc.alloc_semaphore(f"{self.name}_{name}"))
        return self.used[-1]

    def sems(self, name, n=2):
        return [self.sem(f"{name}{i}") for i in range(n)]


def skewed(engine, prepare, consume):
    prepare(0, 0)
    with engine.Fori(0, IT - 1) as i:
        prepare(i, 1)
        consume(i, 0)
        prepare(i + 1, 0)
        consume(i, 1)
    prepare(IT - 1, 1)
    consume(IT - 1, 0)
    consume(IT - 1, 1)


def skewed_by_two(engine, prepare, consume):
    prepare(0, 0)
    prepare(0, 1)
    with engine.Fori(0, IT - 1) as i:
        prepare(i + 1, 0)
        consume(i, 0)
        prepare(i + 1, 1)
        consume(i, 1)
    consume(IT - 1, 0)
    consume(IT - 1, 1)


def next_block(i, h):
    return (i, 1) if h == 0 else (i + 1, 0)


def with_next(engine, body):
    with engine.Fori(0, IT - 1) as i:
        body(i, 0, False)
        body(i, 1, False)
    body(IT - 1, 0, False)
    body(IT - 1, 1, True)


def gather_rows(pool, table, idx, idx_now, rows, w, slot_free, landed, idx_staged, begun):
    with pool.Fori(0, IT) as i:
        for h in range(2):
            pool.wait_ge(slot_free[h], i + 1)
            pool.tensor_copy(idx_now[:, h * BS:(h + 1) * BS], idx[:, bass.ds((2 * i + h) * BS, BS)]).then_inc(idx_staged, 1)
            pool.wait_ge(idx_staged, 2 * i + h + 1)
            pool.sem_inc(begun, 1)
            for u in range(BS):
                pool.indirect_dma_start(
                    out=rows[:, h, u, 0:w], out_offset=None, in_=table,
                    in_offset=bass.IndirectOffsetOnAxis(ap=idx_now[:, h * BS + u:h * BS + u + 1], axis=0),
                ).then_inc(landed[h], 16)



def node_stage_in(nc, io, g):
    with Stage(nc, "nin") as s:
        HB = BS // 2
        src, dst = s.sb("src", [P, COLS], I32), s.sb("dst", [P, COLS], I32)
        srcf, dstf = s.sb("srcf", [P, COLS]), s.sb("dstf", [P, COLS])
        HI_D, LO_D, HI_S, LO_S, MINUS_LO_S = range(5)
        NK = 5
        split = s.sb("split", [P, NB, NK, BS])
        now = s.sb("now", [P, 2, NK, BS])
        one = s.sb("one", [P, 2, HB, 2 * (P + COLS)], F16)
        away = s.sb("away", [P, 2, COLS], F16)
        BY_POOL = 5
        BY_ACT = 4
        iota_i, iota_f, iota_h = s.sb("iota_i", [P, COLS], I32), s.sb("iota_f", [P, COLS]), s.sb("iota_h", [P, COLS], F16)
        zero_h = s.sb("zero_h", [P, P + COLS], F16)
        diag, upper, ones = s.sb("diag", [P, P]), s.sb("upper", [P, P]), s.sb("ones", [P, P])
        zi = s.sb("zi", [P, COLS], I32)
        t = [s.sb(f"t{i}", [P, COLS]) for i in range(4)] + [s.sb("vec", [P, COLS])]
        row = s.sb("row", [P, COLS, W1ROW])
        zrow = s.sb("zrow", [1, D2])
        srcT = s.sb("srcT", [P, 4, P])
        ndeg_in, ndeg_out = s.ps("deg_in", [P, 512]), s.ps("deg_out", [P, 512])
        pcol, pT = s.ps("pcol", [P, 512]), s.ps("pT", [P, 4, P])

        loaded, consts, const_step, split_ready = s.sem("loaded"), s.sem("consts"), s.sem("const_step"), s.sem("split_ready")
        now_free, now_ready = s.sems("now_free"), s.sem("now_ready")
        one_free, one_ready, act_one_ready = s.sems("one_free"), s.sem("one_ready"), s.sem("act_one_ready")
        away_ready, iota_ready, hi_ready, hi_begun = (
            s.sem(n) for n in ("away_ready", "iota_ready", "hi_ready", "hi_begun"))
        counted = s.sem("counted")
        totals_ready, offsets_ready = s.sem("totals_ready"), s.sem("offsets_ready")
        deg_ready, root_ready = s.sem("deg_ready"), s.sem("root_ready")
        diag_ready, row_ready = s.sem("diag_ready"), s.sem("row_ready")
        turned_ready, srct_ready, stored, zero_ready = s.sem("turned_ready"), s.sem("srct_ready"), s.sem("stored"), s.sem("zero_ready")
        x_landed, ex_ready = s.sem("x_landed"), s.sem("ex_ready")
        block = s.ctx.enter_context(nc.Block())

        @block.sync
        def _(sp):
            sp.dma_start(dst[:, :], io.dst.rearrange("(p c) -> p c", p=P)).then_inc(loaded, 16)
            sp.dma_start(src[:, :], io.src.rearrange("(p c) -> p c", p=P)).then_inc(loaded, 16)
            sp.dma_start(zi[:, :], io.node_type.rearrange("(p c) -> p c", p=P)).then_inc(loaded, 16)
            sp.dma_start(t[4][:, :], io.node_vec.rearrange("(p c) -> p c", p=P)).then_inc(loaded, 16)
            sp.dma_start(row[:, :, 0:D], io.x.rearrange("(p c) w -> p c w", p=P)).then_inc(x_landed, 16)
            sp.wait_ge(zero_ready, 1)
            for table, w in g.sum_tables:
                sp.dma_start(table[ZROW:ZROW + 1, :], zrow[:, 0:w]).then_inc(stored, 16)
            sp.wait_ge(srct_ready, 1)
            for k in range(-(-COLS // P)):
                n = min(P, COLS - k * P)
                sp.dma_start(g.src_cols[k * P:k * P + n, :], srcT[0:n, k, :]).then_inc(stored, 16)
            sp.wait_ge(x_landed, 16)
            sp.wait_ge(ex_ready, 1)
            sp.dma_start(g.tab_in.rearrange("(p c) w -> p c w", p=P), row[:, :, :]).then_inc(stored, 16)
            sp.wait_ge(stored, 16 * (len(g.sum_tables) + -(-COLS // P) + 1))

        @block.gpsimd
        def _(pool):
            pool.memset(g.ident[:, :], 0.0).then_inc(const_step, 1)
            pool.memset(upper[:, :], 1.0).then_inc(const_step, 1)
            pool.memset(g.lower[:, :], 1.0).then_inc(const_step, 1)
            pool.memset(ones[:, :], 1.0)
            pool.iota(iota_i[:, :], pattern=[[1, COLS]], base=0, channel_multiplier=0)
            pool.wait_ge(const_step, 3)
            pool.affine_select(out=g.ident[:, :], in_=g.ident[:, :], compare_op=ALU.not_equal, fill=1.0,
                               base=0, pattern=[[-1, P]], channel_multiplier=1)
            pool.affine_select(out=upper[:, :], in_=upper[:, :], compare_op=ALU.is_gt, fill=0.0,
                               base=0, pattern=[[1, P]], channel_multiplier=-1)
            pool.affine_select(out=g.lower[:, :], in_=g.lower[:, :], compare_op=ALU.is_gt, fill=0.0,
                               base=0, pattern=[[-1, P]], channel_multiplier=1).then_inc(consts, 1)
            pool.wait_ge(iota_ready, 1)
            with pool.Fori(0, IT) as i:
                for h in range(2):
                    pool.wait_ge(now_ready, 2 * i + h + 1)
                    for half in range(2):
                        pool.wait_ge(one_free[half], 2 * i + h + 1)
                        pool.sem_inc(hi_begun, 1)
                        for cc in range(BY_POOL):
                            c = half * HB + cc
                            last = pool.tensor_scalar(one[:, half, cc, 0:P], iota_h[:, 0:P], now[:, h, HI_D, c:c + 1], None, ALU.is_equal)
                        last.then_inc(hi_ready, 1)
                    pool.wait_ge(hi_ready, (2 * i + h + 1) * 2)
                    pool.sem_inc(now_free[h], 1)

        @block.vector
        def _(dve):
            for q in now_free:
                dve.sem_inc(q, 1)
            dve.memset(row[:, :, EX + 5:W1ROW], 0.0)
            dve.memset(zrow[:, :], 0.0).then_inc(zero_ready, 1)
            dve.memset(zero_h[:, :], 0.0)
            dve.wait_ge(consts, 1)
            dve.tensor_copy(iota_f[:, :], iota_i[:, :])
            dve.tensor_copy(iota_h[:, :], iota_i[:, :])
            dve.drain()
            dve.tensor_copy(g.iota[:, :], iota_f[:, 0:P]).then_inc(iota_ready, 1)
            dve.wait_ge(loaded, 64)
            dve.tensor_copy(srcf[:, :], src[:, :])
            dve.tensor_copy(dstf[:, :], dst[:, :])
            dve.tensor_copy(g.src_idx[:, :], src[:, :])
            dve.tensor_copy(g.dst_idx[:, :], dst[:, :])
            dve.drain()
            for of, hi, lo in ((dstf, HI_D, LO_D), (srcf, HI_S, LO_S)):
                dve.tensor_scalar(t[0][:, :], of[:, :], 0.5, 1.0 / COLS, ALU.add, ALU.mult)
                dve.drain()
                dve.tensor_scalar(t[1][:, :], t[0][:, :], -0.5, ROUND, ALU.add, ALU.add)
                dve.drain()
                dve.tensor_scalar(t[0][:, :], t[1][:, :], -ROUND, None, ALU.add)
                dve.drain()
                dve.tensor_copy(split[:, :, hi, :], t[0][:, :].rearrange("p (b c) -> p b c", c=BS))
                dve.scalar_tensor_tensor(split[:, :, lo, :], t[0][:, :].rearrange("p (b c) -> p b c", c=BS), -float(COLS),
                                         of[:, :].rearrange("p (b c) -> p b c", c=BS), ALU.mult, ALU.add)
                dve.drain()
            dve.tensor_scalar(split[:, :, MINUS_LO_S, :], split[:, :, LO_S, :], -1.0, None, ALU.mult)
            dve.tensor_tensor(t[0][:, :], srcf[:, :], dstf[:, :], ALU.not_equal)
            dve.drain()
            by_block = t[0][:, :].rearrange("p (b c) -> p b c", c=BS)
            dve.scalar_tensor_tensor(split[:, :, HI_S, :], split[:, :, HI_S, :], 1.0, by_block, ALU.add, ALU.mult)
            dve.drain()
            dve.tensor_scalar(split[:, :, HI_S, :], split[:, :, HI_S, :], -1.0, None, ALU.add).then_inc(split_ready, 1)
            dve.memset(g.sc[:, :, :, :], 0.0)
            dve.drain()
            dve.tensor_copy(g.sc[:, :, EW, :], by_block)
            dve.drain()
            dve.memset(t[0][:, 0:1], 0.0)
            dve.tensor_tensor(t[0][:, 1:COLS], dstf[:, 1:COLS], dstf[:, 0:COLS - 1], ALU.is_equal)
            dve.tensor_scalar(t[1][:, :], dstf[:, :], dstf[:, 0:1], None, ALU.is_equal)
            dve.drain()
            dve.tensor_copy(g.sc[:, :, SAME, :], by_block)
            dve.tensor_copy(g.sc[:, :, FIRST, :], t[1][:, :].rearrange("p (b c) -> p b c", c=BS))
            dve.tensor_scalar(diag[:, :], g.ident[:, :], dstf[:, 0:1], None, ALU.mult).then_inc(diag_ready, 1)
            dve.wait_ge(row_ready, 1)
            dve.scalar_tensor_tensor(g.carries[:, :], pcol[:, 0:P], dstf[:, COLS - 1:COLS], upper[:, :],
                                     ALU.is_equal, ALU.mult)
            dve.wait_ge(turned_ready, 1)
            for k in range(-(-COLS // P)):
                n = min(P, COLS - k * P)
                last = dve.tensor_copy(srcT[0:n, k, :], pT[0:n, k, :])
            last.then_inc(srct_ready, 1)

            def one_hots(i, h, half):
                dve.wait_ge(one_free[half], 2 * i + h + 1)
                for cc in range(HB):
                    c = half * HB + cc
                    o = one[:, half, cc, :]
                    last = dve.tensor_scalar(o[:, P:P + COLS], iota_h[:, :], now[:, h, LO_D, c:c + 1], None, ALU.is_equal)
                    if cc >= BY_POOL:
                        dve.tensor_scalar(o[:, 0:P], iota_h[:, 0:P], now[:, h, HI_D, c:c + 1], None, ALU.is_equal)
                    last = dve.tensor_scalar(o[:, P + COLS:2 * P + COLS], iota_h[:, 0:P], now[:, h, HI_S, c:c + 1], None, ALU.is_equal)
                    if cc >= BY_ACT:
                        last = dve.tensor_scalar(o[:, 2 * P + COLS:], iota_h[:, :], now[:, h, LO_S, c:c + 1], None, ALU.is_equal)
                last.then_inc(one_ready, 1)

            with dve.Fori(0, IT) as i:
                for h in range(2):
                    n = 2 * i + h + 1
                    dve.wait_ge(now_ready, n)
                    one_hots(i, h, 0)
                    one_hots(i, h, 1)
                    dve.drain()
                    dve.sem_inc(now_free[h], 1)

            dve.wait_ge(counted, 1)
            deg_in, has, last_edge, first, tmp = (q[:, :] for q in t)
            dve.tensor_copy(row[:, :, EX + 4], tmp)
            dve.tensor_copy(row[:, :, EX + 3], zi[:, :])
            dve.tensor_copy(deg_in, ndeg_in[:, 0:COLS])
            dve.tensor_copy(first, ndeg_out[:, 0:COLS])
            dve.drain()
            dve.tensor_scalar(iota_f[:, :], deg_in, 1.0, None, ALU.max)
            dve.tensor_scalar(tmp, first, 1.0, None, ALU.max).then_inc(deg_ready, 1)
            dve.wait_ge(root_ready, 1)
            dve.reciprocal(dstf[:, :], dstf[:, :])
            dve.reciprocal(srcf[:, :], srcf[:, :])
            dve.tensor_scalar(has, deg_in, 0.0, None, ALU.is_gt)
            dve.tensor_scalar(first, first, 0.0, None, ALU.is_gt)
            dve.drain()
            dve.tensor_tensor(row[:, :, EX + 0], srcf[:, :], first, ALU.mult)
            dve.tensor_tensor(row[:, :, EX + 1], dstf[:, :], has, ALU.mult)
            dve.memset(iota_f[:, :], 1.0)
            dve.drain()
            dve.tensor_tensor_scan(last_edge, iota_f[:, :], deg_in, 0.0, ALU.mult, ALU.add)
            dve.drain()
            dve.tensor_copy(diag[:, 0:1], last_edge[:, COLS - 1:COLS]).then_inc(totals_ready, 1)
            dve.wait_ge(offsets_ready, 1)
            dve.tensor_copy(diag[:, 1:2], pcol[:, P:P + 1])
            dve.drain()
            dve.tensor_scalar(last_edge, last_edge, diag[:, 1:2], -1.0, ALU.add, ALU.add)
            dve.drain()
            dve.scalar_tensor_tensor(deg_in, deg_in, -1.0, last_edge, ALU.mult, ALU.add)
            dve.tensor_scalar(tmp, last_edge, 0.5, 1.0 / COLS, ALU.add, ALU.mult)
            dve.drain()
            dve.tensor_scalar(first, tmp, -0.5, ROUND, ALU.add, ALU.add)
            dve.drain()
            dve.tensor_scalar(tmp, first, -ROUND, None, ALU.add)
            dve.drain()
            dve.scalar_tensor_tensor(first, tmp, float(COLS), deg_in, ALU.mult, ALU.is_gt)
            dve.tensor_scalar(tmp, tmp, float(NPAD), None, ALU.add)
            dve.drain()
            dve.tensor_tensor(tmp, tmp, last_edge, ALU.subtract)
            dve.drain()
            dve.tensor_tensor(tmp, tmp, first, ALU.mult)
            dve.drain()
            dve.tensor_tensor(last_edge, last_edge, tmp, ALU.add)
            dve.drain()
            dve.scalar_tensor_tensor(last_edge, last_edge, -float(ZROW), has, ALU.add, ALU.mult)
            dve.drain()
            dve.tensor_scalar(row[:, :, EX + 2], last_edge, float(ZROW), None, ALU.add)
            dve.drain()
            dve.sem_inc(ex_ready, 1)
            dve.tensor_copy(g.last_node[:, :], row[:, :, EX + 2])

        @block.scalar
        def _(act):
            act.wait_ge(split_ready, 1)
            act.wait_ge(iota_ready, 1)
            act.sem_inc(act_one_ready, 2)
            flat = split[:, :, :, :].rearrange("p b k c -> p (b k c)")

            def prepare(i, h):
                act.wait_ge(now_free[h], 3 * i + 1)
                nc.scalar.copy(now[:, h, :, :].rearrange("p k c -> p (k c)"),
                               flat[:, bass.ds((2 * i + h) * (NK * BS), NK * BS)]).then_inc(now_ready, 1)

            def one_hots(i, h, half):
                n = 2 * i + h + 1
                act.wait_ge(now_ready, n)
                act.wait_ge(one_free[half], n)
                for cc in range(BY_ACT):
                    c = half * HB + cc
                    k = (n - 1) * (2 * BY_ACT) + half * BY_ACT + cc
                    act.wait_ge(act_one_ready, k + 1)
                    nc.scalar.activation(away[:, (half * BY_ACT + cc) % 2, :], iota_h[:, :], ACT.Abs, bias=now[:, h, MINUS_LO_S, c:c + 1]
                                         ).then_inc(away_ready, 1)
                    act.wait_ge(away_ready, k + 1)
                    nc.scalar.activation(one[:, half, cc, 2 * P + COLS:], away[:, (half * BY_ACT + cc) % 2, :], ACT.Relu,
                                         bias=1.0, scale=-1.0).then_inc(act_one_ready, 1)

            def consume(i, h):
                n = 2 * i + h + 1
                one_hots(i, h, 0)
                one_hots(i, h, 1)
                act.wait_ge(act_one_ready, 2 * n * BY_ACT + 2)
                act.sem_inc(now_free[h], 1)

            skewed(act, prepare, consume)
            act.wait_ge(deg_ready, 1)
            nc.scalar.activation(dstf[:, :], iota_f[:, :], ACT.Sqrt)
            nc.scalar.activation(srcf[:, :], t[4][:, :], ACT.Sqrt).then_inc(root_ready, 1)

        @block.tensor
        def _(pe):
            pe.sem_inc(one_free[0], 1)
            pe.sem_inc(one_free[1], 1)
            pe.wait_ge(diag_ready, 1)
            pe.matmul(pcol[:, 0:P], ones[:, :], diag[:, :], start=True, stop=True).then_inc(row_ready, 1)
            for k in range(-(-COLS // P)):
                n = min(P, COLS - k * P)
                last = pe.transpose(pT[0:n, k, :], srcf[:, k * P:k * P + n], g.ident[:, :])
            last.then_inc(turned_ready, 1)
            for acc in (ndeg_in, ndeg_out):
                pe.matmul(acc[:, 0:COLS], zero_h[:, 0:P], zero_h[:, P:], start=True, stop=False, skip_group_check=True)
            with pe.Fori(0, IT) as i:
                for h in range(2):
                    for half in range(2):
                        n = (2 * i + h) * 2 + half + 1
                        pe.wait_ge(one_ready, n)
                        pe.wait_ge(act_one_ready, n * BY_ACT + 2)
                        pe.wait_ge(hi_ready, n)
                        for c in range(HB):
                            o = one[:, half, c, :]
                            pe.matmul(ndeg_in[:, 0:COLS], o[:, 0:P], o[:, P:P + COLS], start=False, stop=False,
                                      skip_group_check=True)
                            last = pe.matmul(ndeg_out[:, 0:COLS], o[:, P + COLS:2 * P + COLS], o[:, 2 * P + COLS:],
                                             start=False, stop=False, skip_group_check=True)
                        last.then_inc(one_free[half], 1)
            for acc in (ndeg_in, ndeg_out):
                last = pe.matmul(acc[:, 0:COLS], zero_h[:, 0:P], zero_h[:, P:], start=False, stop=True, skip_group_check=True)
            last.then_inc(counted, 1)
            pe.wait_ge(totals_ready, 1)
            pe.matmul(pcol[:, P:P + 1], upper[:, :], diag[:, 0:1], start=True, stop=True).then_inc(offsets_ready, 1)



def weight_stage(nc, io, g):
    with Stage(nc, "wts") as s:
        raw = [s.sb(f"raw{k}", [D2, D2]) for k in range(4)]
        lap, mf, coef = s.sb("lap", [P, K1 + 1]), s.sb("mf", [P, K1 + 1]), s.sb("coef", [P, K1 + 3])
        embT, adT, cmat = s.sb("embT", [EMB, NZ]), s.sb("adT", [EMB, EMB]), s.sb("cmat", [EMB, NZ])
        pm = s.ps("pm", [P, 512])
        zeroed, loaded, tanhed = s.sem("zeroed"), s.sem("loaded"), s.sem("tanhed")
        c_ready, c_copied, m_ready = s.sem("c_ready"), s.sem("c_copied"), s.sem("m_ready")
        bd = [(raw[k], io.w0[k], D) for k in range(4)] + [
            (g.w_rel1, io.w_rel1, D), (g.w_root1, io.w_root1, D), (g.w_rel2, io.w_rel2, D), (g.w_root2, io.w_root2, D),
            (g.W1, io.W1.rearrange("h r -> r h"), R), (g.W2, io.W2.rearrange("h k -> k h"), D)]
        n_dma = 2 * len(bd) + 14
        block = s.ctx.enter_context(nc.Block())

        @block.sync
        def _(sp):
            sp.wait_ge(zeroed, 1)
            with nc.allow_non_contiguous_dma(reason="small transposed weights, once"):
                for to, of, k in bd:
                    for half in range(2):
                        sp.dma_start(to[half * k:(half + 1) * k, half * D:(half + 1) * D], of).then_inc(loaded, 16)
                for to, of in ((g.gamma, io.gamma), (g.beta, io.beta),
                               (g.b_l1, io.b_l1), (g.b_l2, io.b_l2)):
                    sp.dma_start(to[:, :], of.partition_broadcast(P)).then_inc(loaded, 16)
                sp.dma_start(lap[:, :], io.lap.partition_broadcast(P)).then_inc(loaded, 16)
                sp.dma_start(mf[:, :], io.mf.rearrange("a k b -> (a k b)").partition_broadcast(P)).then_inc(loaded, 16)
                sp.dma_start(embT[:, :], io.emb.rearrange("z g -> g z")).then_inc(loaded, 16)
                sp.dma_start(adT[:, :], io.adaptW.rearrange("g k -> k g")).then_inc(loaded, 16)
                for half in range(2):
                    sp.dma_start(g.wh[D2:D2 + 1, half * D:(half + 1) * D], io.bias0.unsqueeze(0)).then_inc(loaded, 16)
                    sp.dma_start(g.W2[D2:D2 + 1, half * D:(half + 1) * D], io.b2.unsqueeze(0)).then_inc(loaded, 16)
                    sp.dma_start(g.b1[half * D:(half + 1) * D, :], io.b1.unsqueeze(1)).then_inc(loaded, 16)
            sp.wait_ge(loaded, 16 * n_dma)

        @block.vector
        def _(dve):
            for k, (to, _, _) in enumerate(bd):
                last = dve.memset(to[:, :], 0.0)
            last.then_inc(zeroed, 1)
            dve.wait_ge(loaded, 16 * n_dma)
            dve.tensor_tensor(g.wh[0:D2, :], raw[0][:, :], raw[2][:, :], ALU.subtract)
            dve.tensor_tensor(g.wu[0][:, :], raw[1][:, :], raw[3][:, :], ALU.subtract)
            dve.tensor_scalar(g.wu[1][:, :], raw[2][:, :], 2.0, None, ALU.mult)
            dve.tensor_scalar(g.wu[2][:, :], raw[3][:, :], 2.0, None, ALU.mult)
            dve.wait_ge(tanhed, 1)
            for k in range(1, K1):
                dve.tensor_tensor(lap[:, k:k + 1], lap[:, k:k + 1], lap[:, k - 1:k], ALU.mult)
                dve.drain()
            dve.memset(coef[:, :], 0.0)
            dve.drain()
            dve.tensor_copy(coef[:, 0:1], mf[:, 0:1])
            dve.tensor_tensor(coef[:, 1:K1 + 1], mf[:, 1:K1 + 1], lap[:, 0:K1], ALU.mult)
            dve.drain()
            for k, norm in enumerate(jacobi_norms()):
                dve.tensor_scalar(coef[:, k:k + 1], coef[:, k:k + 1], 1.0 / norm, None, ALU.mult)
            dve.drain()
            for k in range(K1 - 2, -1, -1):
                dve.scalar_tensor_tensor(coef[:, k:k + 1], coef[:, k + 2:k + 3], jacobi(k + 2)[1], coef[:, k:k + 1],
                                         ALU.mult, ALU.add)
                dve.drain()
            dve.tensor_copy(g.p0w[:, :], coef[:, 0:1])
            for k in range(K1):
                dve.memset(g.betas[:, k:k + 1], BETA[k])
            for k in range(K1):
                dve.tensor_scalar(g.omega[:, k:k + 1], coef[:, k + 1:k + 2], SCALE[k + 1], None, ALU.mult)
            dve.wait_ge(c_ready, 1)
            dve.tensor_copy(cmat[:, :], pm[0:EMB, 0:NZ]).then_inc(c_copied, 1)
            dve.wait_ge(m_ready, 1)
            dve.tensor_copy(g.pair_term[:, :], pm[0:NZ, P:P + NZ])

        @block.scalar
        def _(act):
            act.wait_ge(loaded, 16 * n_dma)
            nc.scalar.activation(lap[:, :], lap[:, :], ACT.Tanh).then_inc(tanhed, 1)

        @block.tensor
        def _(pe):
            pe.wait_ge(loaded, 16 * n_dma)
            pe.matmul(pm[0:EMB, 0:NZ], adT[:, :], embT[:, :], start=True, stop=True).then_inc(c_ready, 1)
            pe.wait_ge(c_copied, 1)
            pe.matmul(pm[0:NZ, P:P + NZ], embT[:, :], cmat[:, :], start=True, stop=True).then_inc(m_ready, 1)



def layernorm_apart(dve, x, xc, out, st, sq, xc_ready, sq_ready, var_ready, std_ready, count, relu=True):
    centre(dve, x, xc, st).then_inc(xc_ready, 1)
    dve.wait_ge(sq_ready, count)
    variance(dve, sq, st).then_inc(var_ready, 1)
    dve.wait_ge(std_ready, count)
    return normalised(dve, xc, out, st, relu)


def take_squares(act, nc, xc, sq, xc_ready, sq_ready, count):
    act.wait_ge(xc_ready, count)
    nc.scalar.activation(sq, xc, ACT.Square).then_inc(sq_ready, 1)


def node_stage_mid(nc, io, g):
    with Stage(nc, "mid") as s:
        rows, idx_now = s.sb("rows", [P, 2, BS, D2]), s.sb("idx_now", [P, 2 * BS], I32)
        own = s.sb("own", [P, 2, BS, W1ROW])
        x1, xc, h1, sq, st = s.sb("x1", [P, BS, D]), s.sb("xc", [P, BS, D]), s.sb("h1", [P, BS, D]), s.sb("sq", [P, BS, D]), s.sb("st", [P, 5, BS])
        a0 = s.sb("a0", [P, 2, BS, D])
        x2, h2 = s.sb("x2", [P, 2, BS, D]), s.sb("h2", [P, 2, BS, H2ROW])
        slot_free, landed, idx_staged, begun = s.sems("slot_free"), s.sems("landed"), s.sem("idx_staged"), s.sem("begun")
        own_landed, own_free = s.sems("own_landed"), s.sems("own_free")
        out_ready, out_free, out_stored = s.sems("out_ready"), s.sems("out_free"), s.sems("out_stored")
        xc_ready, sq_ready, var_ready, std_ready = s.sem("xc_ready"), s.sem("sq_ready"), s.sem("var_ready"), s.sem("std_ready")
        block = s.ctx.enter_context(nc.Block())

        @block.gpsimd
        def _(pool):
            gather_rows(pool, g.tab_both, g.last_node, idx_now, rows, D2, slot_free, landed, idx_staged, begun)

        @block.scalar
        def _(act):
            with act.Fori(0, IT) as i:
                for h in range(2):
                    for n in (4 * i + 2 * h + 1, 4 * i + 2 * h + 2):
                        take_squares(act, nc, xc[:, :, :], sq[:, :, :], xc_ready, sq_ready, n)
                        take_std(act, nc, st, var_ready, std_ready, n)

        @block.sync
        def _(sp):
            def prepare(i, h):
                sp.wait_ge(own_free[h], i + 1)
                sp.dma_start(own[:, h, :, :], block_of(g.tab_own, i, h, W1ROW)).then_inc(own_landed[h], 16)

            def consume(i, h):
                sp.wait_ge(out_ready[h], i + 1)
                sp.dma_start(block_of(g.x2, i, h, D), x2[:, h, :, :]).then_inc(out_stored[h], 16)
                sp.dma_start(block_of(g.tab_h2, i, h, H2ROW), h2[:, h, :, :]).then_inc(out_stored[h], 16)
                sp.wait_ge(out_stored[h], (i + 1) * 32)
                sp.sem_inc(out_free[h], 1)

            sp.sem_inc(out_free[0], 1)
            sp.sem_inc(out_free[1], 1)
            skewed_by_two(sp, prepare, consume)

        @block.vector
        def _(dve):
            dve.memset(h2[:, :, :, D + 2:H2ROW], 0.0)
            for q in slot_free + own_free:
                dve.sem_inc(q, 1)

            def scaled(i, h):
                dve.wait_ge(landed[h], (i + 1) * (16 * BS))
                dve.wait_ge(own_landed[h], (i + 1) * 16)
                scal = own[:, h, :, EX:EX + 5]
                dve.scalar_tensor_tensor(a0[:, h, :, :], rows[:, h, :, 0:D], -1.0, over_features(scal[:, :, 0]), ALU.mult, ALU.mult)
                dve.wait_ge(out_free[h], i + 1)
                dve.tensor_tensor(x2[:, h, :, :], rows[:, h, :, D:D2], over_features(scal[:, :, 1]), ALU.mult)
                dve.tensor_copy(h2[:, h, :, D:D + 2], scal[:, :, 3:5])
                dve.drain()
                dve.sem_inc(slot_free[h], 1)

            def body(i, h, last):
                n = 2 * i + h + 1
                dve.tensor_tensor(x1[:, :, :], a0[:, h, :, :], own[:, h, :, 0:D], ALU.add)
                dve.drain()
                dve.sem_inc(own_free[h], 1)
                layernorm_apart(dve, x1[:, :, :], xc[:, :, :], h1[:, :, :], st, sq[:, :, :], xc_ready, sq_ready,
                                var_ready, std_ready, 2 * n - 1)
                dve.tensor_tensor(x1[:, :, :], x1[:, :, :], x2[:, h, :, :], ALU.add)
                dve.drain()
                dve.scalar_tensor_tensor(x2[:, h, :, :], h1[:, :, :], g.p0w[:, 0:1], x1[:, :, :], ALU.mult, ALU.add)
                dve.drain()
                centre(dve, x2[:, h, :, :], xc[:, :, :], st).then_inc(xc_ready, 1)
                if not last:
                    scaled(*next_block(i, h))
                dve.wait_ge(sq_ready, 2 * n)
                variance(dve, sq[:, :, :], st).then_inc(var_ready, 1)
                dve.wait_ge(std_ready, 2 * n)
                normalised(dve, xc[:, :, :], h2[:, h, :, 0:D], st)
                dve.drain()
                dve.sem_inc(out_ready[h], 1)

            scaled(0, 0)
            with_next(dve, body)


def node_stage_late(nc, io, g):
    with Stage(nc, "late") as s:
        x2, h2, agg = s.sb("x2", [P, 2, BS, D]), s.sb("h2", [P, 2, BS, H2ROW]), s.sb("agg", [P, 2, NAGG, BS, H2ROW])
        total, x2b = s.sb("total", [P, 2, BS, H2ROW]), s.sb("x2b", [P, 2, BS, D])
        y, xc, sq, st = s.sb("y", [P, BS, D]), s.sb("xc", [P, BS, D]), s.sb("sq", [P, BS, D]), s.sb("st", [P, 5, BS])
        x3 = s.sb("x3", [P, 2, BS, D])
        agg_landed, agg_free, h2_landed, h2_free = s.sems("agg_landed"), s.sems("agg_free"), s.sems("h2_landed"), s.sems("h2_free")
        total_ready, total_free, half_ready = s.sem("total_ready"), s.sems("total_free"), s.sem("half_ready")
        out_ready, out_free, out_stored = s.sems("out_ready"), s.sems("out_free"), s.sems("out_stored")
        xc_ready, sq_ready, var_ready, std_ready = s.sem("xc_ready"), s.sem("sq_ready"), s.sem("var_ready"), s.sem("std_ready")
        block = s.ctx.enter_context(nc.Block())

        @block.sync
        def _(sp):
            with sp.Fori(0, IT) as i:
                for h in range(2):
                    sp.wait_ge(agg_free[h], i + 1)
                    for q in range(NAGG):
                        sp.dma_start(agg[:, h, q, :, :], block_of(g.agg[q], i, h, H2ROW)).then_inc(agg_landed[h], 16)
                    sp.dma_start(x2[:, h, :, :], block_of(g.x2, i, h, D)).then_inc(agg_landed[h], 16)
                    sp.wait_ge(h2_free[h], i + 1)
                    sp.dma_start(h2[:, h, :, :], block_of(g.tab_h2, i, h, H2ROW)).then_inc(h2_landed[h], 16)

        @block.tensor
        def _(pe):
            pe.sem_inc(out_free[0], 1)
            pe.sem_inc(out_free[1], 1)
            with pe.Fori(0, IT) as i:
                for h in range(2):
                    pe.wait_ge(out_stored[h], (i + 1) * 16)
                    pe.sem_inc(out_free[h], 1)

        @block.gpsimd
        def _(pool):
            pool.sem_inc(agg_free[0], 1)
            pool.sem_inc(agg_free[1], 1)
            with pool.Fori(0, IT) as i:
                for h in range(2):
                    pool.wait_ge(agg_landed[h], (i + 1) * (16 * (NAGG + 1)))
                    pool.tensor_tensor(agg[:, h, 0, :, :], agg[:, h, 0, :, :], agg[:, h, 1, :, :], ALU.add)
                    pool.tensor_tensor(agg[:, h, 2, :, :], agg[:, h, 2, :, :], agg[:, h, 3, :, :], ALU.add).then_inc(half_ready, 1)
                    pool.wait_ge(total_free[h], i + 1)
                    pool.wait_ge(half_ready, 2 * i + h + 1)
                    pool.tensor_tensor(x2b[:, h, :, :], x2[:, h, :, :], over_columns(g.beta[:, :]), ALU.add)
                    pool.tensor_tensor(total[:, h, :, :], agg[:, h, 0, :, :], agg[:, h, 2, :, :], ALU.add).then_inc(total_ready, 1)
                    pool.wait_ge(total_ready, 2 * i + h + 1)
                    pool.sem_inc(agg_free[h], 1)

        @block.scalar
        def _(act):
            with act.Fori(0, IT) as i:
                for h in range(2):
                    take_squares(act, nc, xc[:, :, :], sq[:, :, :], xc_ready, sq_ready, 2 * i + h + 1)
                    take_std(act, nc, st, var_ready, std_ready, 2 * i + h + 1)
                    act.wait_ge(out_ready[h], i + 1)
                    act.dma_start(block_of(g.x3, i, h, D), x3[:, h, :, :]).then_inc(out_stored[h], 16)

        @block.vector
        def _(dve):
            for q in h2_free + total_free:
                dve.sem_inc(q, 1)
            with dve.Fori(0, IT) as i:
                for h in range(2):
                    n = 2 * i + h + 1
                    a = total[:, h, :, :]
                    dve.wait_ge(total_ready, n)
                    dve.wait_ge(h2_landed[h], (i + 1) * 16)
                    dve.tensor_scalar(st[:, 0, :], a[:, :, D], 1e-8, None, ALU.max)
                    dve.drain()
                    dve.reciprocal(st[:, 1, :], st[:, 0, :])
                    dve.drain()
                    dve.tensor_tensor(y[:, :, :], a[:, :, 0:D], over_features(st[:, 1, :]), ALU.mult)
                    dve.drain()
                    dve.tensor_tensor(y[:, :, :], y[:, :, :], h2[:, h, :, 0:D], ALU.add)
                    dve.drain()
                    dve.sem_inc(h2_free[h], 1)
                    layernorm_apart(dve, y[:, :, :], xc[:, :, :], xc[:, :, :], st, sq[:, :, :], xc_ready, sq_ready,
                                    var_ready, std_ready, n, relu=False)
                    dve.drain()
                    dve.tensor_tensor(xc[:, :, :], xc[:, :, :], over_columns(g.gamma[:, :]), ALU.mult)
                    dve.drain()
                    dve.wait_ge(out_free[h], i + 1)
                    dve.tensor_tensor(x3[:, h, :, :], xc[:, :, :], x2b[:, h, :, :], ALU.add).then_inc(out_ready[h], 1)
                    dve.drain()
                    dve.sem_inc(total_free[h], 1)


def node_stage_out(nc, io, g):
    with Stage(nc, "out") as s:
        rows, idx_now = s.sb("rows", [P, 2, BS, D2]), s.sb("idx_now", [P, 2 * BS], I32)
        x3, xc, sq, st = s.sb("x3", [P, 2, BS, D]), s.sb("xc", [P, BS, D]), s.sb("sq", [P, BS, D]), s.sb("st", [P, 5, BS])
        h3, h3T = s.sb("h3", [P, BS, D]), s.sb("h3T", [P, NPAIR * P])
        a3, h4 = s.sb("a3", [P, BS, D]), s.sb("h4", [P, BS, D])
        aT, hT = s.sb("aT", [P, NPAIR * P]), s.sb("hT", [P, NPAIR * P])
        res = s.sb("res", [P, 2, BS, D])
        ta, tb, mq, mm = s.ps("ta", [P, 2, 512]), s.ps("tb", [P, 2, 512]), s.ps("mq", [P, 2, 512]), s.ps("mm", [P, 2, 512])
        slot_free, landed, idx_staged, begun = s.sems("slot_free"), s.sems("landed"), s.sem("idx_staged"), s.sem("begun")
        x3_landed, x3_free = s.sems("x3_landed"), s.sems("x3_free")
        xc_ready, sq_ready, var_ready, std_ready = s.sem("xc_ready"), s.sem("sq_ready"), s.sem("var_ready"), s.sem("std_ready")
        h3_ready, h3_turned, h3_copied, mq_ready, mq_read = (
            s.sem(n) for n in ("h3_ready", "h3_turned", "h3_copied", "mq_ready", "mq_read"))
        a3_ready, a3_turned, h4_ready, h4_turned, both_copied, mm_ready = (
            s.sem(n) for n in ("a3_ready", "a3_turned", "h4_ready", "h4_turned", "both_copied", "mm_ready"))
        out_ready, out_free, out_stored = s.sems("out_ready"), s.sems("out_free"), s.sems("out_stored")
        block = s.ctx.enter_context(nc.Block())

        @block.gpsimd
        def _(pool):
            gather_rows(pool, g.tab_both2, g.last_node, idx_now, rows, D2, slot_free, landed, idx_staged, begun)

        @block.sync
        def _(sp):
            def prepare(i, h):
                sp.wait_ge(x3_free[h], i + 1)
                sp.dma_start(x3[:, h, :, :], block_of(g.x3, i, h, D)).then_inc(x3_landed[h], 16)

            def consume(i, h):
                sp.wait_ge(out_ready[h], i + 1)
                sp.dma_start(block_of(io.out, i, h, D), res[:, h, :, :]).then_inc(out_stored[h], 16)
                sp.wait_ge(out_stored[h], (i + 1) * 16)
                sp.sem_inc(out_free[h], 1)

            sp.sem_inc(out_free[0], 1)
            sp.sem_inc(out_free[1], 1)
            skewed_by_two(sp, prepare, consume)

        @block.scalar
        def _(act):
            def own_turned(i, h):
                act.wait_ge(h3_turned, 2 * i + h + 1)
                copy_turned(nc, h3T, ta).then_inc(h3_copied, 1)

            def body(i, h, last):
                n = 2 * i + h + 1
                act.wait_ge(landed[h], (i + 1) * (16 * BS))
                nc.scalar.copy(a3[:, :, :], rows[:, h, :, D:D2]).then_inc(a3_ready, 1)
                act.wait_ge(a3_turned, n)
                copy_turned(nc, aT, ta)
                if not last:
                    take_squares(act, nc, xc[:, :, :], sq[:, :, :], xc_ready, sq_ready, n + 1)
                act.wait_ge(h4_turned, n)
                copy_turned(nc, hT, tb).then_inc(both_copied, 1)
                if not last:
                    take_std(act, nc, st, var_ready, std_ready, n + 1)
                    own_turned(*next_block(i, h))

            take_squares(act, nc, xc[:, :, :], sq[:, :, :], xc_ready, sq_ready, 1)
            take_std(act, nc, st, var_ready, std_ready, 1)
            own_turned(0, 0)
            with_next(act, body)

        @block.tensor
        def _(pe):
            def own(i, h):
                n = 2 * i + h + 1
                pe.wait_ge(h3_ready, n)
                transpose_pairs(pe, ta, h3, g.ident[:, :]).then_inc(h3_turned, 1)
                pe.wait_ge(h3_copied, n)
                pe.wait_ge(mq_read, n)
                multiply_pairs(pe, mq, [(h3T, g.w_root1[:, :], D2)]).then_inc(mq_ready, 1)

            def body(i, h, last):
                n = 2 * i + h + 1
                pe.wait_ge(a3_ready, n)
                transpose_pairs(pe, ta, a3, g.ident[:, :]).then_inc(a3_turned, 1)
                pe.wait_ge(h4_ready, n)
                transpose_pairs(pe, tb, h4, g.ident[:, :]).then_inc(h4_turned, 1)
                pe.wait_ge(both_copied, n)
                multiply_pairs(pe, mm, [(aT, g.w_rel2[:, :], D2), (hT, g.w_root2[:, :], D2)]).then_inc(mm_ready, 1)
                if not last:
                    own(*next_block(i, h))

            own(0, 0)
            with_next(pe, body)

        @block.vector
        def _(dve):
            def own(i, h):
                n = 2 * i + h + 1
                dve.wait_ge(x3_landed[h], (i + 1) * 16)
                layernorm_apart(dve, x3[:, h, :, :], xc[:, :, :], h3[:, :, :], st, sq[:, :, :], xc_ready, sq_ready,
                                var_ready, std_ready, n).then_inc(h3_ready, 1)

            def body(i, h, last):
                n = 2 * i + h + 1
                dve.wait_ge(landed[h], (i + 1) * (16 * BS))
                dve.tensor_tensor(h4[:, :, :], rows[:, h, :, 0:D], over_columns(g.b_l1[:, :]), ALU.add)
                dve.drain()
                dve.wait_ge(mq_ready, n)
                for c, piece in products(mq):
                    dve.tensor_tensor(h4[:, c, :], h4[:, c, :], piece, ALU.add)
                dve.drain()
                dve.sem_inc(mq_read, 1)
                dve.tensor_scalar(h4[:, :, :], h4[:, :, :], 0.0, None, ALU.max).then_inc(h4_ready, 1)
                dve.wait_ge(a3_ready, n)
                dve.sem_inc(slot_free[h], 1)
                if not last:
                    own(*next_block(i, h))
                dve.wait_ge(out_free[h], i + 1)
                dve.tensor_tensor(res[:, h, :, :], x3[:, h, :, :], over_columns(g.b_l2[:, :]), ALU.add)
                dve.drain()
                dve.sem_inc(x3_free[h], 1)
                dve.wait_ge(mm_ready, n)
                for c, piece in products(mm):
                    last_add = dve.tensor_tensor(res[:, h, c, :], res[:, h, c, :], piece, ALU.add)
                last_add.then_inc(out_ready[h], 1)
                dve.drain()

            for q in slot_free + x3_free + [mq_read]:
                dve.sem_inc(q, 1)
            own(0, 0)
            with_next(dve, body)



def propagate(nc, g, name, kind, table, w, idx, to, u_old=None, u_new=None, k=None, acc_in=None, acc_out=None,
              r_out=None, own=None, merge=None, zero=None):
    wide = D2 if merge is not None else D
    cheb = kind in ("cheb_first", "cheb", "cheb_last")
    conv = kind == "conv_first"
    product_of = cheb or conv
    early = kind in ("cheb_first", "conv_first")
    normed = early or kind == "jacobi_first" or own is not None
    by_feature = kind in ("jacobi", "jacobi_last")
    with Stage(nc, name) as s:
        rows, idx_now = s.sb("rows", [P, 2, BS, w]), s.sb("idx_now", [P, 2 * BS], I32)
        sc = s.sb("sc", [P, 2, NSC * BS])
        same = s.sb("same", [P, 2, D, BS + 1], F16)
        val, run = s.sb("val", [P, D, BS + 1]), s.sb("run", [P, D, BS + 1])
        tmp = s.sb("tmp", [P, D, BS])
        sums = s.sb("sums", [P, 2, BS, wide])
        fix, part, fixed = s.sb("fix", [P, D]), s.sb("part", [P, D]), s.sb("fixed", [P, wide])
        pfix = s.ps("pfix", [P, 512])
        has_acc = acc_in is not None or acc_out is not None
        acc = s.sb("acc", [P, 2, BS, D]) if has_acc else None
        res = s.sb("res", [P, 2, BS, D]) if r_out is not None else None
        slot_free, landed, idx_staged, begun = s.sems("slot_free"), s.sems("landed"), s.sem("idx_staged"), s.sem("begun")
        sc_free, sc_ready = s.sems("sc_free"), s.sem("sc_ready")
        in_landed = s.sems("in_landed")
        val_ready, val_read, run_ready, run_read = s.sem("val_ready"), s.sem("val_read"), s.sem("run_ready"), s.sem("run_read")
        sums_ready, side_ready, out_free, out_stored = s.sems("sums_ready"), s.sems("side_ready"), s.sems("out_free"), s.sems("out_stored")
        fix_ready, fix_done, fix_copied, fix_stored, old_fix = (
            s.sem("fix_ready"), s.sem("fix_done"), s.sem("fix_copied"), s.sem("fix_stored"), s.sem("old_fix"))
        if normed:
            sq, st = s.sb("sq", [P, BS, D]), s.sb("st", [P, 5, BS])
            var_ready, std_ready = s.sem("var_ready"), s.sem("std_ready")
        if kind == "jacobi_first":
            x1 = s.sb("x1", [P, BS, D])
        if kind in ("jacobi", "jacobi_last"):
            beta, omega = s.sb("beta", [P, 1]), s.sb("omega", [P, 1])
        if product_of:
            left, leftT = s.sb("left", [P, 1 + early, BS, D]), s.sb("leftT", [P, NPAIR * P])
            tp, mm, mm2 = s.ps("tp", [P, 2, 512]), s.ps("mm", [P, 2, 512]), s.ps("mm2", [P, 2, 512])
            left_ready, left_turned, left_copied, mm_ready, mm_read = (
                s.sem(n) for n in ("left_ready", "left_turned", "left_copied", "mm_ready", "mm_read"))
            wu = {"cheb_first": g.wu[0], "cheb": g.wu[1], "cheb_last": g.wu[2], "conv_first": g.w_rel1}[kind]
            wh = {"cheb_first": g.wh, "conv_first": g.w_root1}.get(kind)
        if kind == "cheb_first":
            t1, ex = s.sb("t1", [P, 2, BS]), s.sb("ex", [P, 2, BS, 5])
        if own is not None:
            nodes, own_h, own_hT, own_row = (s.sb("nodes", [P, 2, BS, W1ROW]), s.sb("own_h", [P, BS, D]),
                                             s.sb("own_hT", [P, NPAIR * P]), s.sb("own_row", [P, 2, BS, W1ROW]))
            xc, xc_ready, sq_ready = s.sb("xc", [P, BS, D]), s.sem("xc_ready"), s.sem("sq_ready")
            own_landed, own_ready, own_turned, own_copied, own_mm_ready, own_read, own_row_ready = (
                s.sems("own_landed"), s.sem("own_ready"), s.sem("own_turned"), s.sem("own_copied"), s.sem("own_mm_ready"),
                s.sem("own_read"), s.sems("own_row_ready"))
        n_in = (acc_in is not None) + (merge is not None)
        has_side = acc_out is not None or r_out is not None
        n_out = 1 + (acc_out is not None) + (r_out is not None) + (own is not None)

        def staged(h, which):
            return sc[:, h, which * BS:(which + 1) * BS]

        def rows_of(x):
            return x.rearrange("p f c -> p c f")

        def u_block(u, i, h):
            return u[:, bass.ds((2 * i + h) * (D * BS), D * BS)].rearrange("p (f c) -> p f c", c=BS)

        v = val[:, :, 1:BS + 1]
        block = s.ctx.enter_context(nc.Block())

        @block.gpsimd
        def _(pool):
            gather_rows(pool, table, idx, idx_now, rows, w, slot_free, landed, idx_staged, begun)

        @block.scalar
        def _(act):
            flat = g.sc[:, :, :, :].rearrange("p b k c -> p (b k c)")

            def prepare(i, h):
                at = (2 * i + h) * (NSC * BS)
                act.wait_ge(sc_free[h], i + 1)
                nc.scalar.copy(sc[:, h, :], flat[:, bass.ds(at, NSC * BS)])
                nc.scalar.copy(same[:, h, :, 1:BS + 1], flat[:, bass.ds(at + SAME * BS, BS)].unsqueeze(1).broadcast_to([P, D, BS])
                               ).then_inc(sc_ready, 1)

            def consume(i, h, last_block=False, before=None):
                n = 2 * i + h + 1
                if kind in ("cheb", "cheb_last"):
                    act.wait_ge(val_ready, n)
                    nc.scalar.copy(left[:, 0, :, :], rows_of(v)).then_inc(left_ready, 1)
                if kind == "jacobi_first":
                    take_std(act, nc, st, var_ready, std_ready, n)
                if product_of:
                    act.wait_ge(left_turned, n)
                    copy_turned(nc, leftT, tp).then_inc(left_copied, 1)
                if early and not last_block:
                    take_std(act, nc, st, var_ready, std_ready, n + 1)
                if u_new is not None:
                    act.wait_ge(val_ready, n)
                    nc.scalar.copy(u_block(u_new, i, h), v).then_inc(val_read, 1)
                act.wait_ge(run_ready, n)
                act.wait_ge(out_free[h], i + 1)
                if merge is not None:
                    act.wait_ge(in_landed[h], (i + 1) * (16 * n_in))
                nc.scalar.copy(sums[:, h, :, wide - D:wide], rows_of(run[:, :, 1:BS + 1])).then_inc(sums_ready[h], 1)
                act.wait_ge(sums_ready[h], i + 1)
                act.sem_inc(run_read, 1)
                if own is not None:
                    take_squares(act, nc, xc[:, :, :], sq[:, :, :], xc_ready, sq_ready, n)
                    take_std(act, nc, st, var_ready, std_ready, n)
                    if before is not None:
                        own_rows(*before)
                    act.wait_ge(own_turned, n)
                    copy_turned(nc, own_hT, tp).then_inc(own_copied, 1)

            def own_rows(i, h):
                act.wait_ge(own_mm_ready, 2 * i + h + 1)
                for c, piece in products(mm2):
                    nc.scalar.copy(own_row[:, h, c, 0:D], piece)
                nc.scalar.copy(own_row[:, h, :, D:W1ROW], nodes[:, h, :, D:W1ROW]).then_inc(own_row_ready[h], 1)
                act.wait_ge(own_row_ready[h], i + 1)
                act.sem_inc(own_read, 1)

            if own is not None:
                prepare(0, 0)
                prepare(0, 1)
                consume(0, 0)
                prepare(1, 0)
                consume(0, 1, before=(0, 0))
                with act.Fori(1, IT - 1) as i:
                    prepare(i, 1)
                    consume(i, 0, before=(i - 1, 1))
                    prepare(i + 1, 0)
                    consume(i, 1, before=(i, 0))
                prepare(IT - 1, 1)
                consume(IT - 1, 0, before=(IT - 2, 1))
                consume(IT - 1, 1, before=(IT - 1, 0))
                own_rows(IT - 1, 1)
            elif early:
                prepare(0, 0)
                take_std(act, nc, st, var_ready, std_ready, 1)
                with act.Fori(0, IT - 1) as i:
                    prepare(i, 1)
                    consume(i, 0)
                    prepare(i + 1, 0)
                    consume(i, 1)
                prepare(IT - 1, 1)
                consume(IT - 1, 0)
                consume(IT - 1, 1, last_block=True)
            else:
                skewed(act, prepare, consume)
            if merge is not None:
                act.dma_start(fixed[:, 0:D], merge[NPAD:NPAD + P, :]).then_inc(old_fix, 16)
            act.wait_ge(fix_done, 1)
            nc.scalar.copy(fixed[:, wide - D:wide], pfix[:, 0:D]).then_inc(fix_copied, 1)
            act.wait_ge(fix_copied, 1)
            if merge is not None:
                act.wait_ge(old_fix, 16)
            act.dma_start(to[NPAD:NPAD + P, :], fixed[:, :]).then_inc(fix_stored, 16)
            act.wait_ge(fix_stored, 16)

        @block.sync
        def _(sp):
            def prepare(i, h):
                if n_in:
                    sp.wait_ge(out_free[h], i + 1)
                if own is not None:
                    sp.dma_start(nodes[:, h, :, :], block_of(own[0], i, h, W1ROW)).then_inc(own_landed[h], 16)
                if acc_in is not None:
                    sp.dma_start(acc[:, h, :, :], block_of(acc_in, i, h, D)).then_inc(in_landed[h], 16)
                if merge is not None:
                    sp.dma_start(sums[:, h, :, 0:D], block_of(merge, i, h, D)).then_inc(in_landed[h], 16)

            def consume(i, h):
                if has_side:
                    sp.wait_ge(side_ready[h], i + 1)
                if acc_out is not None:
                    sp.dma_start(block_of(acc_out, i, h, D), acc[:, h, :, :]).then_inc(out_stored[h], 16)
                if r_out is not None:
                    sp.dma_start(block_of(r_out, i, h, D), res[:, h, :, :]).then_inc(out_stored[h], 16)
                if own is not None:
                    sp.wait_ge(own_row_ready[h], i + 1)
                    sp.dma_start(block_of(own[1], i, h, W1ROW), own_row[:, h, :, :]).then_inc(out_stored[h], 16)
                sp.wait_ge(sums_ready[h], i + 1)
                sp.dma_start(block_of(to, i, h, wide), sums[:, h, :, :]).then_inc(out_stored[h], 16)
                sp.wait_ge(out_stored[h], (i + 1) * (16 * n_out))
                sp.sem_inc(out_free[h], 1)

            sp.sem_inc(out_free[0], 1)
            sp.sem_inc(out_free[1], 1)
            skewed(sp, prepare, consume)

        @block.tensor
        def _(pe):
            def edges(i, h, before=None):
                n = 2 * i + h + 1
                if before is not None:
                    pe.wait_ge(own_copied, n - 1)
                pe.wait_ge(left_ready, n)
                transpose_pairs(pe, tp, left[:, h * early, :, :], g.ident[:, :]).then_inc(left_turned, 1)
                pe.wait_ge(left_copied, n)
                if early:
                    pe.wait_ge(mm_read, n)
                if wh is not None:
                    multiply_pairs(pe, mm2, [(leftT, wh[:, :], D2 if conv else D2 + 1)])
                multiply_pairs(pe, mm, [(leftT, wu[:, :], D2)]).then_inc(mm_ready, 1)
                if before is not None:
                    own_products(*before)
                if own is not None:
                    pe.wait_ge(own_ready, n)
                    transpose_pairs(pe, tp, own_h[:, :, :], g.ident[:, :]).then_inc(own_turned, 1)

            def own_products(i, h):
                pe.wait_ge(own_read, 2 * i + h + 1)
                for c in range(NPAIR):
                    pe.matmul(product(mm2, c), own_hT[0:D2 + 1, c * P:(c + 1) * P], g.wh[:, :], start=True, stop=False)
                    last = pe.matmul(product(mm2, c), g.ident[:, :], nodes[:, h, 2 * c:2 * c + 2, 0:D], start=False, stop=True)
                last.then_inc(own_mm_ready, 1)

            if own is not None:
                edges(0, 0)
                edges(0, 1, before=(0, 0))
                with pe.Fori(1, IT) as i:
                    edges(i, 0, before=(i - 1, 1))
                    edges(i, 1, before=(i, 0))
                pe.wait_ge(own_copied, NB)
                own_products(IT - 1, 1)
            elif product_of:
                with pe.Fori(0, IT) as i:
                    edges(i, 0)
                    edges(i, 1)
            pe.wait_ge(fix_ready, 1)
            pe.matmul(pfix[:, 0:D], g.carries[:, :], part[:, :], start=True, stop=False)
            pe.matmul(pfix[:, 0:D], g.ident[:, :], fix[:, :], start=False, stop=True).then_inc(fix_done, 1)

        @block.vector
        def _(dve):
            def values(i, h):
                n = 2 * i + h + 1
                got = rows[:, h, :, :]
                dve.wait_ge(sc_ready, n)
                if not early:
                    dve.wait_ge(landed[h], (i + 1) * (16 * BS))
                if u_new is not None:
                    dve.wait_ge(val_read, n)
                if kind == "cheb_first":
                    at = (2 * i + h) * (NSC * BS)
                    flat = g.sc[:, :, :, :].rearrange("p b k c -> p (b k c)")

                    def put(which):
                        return flat[:, bass.ds(at + which * BS, BS)]

                    dis, dinv = ex[:, h, :, 0], ex[:, h, :, 1]
                    dve.tensor_tensor(t1[:, h, :], staged(h, EW), dis, ALU.mult)
                    dve.tensor_tensor(put(D1), dinv, dinv, ALU.mult)
                    dve.tensor_scalar(put(NDIS), dis, -1.0, None, ALU.mult)
                    dve.tensor_copy(put(DINV), dinv)
                    dve.tensor_copy(put(ZSRC), ex[:, h, :, 3])
                    dve.tensor_copy(g.last_src[:, bass.ds((2 * i + h) * BS, BS)], ex[:, h, :, 2])
                    dve.drain()
                    dve.scalar_tensor_tensor(put(D0), t1[:, h, :], -1.0, dis, ALU.mult, ALU.mult)
                    dve.tensor_tensor(rows_of(v), left[:, h, :, :], over_features(t1[:, h, :]), ALU.mult).then_inc(val_ready, 1)
                elif kind == "cheb":
                    dve.tensor_tensor(rows_of(v), got[:, :, 0:D], over_features(staged(h, D0)), ALU.mult).then_inc(val_ready, 1)
                elif kind == "cheb_last":
                    dve.tensor_tensor(rows_of(tmp[:, :, :]), got[:, :, 0:D], over_features(staged(h, D0)), ALU.mult)
                    dve.drain()
                    dve.sem_inc(slot_free[h], 1)
                    dve.scalar_tensor_tensor(v, tmp[:, :, :], 2.0, u_block(u_old, i, h), ALU.mult, ALU.subtract).then_inc(val_ready, 1)
                    dve.wait_ge(in_landed[h], (i + 1) * (16 * n_in))
                    dve.wait_ge(mm_ready, n)
                    for c, piece in products(mm):
                        dve.tensor_tensor(rows_of(v)[:, c, :], acc[:, h, c, :], piece, ALU.add)
                elif kind == "jacobi_first":
                    dve.tensor_tensor(x1[:, :, :], got[:, :, 0:D], over_features(staged(h, NDIS)), ALU.mult)
                    dve.drain()
                    dve.sem_inc(slot_free[h], 1)
                    dve.wait_ge(in_landed[h], (i + 1) * (16 * n_in))
                    dve.tensor_tensor(x1[:, :, :], acc[:, h, :, :], x1[:, :, :], ALU.add)
                    dve.drain()
                    layernorm(dve, x1[:, :, :], x1[:, :, :], sq[:, :, :], st, var_ready, std_ready, n)
                    dve.tensor_tensor(rows_of(v), x1[:, :, :], over_features(staged(h, DINV)), ALU.mult).then_inc(val_ready, 1)
                elif kind in ("jacobi", "jacobi_last"):
                    dve.tensor_tensor(rows_of(tmp[:, :, :]), got[:, :, 0:D], over_features(staged(h, D1)), ALU.mult)
                    dve.drain()
                    dve.sem_inc(slot_free[h], 1)
                    dve.scalar_tensor_tensor(v, u_block(u_old, i, h), beta[:, 0:1], tmp[:, :, :], ALU.mult, ALU.add).then_inc(val_ready, 1)
                elif kind == "conv_first":
                    dve.wait_ge(mm_ready, n)
                    dve.wait_ge(out_free[h], i + 1)
                    for c, piece in products(mm):
                        dve.tensor_copy(rows_of(v)[:, c, :], piece)
                    for c, piece in products(mm2):
                        last = dve.tensor_tensor(acc[:, h, c, :], piece, over_columns(g.b_l1[:, :], c.stop - c.start), ALU.add)
                    last.then_inc(side_ready[h], 1)
                    dve.drain()
                    dve.sem_inc(mm_read, 1)
                elif kind == "conv_last":
                    dve.wait_ge(in_landed[h], (i + 1) * (16 * n_in))
                    dve.tensor_tensor(rows_of(tmp[:, :, :]), got[:, :, 0:D], acc[:, h, :, :], ALU.add)
                    dve.drain()
                    dve.sem_inc(slot_free[h], 1)
                    dve.tensor_scalar(v, tmp[:, :, :], 0.0, None, ALU.max)

            def beside(i, h):
                n = 2 * i + h + 1
                if kind == "cheb_first":
                    dve.wait_ge(mm_ready, n)
                    for c, piece in products(mm2):
                        dve.tensor_tensor(res[:, h, c, :], res[:, h, c, :], piece, ALU.add)
                    for c, piece in products(mm):
                        last = dve.tensor_tensor(acc[:, h, c, :], piece, t1[:, h, c].unsqueeze(2).broadcast_to([P, c.stop - c.start, D]), ALU.mult)
                    last.then_inc(side_ready[h], 1)
                    dve.drain()
                    dve.sem_inc(mm_read, 1)
                elif kind == "cheb":
                    dve.wait_ge(in_landed[h], (i + 1) * (16 * n_in))
                    dve.wait_ge(mm_ready, n)
                    for c, piece in products(mm):
                        last = dve.tensor_tensor(acc[:, h, c, :], acc[:, h, c, :], piece, ALU.add)
                    last.then_inc(side_ready[h], 1)
                elif kind == "jacobi_first":
                    dve.tensor_scalar(acc[:, h, :, :].rearrange("p c f -> p (c f)").rearrange("p (f c) -> p f c", c=BS), v,
                                      g.omega[:, 0:1], None, ALU.mult).then_inc(side_ready[h], 1)
                elif kind == "jacobi":
                    dve.wait_ge(in_landed[h], (i + 1) * (16 * n_in))
                    acc_f = acc[:, h, :, :].rearrange("p c f -> p (c f)").rearrange("p (f c) -> p f c", c=BS)
                    dve.scalar_tensor_tensor(acc_f, v, omega[:, 0:1], acc_f, ALU.mult, ALU.add).then_inc(side_ready[h], 1)

            def normalise(i, h):
                n = 2 * i + h + 1
                dve.wait_ge(landed[h], (i + 1) * (16 * BS))
                layernorm(dve, rows[:, h, :, 0:D], left[:, h, :, :], sq[:, :, :], st, var_ready, std_ready, n)
                if kind == "cheb_first":
                    dve.tensor_copy(ex[:, h, :, :], rows[:, h, :, EX:EX + 5])
                    dve.wait_ge(out_free[h], i + 1)
                    dve.tensor_copy(res[:, h, :, :], rows[:, h, :, 0:D])
                    dve.drain()
                dve.sem_inc(slot_free[h], 1)
                dve.sem_inc(left_ready, 1)

            def normalise_own(i, h):
                dve.wait_ge(own_landed[h], (i + 1) * 16)
                layernorm_apart(dve, nodes[:, h, :, 0:D], xc[:, :, :], own_h[:, :, :], st, sq[:, :, :], xc_ready, sq_ready,
                                var_ready, std_ready, 2 * i + h + 1).then_inc(own_ready, 1)

            def scan(i, h, last_block=False):
                n = 2 * i + h + 1
                values(i, h)
                if kind == "jacobi_last":
                    dve.drain()
                    dve.wait_ge(in_landed[h], (i + 1) * (16 * n_in))
                    acc_f = acc[:, h, :, :].rearrange("p c f -> p (c f)").rearrange("p (f c) -> p f c", c=BS)
                    dve.scalar_tensor_tensor(v, v, omega[:, 0:1], acc_f, ALU.mult, ALU.add)
                dve.drain()
                if kind == "cheb":
                    dve.sem_inc(slot_free[h], 1)
                dve.wait_ge(run_read, n)
                dve.tensor_tensor_scan(run[:, :, :].rearrange("p f c -> p (f c)"), same[:, h, :, :].rearrange("p f c -> p (f c)"),
                                       val[:, :, :].rearrange("p f c -> p (f c)"), 0.0, ALU.mult, ALU.add).then_inc(run_ready, 1)
                dve.tensor_tensor(tmp[:, :, :], v, staged(h, FIRST).unsqueeze(1).broadcast_to([P, D, BS]), ALU.mult)
                dve.drain()
                dve.tensor_copy(val[:, :, 0], run[:, :, BS])
                dve.reduce_sum(part[:, :], tmp[:, :, :], AX)
                dve.drain()
                dve.tensor_tensor(fix[:, :], fix[:, :], part[:, :], ALU.add)
                if last_block:
                    dve.drain()
                    dve.tensor_copy(part[:, :], run[:, :, BS]).then_inc(fix_ready, 1)
                if own is not None:
                    normalise_own(i, h)
                beside(i, h)
                dve.drain()
                dve.sem_inc(sc_free[h], 1)

            dve.memset(fix[:, :], 0.0)
            dve.memset(val[:, :, 0], 0.0)
            dve.memset(same[:, :, :, 0], 0.0)
            if kind in ("jacobi", "jacobi_last"):
                dve.tensor_copy(beta[:, :], g.betas[:, bass.ds(k, 1)])
                dve.tensor_copy(omega[:, :], g.omega[:, bass.ds(k, 1)])
            dve.drain()
            for q in slot_free + sc_free + [run_read, val_read]:
                dve.sem_inc(q, 1)
            if early:
                dve.sem_inc(mm_read, 1)
            if kind == "cheb_first":
                dve.memset(leftT[D2:D2 + 1, :], 1.0)
            if own is not None:
                dve.memset(own_hT[D2:D2 + 1, :], 1.0)
                dve.sem_inc(own_read, 1)
            if zero is not None:
                dve.memset(zero[:, :], 0.0)
            if early:
                normalise(0, 0)
            with dve.Fori(0, IT - 1) as i:
                for h in range(2):
                    if early:
                        normalise(*next_block(i, h))
                    scan(i, h)
            if early:
                normalise(IT - 1, 1)
            scan(IT - 1, 0)
            scan(IT - 1, 1, last_block=True)



def message_stage(nc, io, g):
    with Stage(nc, "msg") as s:
        rows, idx_now = s.sb("rows", [P, 2, BS, H2ROW]), s.sb("idx_now", [P, 2 * BS], I32)
        cw, dist = s.sb("cw", [P, COLS]), s.sb("dist", [P, COLS])
        sc = s.sb("sc", [P, 2, 2 * BS])
        attr, aT, g1 = s.sb("attr", [P, 2, BS, R]), s.sb("aT", [P, NPAIR * P]), s.sb("g1", [D2 + 1, NPAIR * P])
        one, oneT = s.sb("one", [P, BS, P], F16), s.sb("oneT", [P, 2, BS, P])
        ident_h = s.sb("ident_h", [P, P], F16)
        gate, junk, adapt, wgt = s.sb("gate", [P, 2, BS, D]), s.sb("junk", [P, P]), s.sb("adapt", [P, BS]), s.sb("wgt", [P, BS])
        msg = s.sb("msg", [P, 2, BS, H2ROW])
        half_pi = s.sb("half_pi", [P, 1])
        zeros = s.sb("zeros", [P, BS * H2ROW])
        tp, ph = s.ps("tp", [P, 2, 512]), s.ps("ph", [P, 2, 512])
        pone, pterm = s.ps("pone", [P, 2, 1024], F16), s.ps("pterm", [P, 2, 512])
        HB = BS // 2
        slot_free, landed, idx_staged, begun = s.sems("slot_free"), s.sems("landed"), s.sem("idx_staged"), s.sem("begun")
        dist_landed, dist_ready, cos_ready, cw_ready, zeroed = (s.sem(n) for n in (
            "dist_landed", "dist_ready", "cos_ready", "cw_ready", "zeroed"))
        sc_free, sc_ready = s.sems("sc_free"), s.sem("sc_ready")
        attr_landed, attr_free = s.sems("attr_landed"), s.sems("attr_free")
        attr_turned, attr_copied, hid_ready, silu_done, gate_ready, gate_copied = (s.sem(n) for n in (
            "attr_turned", "attr_copied", "hid_ready", "silu_done", "gate_ready", "gate_copied"))
        one_ready, one_turned, one_copied, term_ready, term_read = (s.sem(n) for n in (
            "one_ready", "one_turned", "one_copied", "term_ready", "term_read"))
        oneT_free, ones_ready = s.sems("oneT_free"), s.sem("ones_ready")
        out_ready, out_free, out_stored = s.sems("out_ready"), s.sems("out_free"), s.sems("out_stored")
        cleared = s.sem("cleared")
        block = s.ctx.enter_context(nc.Block())

        @block.gpsimd
        def _(pool):
            gather_rows(pool, g.tab_h2, g.dst_idx, idx_now, rows, H2ROW, slot_free, landed, idx_staged, begun)

        @block.sync
        def _(sp):
            sp.dma_start(dist[:, :], io.edge_weight.rearrange("(p c) -> p c", p=P)).then_inc(dist_landed, 16)
            sp.sem_inc(out_free[0], 1)
            sp.sem_inc(out_free[1], 1)
            sp.wait_ge(zeroed, 1)
            for q in range(NAGG):
                sp.dma_start(g.agg[q][NPAD:NPAD + P, :], zeros[:, 0:H2ROW]).then_inc(cleared, 16)

            def prepare(i, h):
                sp.wait_ge(attr_free[h], i + 1)
                sp.dma_start(attr[:, h, :, :], block_of(io.edge_attr, i, h, R)).then_inc(attr_landed[h], 16)
                for q in range(NAGG):
                    sp.dma_start(block_of(g.agg[q], i, h, H2ROW), zeros[:, :].rearrange("p (c w) -> p c w", w=H2ROW)).then_inc(cleared, 16)

            def consume(i, h):
                sp.wait_ge(out_ready[h], i + 1)
                sp.dma_start(block_of(g.msg, i, h, H2ROW), msg[:, h, :, :]).then_inc(out_stored[h], 16)
                sp.wait_ge(out_stored[h], (i + 1) * 16)
                sp.sem_inc(out_free[h], 1)

            skewed_by_two(sp, prepare, consume)
            sp.wait_ge(cleared, 16 * NAGG * (NB + 1))

        @block.scalar
        def _(act):
            act.wait_ge(dist_ready, 1)
            nc.scalar.activation(cw[:, :], dist[:, :], ACT.Sin, bias=half_pi[:, 0:1], scale=-math.pi / CUTOFF
                                 ).then_inc(cos_ready, 1)
            act.wait_ge(cw_ready, 1)
            flat = g.sc[:, :, :, :].rearrange("p b k c -> p (b k c)")

            def gates(i, h):
                n = 2 * i + h + 1
                act.wait_ge(sc_free[h], i + 1)
                nc.scalar.copy(sc[:, h, 0:BS], cw[:, bass.ds((2 * i + h) * BS, BS)])
                nc.scalar.copy(sc[:, h, BS:2 * BS], flat[:, bass.ds((2 * i + h) * (NSC * BS) + ZSRC * BS, BS)]
                               ).then_inc(sc_ready, 1)
                act.wait_ge(attr_turned, n)
                copy_turned(nc, aT, tp, 2 * R).then_inc(attr_copied, 1)
                act.wait_ge(one_turned, n)
                act.wait_ge(oneT_free[h], i + 1)
                nc.scalar.copy(oneT[:, h, 0:8, :].rearrange("p c e -> p (c e)"), pone[:, 0, :])
                nc.scalar.copy(oneT[:, h, 8:BS, :].rearrange("p c e -> p (c e)"), pone[:, 1, 0:(BS - 8) * P]).then_inc(one_copied, 1)
                act.wait_ge(hid_ready, n)
                q = 4 * P
                nc.scalar.activation(g1[0:D2, 0:q], ph[0:D2, 0, 0:q], ACT.Silu, bias=g.b1[:, 0:1])
                nc.scalar.activation(g1[0:D2, q:NPAIR * P], ph[0:D2, 1, 0:NPAIR * P - q], ACT.Silu,
                                     bias=g.b1[:, 0:1]).then_inc(silu_done, 1)
                act.wait_ge(gate_ready, n)
                for c, piece in products(tp):
                    last = nc.scalar.copy(gate[:, h, c, :], piece)
                last.then_inc(gate_copied, 1)

            with act.Fori(0, IT) as i:
                for h in range(2):
                    gates(i, h)

        @block.tensor
        def _(pe):
            def turn(i, h):
                n = 2 * i + h + 1
                pe.wait_ge(attr_landed[h], (i + 1) * 16)
                transpose_pairs(pe, tp, attr[:, h, :, :], g.ident[:, :], 2 * R).then_inc(attr_turned, 1)
                pe.wait_ge(one_ready, n)
                for c in range(BS):
                    last = pe.transpose(pone[:, c // 8, (c % 8) * P:(c % 8 + 1) * P], one[:, c, :], ident_h[:, :])
                last.then_inc(one_turned, 1)

            def hidden(i, h):
                n = 2 * i + h + 1
                pe.wait_ge(attr_copied, n)
                pe.sem_inc(attr_free[h], 1)
                pe.matmul(ph[0:D2, 0, :], g.W1[:, :], aT[0:2 * R, 0:4 * P], start=True, stop=True)
                pe.matmul(ph[0:D2, 1, 0:(NPAIR - 4) * P], g.W1[:, :], aT[0:2 * R, 4 * P:NPAIR * P], start=True,
                          stop=True).then_inc(hid_ready, 1)

            def second(i, h):
                pe.wait_ge(silu_done, 2 * i + h + 1)
                multiply_pairs(pe, tp, [(g1, g.W2[:, :], D2 + 1)]).then_inc(gate_ready, 1)

            def term(i, h, half):
                pe.wait_ge(term_read, (2 * i + h) * 2 + half + 1)
                for c in range(HB):
                    last = pe.matmul(pterm[:, c // 4, (c % 4) * P:(c % 4) * P + NZ], oneT[0:NZ, h, half * HB + c, :],
                                     g.pair_term[:, :], start=True, stop=True)
                last.then_inc(term_ready, 1)

            def body(i, h, last):
                n = 2 * i + h + 1
                pe.wait_ge(one_copied, n)
                term(i, h, 0)
                pe.wait_ge(gate_copied, n)
                if not last:
                    turn(*next_block(i, h))
                    hidden(*next_block(i, h))
                term(i, h, 1)
                pe.wait_ge(term_ready, 2 * n)
                pe.sem_inc(oneT_free[h], 1)
                if not last:
                    second(*next_block(i, h))

            for q in attr_free + oneT_free:
                pe.sem_inc(q, 1)
            pe.wait_ge(ones_ready, 1)
            turn(0, 0)
            hidden(0, 0)
            second(0, 0)
            with_next(pe, body)

        @block.vector
        def _(dve):
            dve.memset(zeros[:, :], 0.0).then_inc(zeroed, 1)
            dve.memset(half_pi[:, :], math.pi / 2)
            dve.memset(msg[:, :, :, D + 1:H2ROW], 0.0)
            dve.tensor_copy(ident_h[:, :], g.ident[:, :])
            dve.memset(g1[D2:D2 + 1, :], 1.0).then_inc(ones_ready, 1)
            dve.wait_ge(dist_landed, 16)
            dve.tensor_scalar(cw[:, :], dist[:, :], CUTOFF, 0.5, ALU.is_lt, ALU.mult)
            dve.drain()
            dve.tensor_copy(g.half_keep[:, :], cw[:, :])
            dve.scalar_tensor_tensor(dist[:, :], dist[:, :], -1.0, dist[:, :], ALU.mult, ALU.max)
            dve.drain()
            dve.tensor_scalar(dist[:, :], dist[:, :], CUTOFF, None, ALU.min)
            dve.drain()
            dve.sem_inc(dist_ready, 1)
            dve.wait_ge(cos_ready, 1)
            dve.scalar_tensor_tensor(cw[:, :], cw[:, :], 1.0, g.half_keep[:, :], ALU.add, ALU.mult).then_inc(cw_ready, 1)
            for q in slot_free + sc_free:
                dve.sem_inc(q, 1)
            dve.sem_inc(term_read, 1)

            def one_hots(i, h, first=False):
                n = 2 * i + h + 1
                dve.wait_ge(sc_ready, n)
                if not first:
                    dve.wait_ge(one_turned, n - 1)
                for c in range(BS):
                    last = dve.tensor_scalar(one[:, c, :], g.iota[:, :], sc[:, h, BS + c:BS + c + 1], None, ALU.is_equal)
                last.then_inc(one_ready, 1)

            def terms(i, h, half):
                dve.wait_ge(term_ready, (2 * i + h) * 2 + half + 1)
                for c in range(HB):
                    cc = half * HB + c
                    dve.scalar_tensor_tensor(
                        junk[:, 0:NZ], g.iota[:, 0:NZ], rows[:, h, cc, D:D + 1],
                        pterm[:, c // 4, (c % 4) * P:(c % 4) * P + NZ],
                        ALU.is_equal, ALU.mult, accum_out=adapt[:, cc:cc + 1])
                    dve.drain()
                dve.sem_inc(term_read, 1)

            def messages(i, h):
                n = 2 * i + h + 1
                got, m = rows[:, h, :, :], msg[:, h, :, :]
                dve.wait_ge(landed[h], (i + 1) * (16 * BS))
                dve.tensor_tensor(wgt[:, :], sc[:, h, 0:BS], got[:, :, D + 1], ALU.mult)
                terms(i, h, 0)
                dve.wait_ge(out_free[h], i + 1)
                dve.tensor_tensor(m[:, :, 0:D], got[:, :, 0:D], over_features(wgt[:, :]), ALU.mult)
                dve.tensor_copy(m[:, :, D], got[:, :, D + 1])
                terms(i, h, 1)
                dve.sem_inc(slot_free[h], 1)
                dve.wait_ge(gate_copied, n)
                dve.tensor_tensor(gate[:, h, :, :], gate[:, h, :, :], over_features(adapt[:, :]), ALU.add)
                dve.drain()
                dve.tensor_tensor(m[:, :, 0:D], m[:, :, 0:D], gate[:, h, :, :], ALU.mult).then_inc(out_ready[h], 1)
                dve.drain()
                dve.sem_inc(sc_free[h], 1)

            one_hots(0, 0, first=True)
            with dve.Fori(0, IT - 1) as i:
                one_hots(i, 1)
                messages(i, 0)
                one_hots(i + 1, 0)
                messages(i, 1)
            one_hots(IT - 1, 1)
            messages(IT - 1, 0)
            messages(IT - 1, 1)


def add_up_stage(nc, io, g):
    with Stage(nc, "add") as s:
        msg, out = s.sb("msg", [P, 2, BS, H2ROW]), s.sb("out", [P, 2, BS, H2ROW])
        src_row = s.sb("src_row", [P, 2, BS, P])
        srcs = s.sb("srcs", [P, 2, BS])
        same, junk, before = s.sb("same", [P, 2, BS, P]), s.sb("junk", [P, P]), s.sb("before", [P, BS])
        dump_i, dump = s.sb("dump_i", [P, 1], I32), s.sb("dump", [P, 1])
        where = s.sb("where", [P, 2, BS], I32)
        t0 = s.sb("t0", [P, 2, BS])
        ps = [s.ps(f"ps{h}", [P, 2, 512]) for h in range(2)]
        HB = BS // 2
        in_landed, in_free = s.sems("in_landed"), s.sems("in_free")
        dump_ready = s.sem("dump_ready")
        same_ready, summed, copied = s.sem("same_ready"), s.sem("summed"), s.sem("copied")
        where_ready = s.sem("where_ready")
        slot_done, sums_free = s.sems("slot_done"), s.sems("sums_free")
        srcs_ready, srcs_free = s.sem("srcs_ready"), s.sems("srcs_free")
        added, begun = s.sems("added", NAGG), s.sem("begun")
        block = s.ctx.enter_context(nc.Block())

        @block.sync
        def _(sp):
            with sp.Fori(0, IT) as i:
                for h in range(2):
                    sp.wait_ge(in_free[h], i + 1)
                    sp.dma_start(msg[:, h, :, :], block_of(g.msg, i, h, H2ROW)).then_inc(in_landed[h], 16)
                    sp.dma_start(src_row[:, h, :, :].rearrange("p c e -> p (c e)"),
                                 g.src_cols[bass.ds((2 * i + h) * BS, BS), :].rearrange("c e -> (c e)").partition_broadcast(P)
                                 ).then_inc(in_landed[h], 16)

        @block.scalar
        def _(act):
            with act.Fori(0, IT) as i:
                for h in range(2):
                    act.wait_ge(srcs_free[h], i + 1)
                    nc.scalar.copy(srcs[:, h, :], g.src_idx[:, bass.ds((2 * i + h) * BS, BS)]).then_inc(srcs_ready, 1)
                    act.wait_ge(summed, 2 * i + h + 1)
                    act.wait_ge(slot_done[h], i + 1)
                    for q in range(2):
                        last = nc.scalar.copy(out[:, h, q * HB:(q + 1) * HB, :].rearrange("p c w -> p (c w)"), ps[h][:, q, 0:HB * H2ROW])
                    last.then_inc(copied, 1)
                    act.wait_ge(copied, 2 * i + h + 1)
                    act.sem_inc(sums_free[h], 1)

        @block.tensor
        def _(pe):
            pe.sem_inc(sums_free[0], 1)
            pe.sem_inc(sums_free[1], 1)
            with pe.Fori(0, IT) as i:
                for h in range(2):
                    pe.wait_ge(same_ready, 2 * i + h + 1)
                    pe.wait_ge(sums_free[h], i + 1)
                    for c in range(BS):
                        last = pe.matmul(ps[h][:, c // HB, (c % HB) * H2ROW:(c % HB + 1) * H2ROW], same[:, h, c, :],
                                         msg[:, h, c, :], start=True, stop=True)
                    last.then_inc(summed, 1)
                    pe.wait_ge(summed, 2 * i + h + 1)
                    pe.sem_inc(in_free[h], 1)

        @block.vector
        def _(dve):
            for q in in_free + srcs_free:
                dve.sem_inc(q, 1)
            dve.wait_ge(dump_ready, 1)
            dve.tensor_copy(dump[:, :], dump_i[:, :])
            dve.drain()
            with dve.Fori(0, IT) as i:
                for h in range(2):
                    dve.wait_ge(in_landed[h], (i + 1) * 32)
                    dve.wait_ge(srcs_ready, 2 * i + h + 1)
                    for c in range(BS):
                        dve.tensor_scalar(same[:, h, c, :], src_row[:, h, c, :], srcs[:, h, c:c + 1], None, ALU.is_equal)
                    for c in range(BS):
                        dve.scalar_tensor_tensor(junk[:, :], src_row[:, h, c, :], srcs[:, h, c:c + 1], g.lower[:, :],
                                                 ALU.is_equal, ALU.mult, accum_out=before[:, c:c + 1])
                        dve.drain()
                    dve.sem_inc(same_ready, 1)
                    dve.tensor_scalar(t0[:, 0, :], before[:, :], 0.5, None, ALU.is_lt)
                    dve.tensor_scalar(t0[:, 1, :], srcs[:, h, :], dump[:, 0:1], None, ALU.subtract)
                    dve.drain()
                    dve.sem_inc(srcs_free[h], 1)
                    dve.tensor_tensor(t0[:, 1, :], t0[:, 1, :], t0[:, 0, :], ALU.mult)
                    dve.drain()
                    dve.wait_ge(slot_done[h], i + 1)
                    dve.tensor_scalar(where[:, h, :], t0[:, 1, :], dump[:, 0:1], None, ALU.add).then_inc(where_ready, 1)

        @block.gpsimd
        def _(pool):
            pool.iota(dump_i[:, :], pattern=[[0, 1]], base=NPAD, channel_multiplier=1).then_inc(dump_ready, 1)
            pool.sem_inc(slot_done[0], 1)
            pool.sem_inc(slot_done[1], 1)
            per = 2 * BS // NAGG

            def adds(i, h, first):
                pool.wait_ge(copied, 2 * i + h + 1)
                pool.wait_ge(where_ready, 2 * i + h + 1)
                pool.sem_inc(begun, 1)
                for c in range(BS):
                    n = h * BS + c
                    if n % 2 == 0 and (n >= NAGG or not first):
                        for q in (n, n + 1):
                            pool.wait_ge(added[q % NAGG], i * (16 * per) + 16 * (q // NAGG))
                        pool.sem_inc(begun, 1)
                    if c == NAGG - 2 + NAGG % 2 and not (first and h == 0):
                        pool.sem_inc(slot_done[1 - h], 1)
                    pool.indirect_dma_start(
                        out=g.agg[n % NAGG], out_offset=bass.IndirectOffsetOnAxis(ap=where[:, h, c:c + 1], axis=0),
                        in_=out[:, h, c, :], in_offset=None, compute_op=ALU.add,
                    ).then_inc(added[n % NAGG], 16)

            adds(0, 0, True)
            adds(0, 1, True)
            with pool.Fori(1, IT) as i:
                adds(i, 0, False)
                adds(i, 1, False)
            for q in range(NAGG):
                pool.wait_ge(added[q], IT * (16 * per))


def gnn_program(nc, args, out):
    with Stage(nc, "all") as s:
        io = Names()
        io.x, io.src, io.dst, io.edge_attr = args["x"], args["src"], args["dst"], args["edge_attr"]
        io.edge_weight, io.node_type, io.node_vec, io.w0 = args["edge_weight"], args["node_type"], args["node_vec"], args["w0"]
        io.bias0, io.lap, io.mf, io.W1 = args["bias0"], args["lap"], args["mf"], args["W1"]
        io.b1, io.W2, io.b2, io.emb = args["b1"], args["W2"], args["b2"], args["emb"]
        io.adaptW, io.gamma, io.beta, io.w_rel1 = args["adaptW"], args["gamma"], args["beta"], args["w_rel1"]
        io.w_root1, io.b_l1, io.w_rel2, io.w_root2 = args["w_root1"], args["b_l1"], args["w_rel2"], args["w_root2"]
        io.b_l2 = args["b_l2"]
        io.out = out
        g = Names()
        dram = lambda name, rows, w: nc.dram_tensor(name, [rows, w], F32).ap()
        g.tab_in, g.tab_own = dram("tab_in", NPAD, W1ROW), dram("tab_own", NPAD, W1ROW)
        g.tab_s = [dram("tab_s0", ROWS, D), dram("tab_s1", ROWS, D)]
        g.tab_a0, g.tab_a2 = dram("tab_a0", ROWS, D), dram("tab_a2", ROWS, D)
        g.tab_both, g.tab_both2 = dram("tab_both", ROWS, D2), dram("tab_both2", ROWS, D2)
        g.sum_tables = [(g.tab_s[0], D), (g.tab_s[1], D), (g.tab_a0, D), (g.tab_a2, D), (g.tab_both, D2), (g.tab_both2, D2)]
        g.edge_y, g.edge_r, g.edge_acc, g.edge_q = dram("edge_y", NPAD, D), dram("edge_r", NPAD, D), dram("edge_acc", NPAD, D), dram("edge_q", NPAD, D)
        g.x2, g.x3, g.tab_h2 = dram("x2", NPAD, D), dram("x3", NPAD, D), dram("tab_h2", NPAD, H2ROW)
        g.msg = dram("msg", NPAD, H2ROW)
        g.agg = [dram(f"agg{q}", NPAD + P, H2ROW) for q in range(NAGG)]
        g.src_cols = dram("src_cols", COLS, P)

        g.ident, g.lower, g.carries, g.iota = s.sb("ident", [P, P]), s.sb("lower", [P, P]), s.sb("carries", [P, P]), s.sb("iota", [P, P])
        g.src_idx, g.dst_idx = s.sb("src_idx", [P, COLS], I32), s.sb("dst_idx", [P, COLS], I32)
        g.last_src, g.last_node = s.sb("last_src", [P, COLS], I32), s.sb("last_node", [P, COLS], I32)
        g.sc = s.sb("sc", [P, NB, NSC, BS])
        g.wh, g.wu = s.sb("wh", [D2 + 1, D2]), [s.sb(f"wu{k}", [D2, D2]) for k in range(3)]
        g.w_rel1, g.w_root1 = s.sb("w_rel1", [D2, D2]), s.sb("w_root1", [D2, D2])
        g.w_rel2, g.w_root2 = s.sb("w_rel2", [D2, D2]), s.sb("w_root2", [D2, D2])
        g.W1, g.W2, g.b1 = s.sb("W1", [2 * R, D2]), s.sb("W2", [D2 + 1, D2]), s.sb("b1", [D2, 1])
        g.b_l1, g.b_l2 = s.sb("b_l1", [P, D]), s.sb("b_l2", [P, D])
        g.gamma, g.beta = s.sb("gamma", [P, D]), s.sb("beta", [P, D])
        g.omega, g.betas, g.p0w, g.pair_term = s.sb("omega", [P, K1]), s.sb("betas", [P, K1]), s.sb("p0w", [P, 1]), s.sb("pair_term", [NZ, NZ])

        weight_stage(nc, io, g)
        node_stage_in(nc, io, g)
        s0, s1 = g.tab_s
        with Stage(nc, "values") as vs:
            ua = vs.sb("ua", [P, COLS * D])
            propagate(nc, g, "c0", "cheb_first", g.tab_in, W1ROW, g.src_idx, s0, u_new=ua, acc_out=g.edge_y, r_out=g.edge_r)
            propagate(nc, g, "c1", "cheb", s0, D, g.last_src, s1, acc_in=g.edge_y, acc_out=g.edge_y, own=(g.tab_in, g.tab_own))
            propagate(nc, g, "c2", "cheb_last", s1, D, g.last_src, g.tab_a0, u_old=ua, acc_in=g.edge_y)
            ub = vs.sb("ub", [P, COLS * D])
            propagate(nc, g, "j0", "jacobi_first", g.tab_a0, D, g.last_src, s0, u_new=ua, acc_in=g.edge_r,
                      acc_out=g.edge_acc, zero=ub)
            with nc.Fori(0, (K1 - 2) // 2) as r:
                propagate(nc, g, "jo", "jacobi", s0, D, g.last_src, s1, u_old=ub, u_new=ub, k=2 * r + 1,
                          acc_in=g.edge_acc, acc_out=g.edge_acc)
                propagate(nc, g, "je", "jacobi", s1, D, g.last_src, s0, u_old=ua, u_new=ua, k=2 * r + 2,
                          acc_in=g.edge_acc, acc_out=g.edge_acc)
            propagate(nc, g, "j9", "jacobi_last", s0, D, g.last_src, g.tab_both, u_old=ub, k=K1 - 1,
                      acc_in=g.edge_acc, merge=g.tab_a0)
        node_stage_mid(nc, io, g)
        g.half_keep = s.sb("half_keep", [P, COLS])
        message_stage(nc, io, g)
        add_up_stage(nc, io, g)
        node_stage_late(nc, io, g)
        propagate(nc, g, "g0", "conv_first", g.x3, D, g.src_idx, g.tab_a2, acc_out=g.edge_q)
        propagate(nc, g, "g1", "conv_last", g.tab_a2, D, g.last_src, g.tab_both2, acc_in=g.edge_q, merge=g.tab_a2)
        node_stage_out(nc, io, g)


def kernel(**inputs):
    import numpy as np
    import concourse.bacc as bacc
    from concourse.bass_utils import run_bass_kernel_spmd

    def padded(name, value=0):
        a = np.asarray(inputs[name])
        out = np.full((NPAD,) + a.shape[1:], value, a.dtype)
        out[:N] = a
        return out

    arrays = {"x": padded("x"), "src": padded("src", NPAD - 1), "dst": padded("dst", NPAD - 1),
              "edge_attr": padded("edge_attr_40"), "edge_weight": padded("edge_weight"),
              "node_type": padded("node_type_119"), "node_vec": padded("node_vec")}
    for name, of in (("w0", "L0_gnn_weight"), ("bias0", "L0_gnn_bias"), ("lap", "L1_gnn_lap_coefs"),
                     ("mf", "L1_gnn_mf_weights"), ("W1", "L2_gnn_W1"), ("b1", "L2_gnn_b1"), ("W2", "L2_gnn_W2"),
                     ("b2", "L2_gnn_b2"), ("emb", "L2_gnn_emb"), ("adaptW", "L2_gnn_adaptW"), ("gamma", "L2_gnn_gamma"),
                     ("beta", "L2_gnn_beta"), ("w_rel1", "L3_gnn_w_rel1"), ("w_root1", "L3_gnn_w_root1"),
                     ("b_l1", "L3_gnn_b1"), ("w_rel2", "L3_gnn_w_rel2"), ("w_root2", "L3_gnn_w_root2"), ("b_l2", "L3_gnn_b2")):
        arrays[name] = np.ascontiguousarray(inputs[of])
    nc = bacc.Bacc("TRN2", target_bir_lowering=False, num_devices=1)
    args = {name: nc.dram_tensor(f"in_{name}", a.shape, mybir.dt.from_np(a.dtype), kind="ExternalInput").ap()
            for name, a in arrays.items()}
    out = nc.dram_tensor("out_x", [NPAD, D], F32, kind="ExternalOutput").ap()
    gnn_program(nc, args, out)
    r = run_bass_kernel_spmd(nc, [{f"in_{name}": a for name, a in arrays.items()}], core_ids=[0])
    return np.ascontiguousarray(r.results[0]["out_x"][:N])
```
